# Optimizing a Trainium2 kernel written in Bass

```python
import numpy as np
import jax
import jax.numpy as jnp

def _softmax(x, axis=-1):
    return jax.nn.softmax(x, axis=axis)

def _gelu(x):
    return jax.nn.gelu(x, approximate=True)

def _silu(x):
    return jax.nn.silu(x)

def _sigmoid(x):
    return jax.nn.sigmoid(x)

def _layernorm(x, axis=-1, eps=1e-05):
    m = jnp.mean(x, axis=axis, keepdims=True)
    v = jnp.var(x, axis=axis, keepdims=True)
    return (x - m) / jnp.sqrt(v + eps)

def _scatter_add(tgt, idx, src, axis=0):
    return tgt.at[idx].add(src)

def _segment_sum(src, seg, n):
    return jax.ops.segment_sum(src, seg, n)
kernel_name = 'mk_adaln_ffn_d2_seqx_r4_2950c0'

def setup_inputs(seed: int=0):
    np.random.seed(seed)
    _w = jnp.asarray

    def _rec_inputs():
        import jax
        import jax.numpy as jnp
        _rk = jax.random.key(seed)
        x = -0.0002928 + 1 * jax.random.normal(jax.random.fold_in(_rk, 1), (64, 64, 256), jnp.float32)
        _lenS = 64 - jax.random.randint(jax.random.fold_in(_rk, 7), (64,), 0, max(1, 64 // 4) + 1, jnp.int32)
        _lenS2 = 64 - jax.random.randint(jax.random.fold_in(_rk, 8), (64,), 0, max(1, 64 // 4) + 1, jnp.int32)
        cond_1024 = 0.0061147 + 1.02565 * jax.random.normal(jax.random.fold_in(_rk, 11), (64, 256), jnp.float32)
        return (x, cond_1024)
    x, cond_1024 = _rec_inputs()

    def _L0_cond_setup():
        import jax, jax.numpy as jnp
        import numpy as np
        D, HS, HE, E, K = (256, 512, 256, 8, 2)
        B, T = (4, 256)
        N_SHARED = 1
        key = jax.random.key(seed)
        ks = jax.random.split(key, 9)
        g = lambda k, shape, s: jax.random.normal(k, shape, jnp.float32) * s
        return {'x': g(ks[0], (B, T, D), 1.0), 't_emb': g(ks[1], (B, D), 1.0), 'router_W': g(ks[2], (2 * D, E), 0.01), 'router_bias': jnp.zeros((E,), jnp.float32), 'w1': g(ks[3], (D, HS), 0.02), 'w3': g(ks[4], (D, HS), 0.02), 'w2': g(ks[5], (HS, D), 0.02), 'W1e': g(ks[6], (E, D, HE), 0.02), 'W2e': g(ks[7], (E, HE, D), 0.02)}
    _L0_cond_all = _L0_cond_setup()
    _L0_cond_in = {k: v for k, v in _L0_cond_all.items() if k in ('router_W', 'router_bias', 'w1', 'w3', 'w2', 'W1e', 'W2e')}
    del _L0_cond_all

    def _L0_ffn_setup():
        import jax, jax.numpy as jnp
        import numpy as np
        B, S, H, E, K = (2, 256, 256, 8, 2)
        D = 2 * H
        key = jax.random.key(seed)
        ks = jax.random.split(key, 7)
        x = jax.random.normal(ks[0], (B, S, H), dtype=jnp.float32)
        Wr = jax.random.normal(ks[1], (H, E), dtype=jnp.float32) / np.sqrt(H)
        br = jnp.zeros((E,), dtype=jnp.float32)
        W1 = jax.random.normal(ks[2], (E, H, D), dtype=jnp.float32) / np.sqrt(H)
        b1 = jnp.zeros((E, D), dtype=jnp.float32)
        W2 = jax.random.normal(ks[3], (E, D, H), dtype=jnp.float32) / np.sqrt(D)
        b2 = jnp.zeros((E, H), dtype=jnp.float32)
        return {'x': x, 'Wr': Wr, 'br': br, 'W1': W1, 'b1': b1, 'W2': W2, 'b2': b2}
    _L0_ffn_all = _L0_ffn_setup()
    _L0_ffn_in = {k: v for k, v in _L0_ffn_all.items() if k in ('Wr', 'br', 'W1', 'b1', 'W2', 'b2')}
    del _L0_ffn_all

    def _L1_cond_setup():
        import jax, jax.numpy as jnp
        import numpy as np
        import math
        IN_F = 256
        OUT_F = 256
        B = 16
        L = 1024
        key = jax.random.key(seed)
        k1, k2, k3 = jax.random.split(key, 3)
        Efou = jax.random.normal(k1, (B, L, IN_F), dtype=jnp.float32)
        y = jax.random.normal(k2, (B, IN_F), dtype=jnp.float32)
        weight = jax.random.normal(k3, (1, OUT_F, IN_F, 1), dtype=jnp.float32)
        return {'Efou': Efou, 'y': y, 'weight': weight}
    _L1_cond_all = _L1_cond_setup()
    _L1_cond_in = {k: v for k, v in _L1_cond_all.items() if k in ('weight',)}
    del _L1_cond_all

    def _L1_ffn_setup():
        import jax, jax.numpy as jnp
        import numpy as np
        EPS = 1e-05

        def _quantize(W):
            gamma = jnp.mean(jnp.abs(W))
            return jnp.clip(jnp.round(W / (gamma + EPS)), -1.0, 1.0)
        key = jax.random.key(seed)
        k_x, k_w1, k_b1, k_w2, k_b2 = jax.random.split(key, 5)
        n_embd = 256
        d_ff = 4 * n_embd
        B, S = (4, 1024)
        bound1 = 1.0 / np.sqrt(n_embd)
        bound2 = 1.0 / np.sqrt(d_ff)
        x = jax.random.normal(k_x, (B, S, n_embd), dtype=jnp.float32)
        W1 = jax.random.uniform(k_w1, (d_ff, n_embd), jnp.float32, -bound1, bound1)
        b1 = jax.random.uniform(k_b1, (d_ff,), jnp.float32, -bound1, bound1)
        W2 = jax.random.uniform(k_w2, (n_embd, d_ff), jnp.float32, -bound2, bound2)
        b2 = jax.random.uniform(k_b2, (n_embd,), jnp.float32, -bound2, bound2)
        return {'x': x, 'W1': W1, 'b1': b1, 'W2': W2, 'b2': b2}
    _L1_ffn_all = _L1_ffn_setup()
    _L1_ffn_in = {k: v for k, v in _L1_ffn_all.items() if k in ('W1', 'b1', 'W2', 'b2')}
    del _L1_ffn_all
    return {'x': x, 'cond_1024': cond_1024, 'L0_cond_router_W': _L0_cond_in['router_W'], 'L0_cond_router_bias': _L0_cond_in['router_bias'], 'L0_cond_w1': _L0_cond_in['w1'], 'L0_cond_w3': _L0_cond_in['w3'], 'L0_cond_w2': _L0_cond_in['w2'], 'L0_cond_W1e': _L0_cond_in['W1e'], 'L0_cond_W2e': _L0_cond_in['W2e'], 'L0_ffn_Wr': _L0_ffn_in['Wr'], 'L0_ffn_br': _L0_ffn_in['br'], 'L0_ffn_W1': _L0_ffn_in['W1'], 'L0_ffn_b1': _L0_ffn_in['b1'], 'L0_ffn_W2': _L0_ffn_in['W2'], 'L0_ffn_b2': _L0_ffn_in['b2'], 'L1_cond_weight': _L1_cond_in['weight'], 'L1_ffn_W1': _L1_ffn_in['W1'], 'L1_ffn_b1': _L1_ffn_in['b1'], 'L1_ffn_W2': _L1_ffn_in['W2'], 'L1_ffn_b2': _L1_ffn_in['b2']}

def reference(x, cond_1024, L0_cond_router_W, L0_cond_router_bias, L0_cond_w1, L0_cond_w3, L0_cond_w2, L0_cond_W1e, L0_cond_W2e, L0_ffn_Wr, L0_ffn_br, L0_ffn_W1, L0_ffn_b1, L0_ffn_W2, L0_ffn_b2, L1_cond_weight, L1_ffn_W1, L1_ffn_b1, L1_ffn_W2, L1_ffn_b2):
    import jax
    import jax.numpy as jnp

    def _L0_cond_ref(x, t_emb, router_W, router_bias, w1, w3, w2, W1e, W2e):
        import jax, jax.numpy as jnp
        import numpy as np
        D, HS, HE, E, K = (256, 512, 256, 8, 2)
        B, T = (4, 256)
        N_SHARED = 1
        Bb, Tt, C = x.shape
        xf = x.reshape(-1, C)
        tf = jnp.broadcast_to(t_emb[:, None, :], (Bb, Tt, C)).reshape(-1, C)
        N = xf.shape[0]
        shared = jax.nn.silu(xf @ w1) * (xf @ w3) @ w2
        s = jax.nn.sigmoid((jnp.concatenate([xf, tf], axis=-1) @ router_W).astype(jnp.float32))
        sel_scores = s + router_bias
        _, topk_idx = jax.lax.top_k(sel_scores, K)
        s_sel = jnp.take_along_axis(s, topk_idx, axis=1)
        denom = s_sel.sum(axis=1, keepdims=True)
        gates = jnp.where(denom > 1e-09, s_sel / (denom + 1e-09), 1.0 / K).astype(x.dtype)
        combine = jnp.zeros((N, E), x.dtype).at[jnp.arange(N)[:, None], topk_idx].add(gates)
        h = jax.nn.gelu(jnp.einsum('nc,ech->enh', xf, W1e), approximate=False)
        y = jnp.einsum('enh,ehc->enc', h, W2e)
        routed = jnp.einsum('ne,enc->nc', combine, y)
        return ((shared + routed) / (N_SHARED + K)).reshape(Bb, Tt, C)

    def _L0_ffn_ref(x, Wr, br, W1, b1, W2, b2):
        import jax, jax.numpy as jnp
        import numpy as np
        B, S, H, E, K = (2, 256, 256, 8, 2)
        D = 2 * H
        logits = jnp.einsum('bsh,he->bse', x, Wr) + br
        probs = jax.nn.softmax(logits, axis=-1)
        top_p, top_i = jax.lax.top_k(probs, K)
        cw = jnp.sum(jax.nn.one_hot(top_i, E, dtype=x.dtype) * top_p[..., None], axis=-2)
        h = jax.nn.relu(jnp.einsum('bsh,ehd->bsed', x, W1) + b1)
        y = jnp.einsum('bsed,edh->bseh', h, W2) + b2
        out = jnp.einsum('bseh,bse->bsh', y, cw)
        return out

    def _L1_cond_ref(Efou, y, weight):
        import jax, jax.numpy as jnp
        import numpy as np
        import math
        IN_F = 256
        OUT_F = 256
        B = 16
        L = 1024
        b, img_size, in_f = Efou.shape
        out_f = weight.shape[1]
        scale = 1.0 / math.sqrt(in_f)
        w = scale * weight[:, :, :, 0] * y[:, None, :]
        dnorm = jax.lax.rsqrt(jnp.sum(w * w, axis=2, keepdims=True) + 1e-08)
        w = w * dnorm
        E = Efou.reshape(b, in_f, img_size)
        x = jnp.einsum('boi,bil->bol', w, E)
        return x.reshape(b, img_size, out_f)

    def _L1_ffn_ref(x, W1, b1, W2, b2):
        import jax, jax.numpy as jnp
        import numpy as np
        EPS = 1e-05

        def _quantize(W):
            gamma = jnp.mean(jnp.abs(W))
            return jnp.clip(jnp.round(W / (gamma + EPS)), -1.0, 1.0)
        Wq1 = _quantize(W1)
        Wq2 = _quantize(W2)
        h = jax.nn.relu(jnp.einsum('bsd,fd->bsf', x, Wq1) + b1)
        out = jnp.einsum('bsf,df->bsd', h, Wq2) + b2
        return out
    x = x + _L0_ffn_ref(_L0_cond_ref(x, cond_1024, L0_cond_router_W, L0_cond_router_bias, L0_cond_w1, L0_cond_w3, L0_cond_w2, L0_cond_W1e, L0_cond_W2e), L0_ffn_Wr, L0_ffn_br, L0_ffn_W1, L0_ffn_b1, L0_ffn_W2, L0_ffn_b2)
    x = x + _L1_ffn_ref(_L1_cond_ref(x, cond_1024, L1_cond_weight), L1_ffn_W1, L1_ffn_b1, L1_ffn_W2, L1_ffn_b2)
    return x

_drawn_inputs = setup_inputs


def setup_inputs(seed=0):
    import zlib

    import numpy as np

    out = dict(_drawn_inputs(seed))
    spreads = {'L0_cond_router_bias': (0.0, 0.8),
     'L0_ffn_br': (0.0, 0.481),
     'L0_ffn_b1': (0.0, 2.0),
     'L0_ffn_b2': (0.0, 2.0)}
    factors = {'L0_cond_router_W': 8.0,
     'L0_cond_w1': 8.0,
     'L0_cond_w3': 8.0,
     'L0_cond_w2': 8.0,
     'L0_cond_W1e': 8.0,
     'L0_cond_W2e': 8.0,
     'L0_ffn_Wr': 8.0,
     'L0_ffn_W1': 8.0,
     'L0_ffn_W2': 3.71,
     'L1_ffn_b1': 64.0,
     'L1_ffn_b2': 64.0}
    for name, (base, spread) in spreads.items():
        noise = np.random.default_rng([zlib.crc32(name.encode()), seed]).standard_normal(out[name].shape)
        drawn = base * np.exp(spread * noise) if base else spread * noise
        out[name] = jnp.asarray(drawn.astype(out[name].dtype))
    for name, factor in factors.items():
        out[name] = (out[name] * factor).astype(out[name].dtype)
    return out
```

```python
import concourse.bass as bass
from concourse import mybir
from concourse.alu_op_type import AluOpType as ALU
from contextlib import ExitStack

P = 128
BATCH, SEQ, D = 64, 64, 256
N = BATCH * SEQ
NT = N // P
KC = D // P
E = 8
HS = 512
HE = 256
HF = 512
DF = 1024
SLOT_TILES = 2 * NT + E
GT = 4
NG = NT // GT
HALF = NT // 2
UNROLL = 4

C_IDENT, C_REV, C_VALUE, C_TILE, C_PAD, C_SEL, C_OWN = 0, 128, 136, 168, 240, 312, 440
C_END = C_OWN + NT
H_LTRI, H_ONES, H_IOTA, H_TILE = 0, 128, 256, 384
H_END = H_TILE + SLOT_TILES


class Tile:

    def __init__(self, t, slot, turn):
        self.t, self.slot, self.turn = t, slot, turn


def pipeline(eng, tiles, lag, body, unroll=UNROLL):

    for s in range(lag):
        for stage in range(lag + 1):
            if s >= stage:
                body(stage, Tile(s - stage, (s - stage) % unroll, (s - stage) // unroll))
    loops = (tiles - lag) // unroll
    with eng.Fori(0, loops) as i:
        for k in range(unroll):
            for stage in range(lag + 1):
                n = lag + k - stage
                body(stage, Tile(i * unroll + n, n % unroll, i + n // unroll))
    for s in range(lag + loops * unroll, tiles + lag):
        for stage in range(lag + 1):
            if s - stage < tiles:
                body(stage, Tile(s - stage, (s - stage) % unroll, (s - stage) // unroll))


def program(nc, x, xT, cond, condTI, modulation, rW, rWc, Wr, rb, br, w13, w2, wexp, b1f, b2f,
            WcT, V1, c1, V2, c2, constf, consth, out):
    F, H, I = mybir.dt.float32, mybir.dt.float16, mybir.dt.int32
    ACT, AX = mybir.ActivationFunctionType, mybir.AxisListType
    TT, TS = nc.vector.tensor_tensor, nc.vector.tensor_scalar
    STT, VCOPY = nc.vector.scalar_tensor_tensor, nc.vector.tensor_copy
    MM, TR = nc.tensor.matmul, nc.tensor.transpose

    def dram(name, shape):
        return nc.dram_tensor(name, shape, F).ap()

    shared_d = dram("shared_out", (N, D))
    cond_d = dram("cond_out", (N, D))
    y_d = dram("cond_slots_out", (2 * N + SLOT_TILES * P, D))
    z_d = dram("ffn_slots_out", (2 * N + SLOT_TILES * P, D))
    norm_d = dram("norms", (KC * 2, BATCH, SEQ))

    root = ExitStack()
    with root:
        def scope():
            st = ExitStack()
            return st, lambda name, shape, dt: st.enter_context(nc.sbuf_tensor(name, shape, dt))

        def sem(name):
            return root.enter_context(nc.semaphore(name))

        def sems(name, n):
            return [sem(f"{name}{i}") for i in range(n)]

        sb = lambda name, shape, dt: root.enter_context(nc.sbuf_tensor(name, shape, dt))
        bank = [root.enter_context(nc.psum_tensor(f"bank{i}", [P, 512], F)) for i in range(8)]

        cf = sb("cf", [P, C_END], F)
        ch = sb("ch", [P, H_END], H)
        ident = cf[:, C_IDENT:C_IDENT + P]
        W1f_hi = sb("W1f_hi", [P, E, KC, HF], H)
        W1f_lo = sb("W1f_lo", [P, E, KC, HF], H)
        W2f_hi = sb("W2f_hi", [P, E, HF // P, D], H)
        W2f_lo = sb("W2f_lo", [P, E, HF // P, D], H)
        gates = [sb("gates_cond", [P, 2, NT], F), sb("gates_ffn", [P, 2, NT], F)]
        gather_idx = sb("gather_idx", [P, SLOT_TILES], I)
        scatter_idx = sb("scatter_idx", [P, SLOT_TILES], I)
        tile_expert = sb("tile_expert", [P, SLOT_TILES], I)
        logits = sb("logits", [P, NT, E], F)
        router_bias = sb("router_bias", [P, 2, E], F)
        ready = lambda t: t + 3
        free = lambda t: t + 1

        pool_passed, pe_passed = sem("pool_passed"), sem("pe_passed")

        chained = sem("vector_chain")
        chain_n = [0]

        def link(ins):
            chain_n[0] += 1
            ins.then_inc(chained, 1)
            nc.vector.wait_ge(chained, chain_n[0])

        def routing(lay, st_sb, names):
            r = {}
            f3 = lambda nm: st_sb(f"{nm}{lay}", [P, NT, E], F)
            r["score"], r["sel"], r["eq"], r["oh1"], r["oh2"], r["pos"] = map(
                f3, ("score", "sel", "eq", "oh1_", "oh2_", "pos"))
            r["m"] = st_sb(f"m{lay}", [P, NT], F)
            r["val"] = st_sb(f"val{lay}", [P, 2, NT], F)
            r["den"] = st_sb(f"den{lay}", [P, NT], F)
            r["choice"] = st_sb(f"choice{lay}", [P, NT, E], H)
            r["cum"] = st_sb(f"cum{lay}", [P, E, NT + 1], F)
            r["scan"] = st_sb(f"scan{lay}", [P, E, NT + 1], F)
            r["zero"] = st_sb(f"zero{lay}", [P, E * (NT + 1)], F)
            r["cnt"] = st_sb(f"cnt{lay}", [P, E], F)
            r["cnti"] = st_sb(f"cnti{lay}", [P, E], I)
            r["posi"] = st_sb(f"posi{lay}", [P, 2, 2 * NT], I)
            r["ab"] = st_sb(f"ab{lay}", [P, 2, 2 * NT], F)
            r["ohb"] = st_sb(f"ohb{lay}", [P, UNROLL, P], H)
            r["oha"] = st_sb(f"oha{lay}", [P, UNROLL, SLOT_TILES], H)
            r["inv"] = st_sb(f"inv{lay}", [P, 4, SLOT_TILES], F)
            r["iw"] = st_sb(f"iw{lay}", [P, 3, SLOT_TILES], F)
            r["ge"] = st_sb(f"ge{lay}", [P, SLOT_TILES, E], F)
            for nm in ("choice_ready", "counted", "onehot_ready", "onehot_used", "inverted"):
                r[nm] = sem(f"{nm}{lay}")
            return r

        def bc_e(ap):
            return ap.unsqueeze(2).to_broadcast([P, NT, E])

        def select_top2(r, lay):
            rev = cf[:, C_REV:C_REV + E].unsqueeze(1).to_broadcast([P, NT, E])
            for k, oh in ((0, r["oh1"]), (1, r["oh2"])):
                link(nc.vector.reduce_max(r["m"][:], r["sel"][:], AX.X))
                link(TT(r["eq"][:], r["sel"][:], bc_e(r["m"][:]), ALU.is_equal))
                link(TT(r["eq"][:], r["eq"][:], rev, ALU.mult))
                link(nc.vector.reduce_max(r["m"][:], r["eq"][:], AX.X))
                link(TT(oh[:], r["eq"][:], bc_e(r["m"][:]), ALU.is_equal))
                if k == 0:
                    link(STT(r["sel"][:], oh[:], -1e30, r["sel"][:], ALU.mult, ALU.add))
                link(TT(r["eq"][:], oh[:], r["score"][:], ALU.mult))
                link(nc.vector.reduce_sum(r["val"][:, k, :], r["eq"][:], AX.X))
            TT(r["choice"][:], r["oh1"][:], r["oh2"][:], ALU.add).then_inc(r["choice_ready"], 1)

        def assign_slots(dve, r, lay, prefix, totals):
            dve.wait_ge(r["counted"], 1)
            te = totals.rearrange("p (t e) -> p e t", e=E)
            link(nc.vector.memset(r["zero"][:], 0.0))
            link(VCOPY(r["cum"][:, :, 0:NT], te))
            link(nc.vector.reduce_sum(r["cnt"][:], r["cum"][:, :, 0:NT], AX.X))
            link(TS(r["cnti"][:], r["cnt"][:], float(P - 1), None, ALU.add))
            link(TS(r["cnti"][:], r["cnti"][:], 7, 7, ALU.logical_shift_right, ALU.logical_shift_left))
            link(TT(r["cum"][:, :, NT], r["cnti"][:], r["cnt"][:], ALU.subtract))
            flat = lambda a: a[:].rearrange("p e t -> p (e t)")
            link(nc.vector.tensor_tensor_scan(flat(r["scan"]), flat(r["cum"]), r["zero"][:], 0.0,
                                              ALU.add, ALU.add))
            ends = r["scan"][:, :, NT].unsqueeze(1).to_broadcast([P, SLOT_TILES, E])
            starts = cf[:, C_TILE:C_TILE + SLOT_TILES].unsqueeze(2).to_broadcast([P, SLOT_TILES, E])
            link(TT(r["ge"][:], ends, starts, ALU.is_le))
            link(nc.vector.reduce_sum(r["iw"][:, 0, :], r["ge"][:], AX.X))
            link(TS(tile_expert[:], r["iw"][:, 0, :], float(E - 1), None, ALU.min))
            link(TT(r["scan"][:], r["scan"][:], r["cum"][:], ALU.subtract))
            link(TT(r["pos"][:], prefix.rearrange("p (t e) -> p t e", e=E),
                    r["scan"][:, :, 0:NT].rearrange("p e t -> p t e"), ALU.add))
            for k, oh in ((0, r["oh1"]), (1, r["oh2"])):
                link(TT(r["eq"][:], oh[:], r["pos"][:], ALU.mult))
                link(nc.vector.reduce_sum(r["m"][:], r["eq"][:], AX.X))
                link(VCOPY(r["posi"][:, 1, k * NT:(k + 1) * NT], r["m"][:]))
            link(TS(r["posi"][:, 0, :], r["posi"][:, 1, :], 7, None, ALU.logical_shift_right))
            link(TS(r["posi"][:, 1, :], r["posi"][:, 1, :], P - 1, None, ALU.bitwise_and))
            link(VCOPY(r["ab"][:], r["posi"][:]))

        def invert_vector(dve, r):
            dve.sem_inc(r["onehot_used"], UNROLL)
            for k in range(2):
                for half in range(2):
                    base = k * NT + half * HALF
                    with dve.Fori(0, HALF // UNROLL) as i:
                        for u in range(UNROLL):
                            c = i * UNROLL + (base + u)
                            tok = i * UNROLL + (half * HALF + u)
                            dve.wait_ge(r["onehot_used"], c + 1)
                            TS(r["ohb"][:, u, :], ch[:, H_IOTA:H_IOTA + P],
                               r["ab"][:, 1, bass.ds(c, 1)], None, ALU.is_equal)
                            TS(r["oha"][:, u, :], ch[:, H_TILE:H_TILE + SLOT_TILES],
                               r["ab"][:, 0, bass.ds(c, 1)],
                               cf[:, bass.ds(tok + C_VALUE, 1)],
                               ALU.is_equal, ALU.mult).then_inc(r["onehot_ready"], 1)

        def invert_tensor(pe, r, inverse):
            for k in range(2):
                for half in range(2):
                    g = 2 * k + half
                    base = k * NT + half * HALF

                    def pair(c, u, first, last):
                        pe.wait_ge(r["onehot_ready"], c + 1)
                        MM(inverse[:, g * SLOT_TILES:(g + 1) * SLOT_TILES], r["ohb"][:, u, :],
                           r["oha"][:, u, :], start=first, stop=last).then_inc(r["onehot_used"], 1)

                    for u in range(UNROLL):
                        pair(base + u, u, u == 0, False)
                    with pe.Fori(1, HALF // UNROLL - 1) as i:
                        for u in range(UNROLL):
                            pair(i * UNROLL + (base + u), u, False, False)
                    for u in range(UNROLL):
                        pair(base + HALF - UNROLL + u, u, False, u == UNROLL - 1)

        def count_choices(pe, r, prefix, totals):
            pe.wait_ge(r["choice_ready"], 1)
            rhs = r["choice"][:].rearrange("p t e -> p (t e)")
            MM(prefix, ch[:, H_LTRI:H_LTRI + P], rhs, start=True, stop=True)
            MM(totals, ch[:, H_ONES:H_ONES + P], rhs, start=True, stop=True).then_inc(r["counted"], 1)

        def finish_slots(dve, r, inverse):
            dve.wait_ge(r["onehot_used"], UNROLL + 2 * NT)
            inv, iw = r["inv"], r["iw"]
            link(VCOPY(inv[:].rearrange("p g s -> p (g s)"), inverse[:, 0:4 * SLOT_TILES]))
            link(TT(iw[:, 0, :], inv[:, 1, :], inv[:, 3, :], ALU.add))
            link(TT(iw[:, 1, :], inv[:, 2, :], inv[:, 3, :], ALU.add))
            link(TT(inv[:, 0, :], inv[:, 0, :], inv[:, 2, :], ALU.add))
            link(TT(inv[:, 0, :], inv[:, 0, :], iw[:, 0, :], ALU.add))
            link(TS(iw[:, 0, :], iw[:, 0, :], 0.0, float(HALF * P), ALU.is_gt, ALU.mult))
            link(TT(inv[:, 0, :], inv[:, 0, :], iw[:, 0, :], ALU.add))
            link(TS(gather_idx[:], inv[:, 0, :], -1.0, 0.0, ALU.add, ALU.max))
            link(TS(iw[:, 1, :], iw[:, 1, :], 0.0, float(N), ALU.is_gt, ALU.mult))
            link(TS(iw[:, 2, :], inv[:, 0, :], 0.0, None, ALU.is_equal))
            link(TT(iw[:, 2, :], iw[:, 2, :], cf[:, C_PAD:C_PAD + SLOT_TILES], ALU.mult))
            link(TT(iw[:, 1, :], iw[:, 1, :], iw[:, 2, :], ALU.add))
            link(TT(iw[:, 1, :], iw[:, 1, :], inv[:, 0, :], ALU.add))
            link(TS(scatter_idx[:], iw[:, 1, :], -1.0, None, ALU.add))

        def experts(lay, src, dst, up_hi, up_lo, down_hi, down_lo, hidden, b1_all, b2_all):
            HC = hidden // P
            ffn = b1_all is not None
            nm = "ffn_" if ffn else "cond_"
            S = lambda n: sem(nm + n)
            x_in, y_out = sems(nm + "x_in", UNROLL), sems(nm + "y_out", UNROLL)
            gidx_ready, sidx_ready = S("gidx_ready"), S("sidx_ready")
            x_posed, xhi_done, xlo_done, up_done = S("x_posed"), S("xhi_done"), S("xlo_done"), S("up_done")
            act_done, h_posed, hhi_done, hlo_done = S("act_done"), S("h_posed"), S("hhi_done"), S("hlo_done")
            down_done, y_done = S("down_done"), S("y_done")
            st, psb = scope()
            with st:
                xg = psb(nm + "xg", [P, UNROLL, D], F)
                gi = psb(nm + "gi", [P, UNROLL, 1], I)
                si = psb(nm + "si", [P, UNROLL, 1], I)
                xb_hi = psb(nm + "xb_hi", [P, 2, KC, P], H)
                xb_lo = psb(nm + "xb_lo", [P, 2, KC, P], H)
                hs = psb(nm + "hs", [P, 2, hidden], F)
                hb_hi = psb(nm + "hb_hi", [P, 2, HC, P], H)
                hb_lo = psb(nm + "hb_lo", [P, 2, HC, P], H)
                yo = psb(nm + "yo", [P, UNROLL, D], F)
                xT_ps = [bank[0][:, 0:D], bank[1][:, 0:D]]
                up_ps = [bank[2][:, 0:hidden], bank[3][:, 0:hidden]]
                hT_ps = [bank[4][:, 0:hidden], bank[5][:, 0:hidden]]
                y_ps = [bank[6][:, 0:D], bank[7][:, 0:D]]
                flat = lambda a, b: a[:, b].rearrange("p c n -> p (c n)")

                with nc.Block() as block:
                    @block.gpsimd
                    def _(pool):
                        def body(stage, c):
                            if stage == 0:
                                pool.wait_ge(x_posed, free(c.t))
                                nc.gpsimd.tensor_copy(gi[:, c.slot, :], gather_idx[:, bass.ds(c.t, 1)]).then_inc(gidx_ready, 1)
                                pool.wait_ge(gidx_ready, c.t + 1)
                                pool.sem_inc(pool_passed, 1)
                                pool.indirect_dma_start(
                                    out=xg[:, c.slot, :], out_offset=None, in_=src,
                                    in_offset=bass.IndirectOffsetOnAxis(ap=gi[:, c.slot, :], axis=0),
                                ).then_inc(x_in[c.slot], 16)
                            if stage == 5:
                                pool.wait_ge(y_out[c.slot], c.turn * 16)
                                nc.gpsimd.tensor_copy(si[:, c.slot, :], scatter_idx[:, bass.ds(c.t, 1)]).then_inc(sidx_ready, 1)
                                pool.wait_ge(sidx_ready, c.t + 1)
                                pool.wait_ge(y_done, ready(c.t))
                                pool.sem_inc(pool_passed, 1)
                                pool.indirect_dma_start(
                                    out=dst, out_offset=bass.IndirectOffsetOnAxis(ap=si[:, c.slot, :], axis=0),
                                    in_=yo[:, c.slot, :], in_offset=None).then_inc(y_out[c.slot], 16)

                        pool.sem_inc(x_posed, UNROLL)
                        pipeline(pool, SLOT_TILES, 5, body)
                        for u in range(UNROLL):
                            pool.wait_ge(y_out[u], 16 * (SLOT_TILES // UNROLL))

                    @block.tensor
                    def _(pe):
                        def expert_of(t):
                            return pe.value_load(tile_expert[0:1, bass.ds(t, 1)], min_val=0, max_val=E - 1)

                        def body(stage, c):
                            b = c.slot % 2
                            if stage == 0:
                                pe.wait_ge(x_in[c.slot], (c.turn + 1) * 16)
                                pe.wait_ge(xlo_done, free(c.t))
                                for kc in range(KC):
                                    last = TR(xT_ps[b][:, kc * P:(kc + 1) * P],
                                              xg[:, c.slot, kc * P:(kc + 1) * P], ident)
                                last.then_inc(x_posed, 1)
                            if stage == 1:
                                e = expert_of(c.t)
                                pe.wait_ge(xlo_done, ready(c.t))
                                pe.wait_ge(act_done, free(c.t))
                                for kc in range(KC):
                                    wh = up_hi[:, bass.ds(e, 1), kc, :].rearrange("p o n -> p (o n)")
                                    wl = up_lo[:, bass.ds(e, 1), kc, :].rearrange("p o n -> p (o n)")
                                    MM(up_ps[b], xb_hi[:, b, kc, :], wh, start=(kc == 0), stop=False)
                                    MM(up_ps[b], xb_lo[:, b, kc, :], wh, start=False, stop=False)
                                    last = MM(up_ps[b], xb_hi[:, b, kc, :], wl, start=False, stop=(kc == KC - 1))
                                last.then_inc(up_done, 1)
                            if stage == 2:
                                pe.wait_ge(act_done, ready(c.t))
                                pe.wait_ge(hlo_done, free(c.t))
                                for hc in range(HC):
                                    last = TR(hT_ps[b][:, hc * P:(hc + 1) * P],
                                              hs[:, b, hc * P:(hc + 1) * P], ident)
                                last.then_inc(h_posed, 1)
                            if stage == 3:
                                e = expert_of(c.t)
                                pe.wait_ge(hlo_done, ready(c.t))
                                pe.wait_ge(y_done, free(c.t))
                                for hc in range(HC):
                                    wh = down_hi[:, bass.ds(e, 1), hc, :].rearrange("p o n -> p (o n)")
                                    wl = down_lo[:, bass.ds(e, 1), hc, :].rearrange("p o n -> p (o n)")
                                    MM(y_ps[b], hb_hi[:, b, hc, :], wh, start=(hc == 0), stop=False)
                                    MM(y_ps[b], hb_lo[:, b, hc, :], wh, start=False, stop=False)
                                    last = MM(y_ps[b], hb_hi[:, b, hc, :], wl, start=False, stop=(hc == HC - 1))
                                last.then_inc(down_done, 1)

                        pipeline(pe, SLOT_TILES, 3, body)

                    @block.scalar
                    def _(act):
                        def body(stage, c):
                            b = c.slot % 2
                            if stage == 0:
                                act.wait_ge(x_posed, c.t + 1 + UNROLL)
                                act.wait_ge(up_done, free(c.t))
                                nc.scalar.activation(flat(xb_hi, b), xT_ps[b], ACT.Copy).then_inc(xhi_done, 1)
                            if stage == 1 and not ffn:
                                act.wait_ge(up_done, ready(c.t))
                                act.wait_ge(h_posed, free(c.t))
                                nc.scalar.activation(hs[:, b, :], up_ps[b], ACT.Gelu).then_inc(act_done, 1)
                            if stage == 2:
                                act.wait_ge(h_posed, ready(c.t))
                                act.wait_ge(down_done, free(c.t))
                                nc.scalar.activation(flat(hb_hi, b), hT_ps[b],
                                                     ACT.Relu if ffn else ACT.Copy).then_inc(hhi_done, 1)

                        for s in (up_done, h_posed, down_done):
                            act.sem_inc(s, 2)
                        pipeline(act, SLOT_TILES, 2, body)

                    @block.vector
                    def _(dve):
                        def expert_of(t):
                            return dve.value_load(tile_expert[0:1, bass.ds(t, 1)], min_val=0, max_val=E - 1)

                        def body(stage, c):
                            b = c.slot % 2
                            if stage == 0:
                                dve.wait_ge(xhi_done, c.t + 1)
                                TT(flat(xb_lo, b), xT_ps[b], flat(xb_hi, b), ALU.subtract).then_inc(xlo_done, 1)
                            if stage == 1 and ffn:
                                e = expert_of(c.t)
                                dve.wait_ge(up_done, ready(c.t))
                                dve.wait_ge(h_posed, free(c.t))
                                TT(hs[:, b, :], up_ps[b],
                                   b1_all[:, bass.ds(e, 1), :].rearrange("p o n -> p (o n)"),
                                   ALU.add).then_inc(act_done, 1)
                            if stage == 2:
                                dve.wait_ge(hhi_done, c.t + 1)
                                if ffn:
                                    i = STT(flat(hb_lo, b), hT_ps[b], 0.0, flat(hb_hi, b), ALU.max, ALU.subtract)
                                else:
                                    i = TT(flat(hb_lo, b), hT_ps[b], flat(hb_hi, b), ALU.subtract)
                                i.then_inc(hlo_done, 1)
                            if stage == 3:
                                if ffn:
                                    e = expert_of(c.t)
                                dve.wait_ge(down_done, ready(c.t))
                                dve.wait_ge(y_out[c.slot], c.turn * 16)
                                if ffn:
                                    i = TT(yo[:, c.slot, :], y_ps[b],
                                           b2_all[:, bass.ds(e, 1), :].rearrange("p o n -> p (o n)"), ALU.add)
                                else:
                                    i = VCOPY(yo[:, c.slot, :], y_ps[b])
                                i.then_inc(y_done, 1)

                        for s in (xlo_done, act_done, hlo_done, y_done):
                            dve.sem_inc(s, 2)
                        pipeline(dve, SLOT_TILES, 3, body)

        cond_scope, csb = scope()
        with cond_scope:
            W1e_hi, W1e_lo = csb("W1e_hi", [P, E, KC, HE], H), csb("W1e_lo", [P, E, KC, HE], H)
            W2e_hi, W2e_lo = csb("W2e_hi", [P, E, HE // P, D], H), csb("W2e_lo", [P, E, HE // P, D], H)
            parts = []
            at = 0
            for hi, lo, n in ((W1e_hi, W1e_lo, KC * HE), (W2e_hi, W2e_lo, HE // P * D),
                              (W1f_hi, W1f_lo, KC * HF), (W2f_hi, W2f_lo, HF // P * D)):
                parts.append((hi, lo, at, at + n))
                at += n
            WEXP = at
            SC = HS // P

            a_scope, asb = scope()
            with a_scope:
                xT_hi, xT_lo = asb("xT_hi", [P, NG, KC, 512], H), asb("xT_lo", [P, NG, KC, 512], H)
                w13_hi, w13_lo = asb("w13_hi", [P, KC, 2 * HS], H), asb("w13_lo", [P, KC, 2 * HS], H)
                w2_hi, w2_lo = asb("w2_hi", [P, SC, D], H), asb("w2_lo", [P, SC, D], H)
                stage = asb("stage", [P, WEXP], F)
                rW_f, rW_hi, rW_lo = (asb("rW_f", [P, KC, E], F), asb("rW_hi", [P, KC, E], H),
                                      asb("rW_lo", [P, KC, E], H))
                rWc_sb = asb("rWc_sb", [P, KC, E], F)
                condT = asb("condT", [P, KC, BATCH], F)
                cond_logit = asb("cond_logit", [BATCH, NT, E], F)
                logT = asb("logT", [E, 2, 512], F)
                h_hi, h_lo = asb("h_hi", [P, 2, SC, 512], H), asb("h_lo", [P, 2, SC, 512], H)
                work = asb("work", [P, 4, 512], F)
                xstage = work[:].rearrange("p (b k) n -> p b k n", b=2)
                silu, prod = work[:, 0:2, :], work[:, 2:4, :]
                ys = asb("ys", [P, GT, D], F)
                r = routing(0, asb, None)

                consts_in, rw_in, shared_w_in = sem("consts_in"), sem("rw_in"), sem("shared_w_in")
                xT_in = sems("xT_in", 2)
                rw_split, x_hi_done, x_lo_done = sem("rw_split"), sem("x_hi_done"), sem("x_lo_done")
                logT_done, logT_copied, log_posed, log_copied = map(
                    sem, ("logT_done", "logT_copied", "log_posed", "log_copied"))
                cl_done, cl_spread, cl_added = sem("cl_done"), sem("cl_spread"), sem("cl_added")
                z_ready, s_ready = sem("z_ready"), sem("s_ready")
                shw_hi, shw_lo = sem("shw_hi"), sem("shw_lo")
                exp_in, exp_hi, exp_lo = sem("exp_in"), sem("exp_hi"), sem("exp_lo")
                sh_up, sh_silu, sh_prod, sh_hi, sh_lo = map(
                    sem, ("sh_up", "sh_silu", "sh_prod", "sh_hi", "sh_lo"))
                sh_down, sh_y = sem("sh_down"), sem("sh_y")
                sh_out = sems("sh_out", GT)
                SHW = 2 * KC * HS + SC * D
                f2 = lambda ap: ap.rearrange("p k n -> p (k n)")

                with nc.Block() as block:
                    @block.sync
                    def _(sp):
                        sp.dma_start(cf[:], constf).then_inc(consts_in, 16)
                        sp.dma_start(ch[:], consth).then_inc(consts_in, 16)
                        sp.dma_start(router_bias[:, 0, :], rb.partition_broadcast(P)).then_inc(consts_in, 16)
                        sp.dma_start(router_bias[:, 1, :], br.partition_broadcast(P)).then_inc(consts_in, 16)
                        sp.dma_start(rW_f[:], rW).then_inc(rw_in, 16)
                        sp.dma_start(rWc_sb[:], rWc).then_inc(rw_in, 16)
                        sp.dma_start(condT[:], cond).then_inc(rw_in, 16)
                        for g in range(2):
                            sp.dma_start(xstage[:, g], xT[:, g]).then_inc(xT_in[g], 16)
                        sp.dma_start(stage[:, 0:2 * KC * HS], w13).then_inc(shared_w_in, 16)
                        sp.dma_start(stage[:, 2 * KC * HS:SHW], w2).then_inc(shared_w_in, 16)
                        with sp.Fori(1, NG // 2) as i:
                            for b in range(2):
                                sp.wait_ge(x_lo_done, i * 2 + (b - 1))
                                sp.dma_start(xstage[:, b], xT[:, bass.ds(i * 2 + b, 1)].rearrange(
                                    "p o k n -> p (o k) n")).then_inc(xT_in[b], 16)
                        sp.wait_ge(shw_lo, 1)
                        sp.dma_start(stage[:], wexp[:, 0]).then_inc(exp_in, 16)

                        def body(st, c):
                            if st == 1:
                                for u in range(GT):
                                    sp.wait_ge(sh_y, ready(c.t * GT + u))
                                    sp.dma_start(shared_d[bass.ds(c.t * (GT * P) + u * P, P), :],
                                                 ys[:, u, :]).then_inc(sh_out[u], 16)
                            if st == 0 and not (isinstance(c.t, int) and c.t == 0):
                                sp.wait_ge(exp_lo, c.t)
                                sp.dma_start(stage[:], wexp[:, bass.ds(c.t, 1)].rearrange(
                                    "p o n -> p (o n)")).then_inc(exp_in, 16)

                        pipeline(sp, NG, 1, body, unroll=2)
                        for u in range(GT):
                            sp.wait_ge(sh_out[u], 16 * NG)

                    @block.tensor
                    def _(pe):
                        pe.wait_ge(rw_in, 48)
                        for kc in range(KC):
                            last = MM(bank[4][0:BATCH, 0:E], condT[:, kc, :], rWc_sb[:, kc, :],
                                      start=(kc == 0), stop=(kc == KC - 1))
                        last.then_inc(cl_done, 1)
                        pe.wait_ge(cl_spread, 1)
                        MM(bank[3][:, 0:NT * E], cf[0:BATCH, C_SEL:C_SEL + P],
                           cond_logit[:].rearrange("b t e -> b (t e)"), start=True, stop=True).then_inc(cl_added, 1)
                        pe.wait_ge(rw_split, 2)

                        def body(st, c):
                            b = c.slot % 2
                            if st == 0:
                                pe.wait_ge(x_lo_done, c.t + 1)
                                pe.wait_ge(logT_copied, free(c.t))
                                for kc in range(KC):
                                    xh = xT_hi[:, bass.ds(c.t, 1), kc, :].rearrange("p o n -> p (o n)")
                                    xl = xT_lo[:, bass.ds(c.t, 1), kc, :].rearrange("p o n -> p (o n)")
                                    o = bank[5 + b][0:E, :]
                                    MM(o, rW_hi[:, kc, :], xh, start=(kc == 0), stop=False)
                                    MM(o, rW_lo[:, kc, :], xh, start=False, stop=False)
                                    last = MM(o, rW_hi[:, kc, :], xl, start=False, stop=(kc == KC - 1))
                                last.then_inc(logT_done, 1)
                            if st == 1:
                                pe.wait_ge(logT_copied, ready(c.t))
                                pe.wait_ge(log_copied, free(c.t))
                                pe.sem_inc(pe_passed, 1)
                                for u in range(GT):
                                    last = TR(bank[1 + b][:, u * E:(u + 1) * E], logT[:, b, u * P:(u + 1) * P],
                                              cf[0:E, C_IDENT:C_IDENT + E])
                                last.then_inc(log_posed, 1)

                        pipeline(pe, NG, 1, body, unroll=2)
                        count_choices(pe, r, bank[0][:, 0:NT * E], bank[1][:, 0:NT * E])
                        invert_tensor(pe, r, bank[7])

                        pe.wait_ge(shw_lo, 1)

                        def shared(st, c):
                            b = c.slot % 2
                            if st == 0:
                                for j in range(SC):
                                    n = c.t * SC + j
                                    pe.wait_ge(sh_prod, free(n))
                                    for m in range(2):
                                        o = bank[2 * (j % 2) + m][:, :]
                                        cols = slice(m * HS + j * P, m * HS + (j + 1) * P)
                                        for kc in range(KC):
                                            xh = xT_hi[:, bass.ds(c.t, 1), kc, :].rearrange("p o n -> p (o n)")
                                            xl = xT_lo[:, bass.ds(c.t, 1), kc, :].rearrange("p o n -> p (o n)")
                                            MM(o, w13_hi[:, kc, cols], xh, start=(kc == 0), stop=False)
                                            MM(o, w13_hi[:, kc, cols], xl, start=False, stop=False)
                                            last = MM(o, w13_lo[:, kc, cols], xh, start=False, stop=(kc == KC - 1))
                                    last.then_inc(sh_up, 1)
                            else:
                                pe.wait_ge(sh_lo, (c.t + 1) * SC)
                                for u in range(GT):
                                    pe.wait_ge(sh_y, free(c.t * GT + u))
                                    o = bank[4 + u % 2][:, 0:D]
                                    for hc in range(SC):
                                        tok = slice(u * P, (u + 1) * P)
                                        MM(o, h_hi[:, b, hc, tok], w2_hi[:, hc, :], start=(hc == 0), stop=False)
                                        MM(o, h_hi[:, b, hc, tok], w2_lo[:, hc, :], start=False, stop=False)
                                        last = MM(o, h_lo[:, b, hc, tok], w2_hi[:, hc, :], start=False, stop=(hc == SC - 1))
                                    last.then_inc(sh_down, 1)

                        pipeline(pe, NG, 1, shared, unroll=2)

                    @block.scalar
                    def _(act):
                        act.sem_inc(logT_copied, 2)
                        act.sem_inc(log_copied, 2)
                        act.sem_inc(log_posed, 2)
                        act.sem_inc(sh_y, 2)
                        act.sem_inc(sh_down, 2 * GT)
                        act.wait_ge(rw_in, 48)
                        nc.scalar.activation(f2(rW_hi[:]), f2(rW_f[:]), ACT.Copy).then_inc(rw_split, 1)

                        def body(st, c):
                            b = c.slot % 2
                            if st == 0:
                                act.wait_ge(xT_in[b], (c.turn + 1) * 16)
                                nc.scalar.activation(
                                    xT_hi[:, bass.ds(c.t, 1), :, :].rearrange("p o k n -> p (o k n)"),
                                    f2(xstage[:, b]), ACT.Copy).then_inc(x_hi_done, 1)
                            if st == 1:
                                act.wait_ge(logT_done, c.t + 1)
                                act.wait_ge(log_posed, free(c.t))
                                nc.scalar.activation(logT[:, b, :], bank[5 + b][0:E, :], ACT.Copy).then_inc(logT_copied, 1)
                            if st == 2:
                                act.wait_ge(log_posed, ready(c.t))
                                nc.scalar.activation(
                                    logits[:, bass.ds(c.t * GT, GT), :].rearrange("p t e -> p (t e)"),
                                    bank[1 + b][:, 0:GT * E], ACT.Copy).then_inc(log_copied, 1)

                        pipeline(act, NG, 2, body, unroll=2)
                        act.wait_ge(z_ready, 1)
                        nc.scalar.activation(r["score"][:], r["sel"][:], ACT.Sigmoid).then_inc(s_ready, 1)
                        act.wait_ge(shared_w_in, 32)
                        nc.scalar.activation(f2(w13_hi[:]), stage[:, 0:2 * KC * HS], ACT.Copy)
                        nc.scalar.activation(f2(w2_hi[:]), stage[:, 2 * KC * HS:SHW], ACT.Copy).then_inc(shw_hi, 1)

                        def shared(st, c):
                            b = c.slot % 2
                            if st == 0:
                                for j in range(SC):
                                    n = c.t * SC + j
                                    act.wait_ge(sh_up, n + 1)
                                    act.wait_ge(sh_prod, free(n))
                                    nc.scalar.activation(silu[:, j % 2, :], bank[2 * (j % 2)][:, :],
                                                         ACT.Silu).then_inc(sh_silu, 1)
                                act.wait_ge(exp_in, (c.t + 1) * 16)
                                for hi, lo, a, z in parts:
                                    last = nc.scalar.activation(
                                        hi[:, bass.ds(c.t, 1), :, :].rearrange("p o k n -> p (o k n)"),
                                        stage[:, a:z], ACT.Copy)
                                last.then_inc(exp_hi, 1)
                            else:
                                for u in range(GT):
                                    n = c.t * GT + u
                                    act.wait_ge(sh_down, n + (1 + 2 * GT))
                                    act.wait_ge(sh_out[u], c.t * 16)
                                    nc.scalar.activation(ys[:, u, :], bank[4 + u % 2][:, 0:D], ACT.Copy,
                                                         scale=1.0 / 3.0).then_inc(sh_y, 1)

                        pipeline(act, NG, 1, shared, unroll=2)

                    @block.vector
                    def _(dve):
                        dve.sem_inc(sh_prod, 2)
                        dve.wait_ge(rw_split, 1)
                        TT(f2(rW_lo[:]), f2(rW_f[:]), f2(rW_hi[:]), ALU.subtract).then_inc(rw_split, 1)
                        dve.wait_ge(consts_in, 64)
                        dve.wait_ge(cl_done, 1)
                        TT(cond_logit[:], bank[4][0:BATCH, 0:E].unsqueeze(1).to_broadcast([BATCH, NT, E]),
                           cf[0:BATCH, C_OWN:C_OWN + NT].unsqueeze(2).to_broadcast([BATCH, NT, E]),
                           ALU.mult).then_inc(cl_spread, 1)

                        def body(st, c):
                            b = c.slot % 2
                            dve.wait_ge(x_hi_done, c.t + 1)
                            TT(xT_lo[:, bass.ds(c.t, 1), :, :].rearrange("p o k n -> p (o k n)"),
                               f2(xstage[:, b]),
                               xT_hi[:, bass.ds(c.t, 1), :, :].rearrange("p o k n -> p (o k n)"),
                               ALU.subtract).then_inc(x_lo_done, 1)

                        pipeline(dve, NG, 0, body, unroll=2)
                        dve.wait_ge(log_copied, 2 + NG)
                        dve.wait_ge(cl_added, 1)
                        TT(r["sel"][:], logits[:], bank[3][:, 0:NT * E].rearrange("p (t e) -> p t e", e=E),
                           ALU.add).then_inc(z_ready, 1)
                        dve.wait_ge(s_ready, 1)
                        link(TT(r["sel"][:], r["score"][:],
                                router_bias[:, 0, :].unsqueeze(1).to_broadcast([P, NT, E]), ALU.add))
                        select_top2(r, 0)
                        g0 = gates[0]
                        link(TT(r["den"][:], r["val"][:, 0, :], r["val"][:, 1, :], ALU.add))
                        link(TS(r["m"][:], r["den"][:], 1e-9, None, ALU.is_gt))
                        link(TS(r["den"][:], r["den"][:], 1e-9, None, ALU.add))
                        link(nc.vector.reciprocal(r["den"][:], r["den"][:]))
                        for k in range(2):
                            link(TT(g0[:, k, :], r["val"][:, k, :], r["den"][:], ALU.mult))
                            link(TS(g0[:, k, :], g0[:, k, :], -0.5, None, ALU.add))
                            link(TT(g0[:, k, :], g0[:, k, :], r["m"][:], ALU.mult))
                            link(TS(g0[:, k, :], g0[:, k, :], 0.5, 1.0 / 3.0, ALU.add, ALU.mult))
                        assign_slots(dve, r, 0, bank[0][:, 0:NT * E], bank[1][:, 0:NT * E])
                        invert_vector(dve, r)
                        finish_slots(dve, r, bank[7])
                        dve.wait_ge(shw_hi, 1)
                        TT(f2(w13_lo[:]), stage[:, 0:2 * KC * HS], f2(w13_hi[:]), ALU.subtract)
                        TT(f2(w2_lo[:]), stage[:, 2 * KC * HS:SHW], f2(w2_hi[:]), ALU.subtract).then_inc(shw_lo, 1)

                        def shared(st, c):
                            b = c.slot % 2
                            for j in range(SC):
                                n = c.t * SC + j
                                dve.wait_ge(sh_silu, n + 1)
                                TT(prod[:, j % 2, :], silu[:, j % 2, :], bank[2 * (j % 2) + 1][:, :],
                                   ALU.mult).then_inc(sh_prod, 1)
                                dve.wait_ge(sh_prod, ready(n))
                                if j == 0:
                                    dve.wait_ge(sh_down, c.t * GT + GT)
                                VCOPY(h_hi[:, b, j, :], prod[:, j % 2, :]).then_inc(sh_hi, 1)
                                dve.wait_ge(sh_hi, n + 1)
                                TT(h_lo[:, b, j, :], prod[:, j % 2, :], h_hi[:, b, j, :], ALU.subtract).then_inc(sh_lo, 1)
                            dve.wait_ge(exp_hi, c.t + 1)
                            for hi, lo, a, z in parts:
                                last = TT(lo[:, bass.ds(c.t, 1), :, :].rearrange("p o k n -> p (o k n)"),
                                          stage[:, a:z],
                                          hi[:, bass.ds(c.t, 1), :, :].rearrange("p o k n -> p (o k n)"),
                                          ALU.subtract)
                            last.then_inc(exp_lo, 1)

                        pipeline(dve, NG, 0, shared, unroll=2)

            experts(0, x, y_d, W1e_hi, W1e_lo, W2e_hi, W2e_lo, HE, None, None)

        late_scope, lsb = scope()
        with late_scope:
            b1_all, b2_all = lsb("b1_all", [P, E, HF], F), lsb("b2_all", [P, E, D], F)
            WT_hi, WT_lo = lsb("WT_hi", [P, 2, D], H), lsb("WT_lo", [P, 2, D], H)
            FC = DF // P
            V1_q, V2_q = lsb("V1_q", [P, KC, DF], H), lsb("V2_q", [P, FC, D], H)
            c1_sb, c2_sb = lsb("c1_sb", [P, FC], F), lsb("c2_sb", [P, D], F)
            modul = lsb("modul", [P, NT, 4], F)

            c_scope, csb2 = scope()
            with c_scope:
                r = routing(1, csb2, None)
                y0, y1, sh = (csb2(n, [P, UNROLL, D], F) for n in ("y0", "y1", "sh"))
                part, co = csb2("part", [P, 2, D], F), csb2("co", [P, UNROLL, D], F)
                xc_hi, xc_lo = csb2("xc_hi", [P, 2, KC, P], H), csb2("xc_lo", [P, 2, KC, P], H)
                Wr_f, Wr_hi, Wr_lo = (csb2("Wr_f", [P, KC, E], F), csb2("Wr_hi", [P, KC, E], H),
                                      csb2("Wr_lo", [P, KC, E], H))
                V_f = csb2("V_f", [P, 2, KC * DF], F)
                above = csb2("above", [P, KC * DF], H)
                below = csb2("below", [P, KC * DF], H)
                asum, limit = csb2("asum", [P, 2], F), csb2("limit", [P, 2, 2], F)
                Wc_f = csb2("Wc_f", [P, 2, D], F)
                Wsq = csb2("Wsq", [P, 2, D], F)
                cI, cIsq = csb2("cI", [P, 2, BATCH], F), csb2("cIsq", [P, 2, BATCH], F)
                nrm = csb2("nrm", [BATCH, D], F)
                onesf = csb2("onesf", [P, P], F)
                y_in = sems("cy_in", UNROLL)
                c_out = sems("c_out", UNROLL)
                (wr_in, wr_split, w_in, v_in, part_done, part_sum, co_done, co_posed, xchi_done, xclo_done,
                 rl_done, rl_copied, c_shift, c_exp) = map(sem, (
                     "wr_in", "wr_split", "w_in", "v_in", "part_done", "part_sum", "co_done", "co_posed",
                     "xchi_done", "xclo_done", "rl_done", "rl_copied", "c_shift", "c_exp"))
                (abs_done, ones_done, sum_done, limit_done, above_done, below_done, quant_done, sq_done,
                 ss_done, eps_done, root_done, nrm_done, wt_hi, nrm_out) = map(sem, (
                     "abs_done", "ones_done", "sum_done", "limit_done", "above_done", "below_done",
                     "quant_done", "sq_done", "ss_done", "eps_done", "root_done", "nrm_done", "wt_hi",
                     "nrm_out"))
                f2 = lambda ap: ap.rearrange("p k n -> p (k n)")

                with nc.Block() as block:
                    @block.sync
                    def _(sp):
                        sp.dma_start(Wr_f[:], Wr).then_inc(wr_in, 16)

                        def body(st, c):
                            if st == 0:
                                sp.wait_ge(co_done, free(c.t) + (-2)) if not isinstance(c.t, int) or c.t >= 4 else None
                                for t, s in ((y0, y_d[bass.ds(c.t * P, P), :]),
                                             (y1, y_d[bass.ds(c.t * P + N, P), :]),
                                             (sh, shared_d[bass.ds(c.t * P, P), :])):
                                    sp.dma_start(t[:, c.slot, :], s).then_inc(y_in[c.slot], 16)
                            if st == 4:
                                sp.wait_ge(co_done, ready(c.t))
                                sp.dma_start(cond_d[bass.ds(c.t * P, P), :], co[:, c.slot, :]).then_inc(c_out[c.slot], 16)

                        pipeline(sp, NT, 4, body)
                        for t, s in ((b1_all[:], b1f.partition_broadcast(P)), (b2_all[:], b2f.partition_broadcast(P)),
                                     (c1_sb[:], c1), (c2_sb[:], c2.partition_broadcast(P)),
                                     (modul[:], modulation), (cI[:], condTI), (Wc_f[:], WcT)):
                            sp.dma_start(t, s).then_inc(w_in, 16)
                        sp.dma_start(V_f[:, 0, :], V1).then_inc(v_in, 16)
                        sp.dma_start(V_f[:, 1, :], V2).then_inc(v_in, 16)
                        for u in range(UNROLL):
                            sp.wait_ge(c_out[u], 16 * (NT // UNROLL))
                        sp.wait_ge(w_in, 16 * 7)
                        sp.wait_ge(nrm_done, 1)
                        sp.dma_start(norm_d.rearrange("g b t -> b g t"),
                                     nrm[:].rearrange("b (g t) -> b g t", t=SEQ)).then_inc(nrm_out, 16)
                        sp.wait_ge(nrm_out, 16)

                    @block.gpsimd
                    def _(pool):
                        nc.gpsimd.memset(onesf[:], 1.0).then_inc(ones_done, 1)

                        def body(st, c):
                            b = c.slot % 2
                            pool.wait_ge(part_done, ready(c.t))
                            nc.gpsimd.tensor_tensor(part[:, b, :], part[:, b, :], sh[:, c.slot, :],
                                                    ALU.add).then_inc(part_sum, 1)

                        pipeline(pool, NT, 0, body)
                        pool.wait_ge(limit_done, 2)
                        for m, q in ((0, f2(V1_q[:])), (1, f2(V2_q[:]))):
                            if m:
                                pool.wait_ge(quant_done, 1)
                            nc.gpsimd.tensor_scalar(above[:], V_f[:, m, :], limit[:, 0, m:m + 1], None,
                                                    ALU.is_gt).then_inc(above_done, 1)
                            nc.gpsimd.tensor_scalar(below[:], V_f[:, m, :], limit[:, 1, m:m + 1], None,
                                                    ALU.is_lt).then_inc(above_done, 1)
                            pool.wait_ge(above_done, 2 * (m + 1))
                            nc.gpsimd.tensor_tensor(q, above[:], below[:], ALU.subtract).then_inc(quant_done, 1)

                    @block.tensor
                    def _(pe):
                        pe.wait_ge(wr_split, 2)

                        def body(st, c):
                            b = c.slot % 2
                            if st == 0:
                                pe.wait_ge(co_done, ready(c.t))
                                pe.wait_ge(xclo_done, free(c.t))
                                for kc in range(KC):
                                    last = TR(bank[b][:, kc * P:(kc + 1) * P], co[:, c.slot, kc * P:(kc + 1) * P], ident)
                                last.then_inc(co_posed, 1)
                            if st == 1:
                                pe.wait_ge(xclo_done, ready(c.t))
                                pe.wait_ge(rl_copied, free(c.t))
                                o = bank[2 + b][:, 0:E]
                                for kc in range(KC):
                                    MM(o, xc_hi[:, b, kc, :], Wr_hi[:, kc, :], start=(kc == 0), stop=False)
                                    MM(o, xc_hi[:, b, kc, :], Wr_lo[:, kc, :], start=False, stop=False)
                                    last = MM(o, xc_lo[:, b, kc, :], Wr_hi[:, kc, :], start=False, stop=(kc == KC - 1))
                                last.then_inc(rl_done, 1)

                        pipeline(pe, NT, 1, body)
                        count_choices(pe, r, bank[4][:, 0:NT * E], bank[5][:, 0:NT * E])
                        pe.wait_ge(ones_done, 1)
                        pe.wait_ge(abs_done, 1)
                        MM(bank[6][:, 0:2], onesf[:], asum[:], start=True, stop=True).then_inc(sum_done, 1)
                        pe.wait_ge(sq_done, 1)
                        for ql in range(2):
                            last = MM(bank[3][0:BATCH, 0:D], cIsq[:, ql, :], Wsq[:, ql, :], start=(ql == 0), stop=(ql == 1))
                        last.then_inc(ss_done, 1)
                        invert_tensor(pe, r, bank[7])

                    @block.scalar
                    def _(act):
                        act.sem_inc(part_done, 2)
                        act.sem_inc(rl_copied, 2)
                        act.sem_inc(co_posed, 2)
                        act.sem_inc(rl_done, 2)
                        act.wait_ge(wr_in, 16)
                        nc.scalar.activation(f2(Wr_hi[:]), f2(Wr_f[:]), ACT.Copy).then_inc(wr_split, 1)

                        def body(st, c):
                            b = c.slot % 2
                            if st == 0:
                                act.wait_ge(y_in[c.slot], (c.turn + 1) * 48)
                                act.wait_ge(co_done, free(c.t))
                                nc.scalar.activation(part[:, b, :], y0[:, c.slot, :], ACT.Copy,
                                                     scale=gates[0][:, 0, bass.ds(c.t, 1)]).then_inc(part_done, 1)
                            if st == 1:
                                act.wait_ge(co_posed, ready(c.t))
                                act.wait_ge(rl_done, free(c.t))
                                nc.scalar.activation(f2(xc_hi[:, b]), bank[b][:, 0:D], ACT.Copy).then_inc(xchi_done, 1)
                            if st == 2:
                                act.wait_ge(rl_done, ready(c.t))
                                nc.scalar.activation(logits[:, bass.ds(c.t, 1), :].rearrange("p o e -> p (o e)"),
                                                     bank[2 + b][:, 0:E], ACT.Copy).then_inc(rl_copied, 1)

                        pipeline(act, NT, 2, body)
                        act.wait_ge(c_shift, 1)
                        nc.scalar.activation(r["score"][:], r["sel"][:], ACT.Exp).then_inc(c_exp, 1)
                        act.wait_ge(v_in, 32)
                        nc.scalar.activation(above[:], V_f[:, 0, :], ACT.Abs, accum_out=asum[:, 0:1])
                        nc.scalar.activation(below[:], V_f[:, 1, :], ACT.Abs, accum_out=asum[:, 1:2]).then_inc(abs_done, 1)
                        act.wait_ge(w_in, 16 * 7)
                        nc.scalar.activation(cIsq[:], cI[:], ACT.Square)
                        nc.scalar.activation(Wsq[:], Wc_f[:], ACT.Square).then_inc(sq_done, 1)
                        act.wait_ge(sum_done, 1)
                        for s, sign in ((0, 1.0), (1, -1.0)):
                            nc.scalar.activation(limit[:, s, :], bank[6][:, 0:2], ACT.Copy,
                                                 scale=sign * 0.5 / (D * DF), bias=sign * 0.5e-5).then_inc(limit_done, 1)
                        nc.scalar.activation(WT_hi[:], Wc_f[:], ACT.Copy).then_inc(wt_hi, 1)
                        act.wait_ge(eps_done, 1)
                        nc.scalar.activation(nrm[:], nrm[:], ACT.Sqrt).then_inc(root_done, 1)

                    @block.vector
                    def _(dve):
                        dve.sem_inc(co_done, 2)
                        dve.sem_inc(xclo_done, 2)
                        dve.wait_ge(wr_split, 1)
                        TT(f2(Wr_lo[:]), f2(Wr_f[:]), f2(Wr_hi[:]), ALU.subtract).then_inc(wr_split, 1)

                        def body(st, c):
                            b = c.slot % 2
                            if st == 0:
                                dve.wait_ge(part_sum, c.t + 1)
                                dve.wait_ge(c_out[c.slot], c.turn * 16)
                                dve.wait_ge(co_posed, c.t + (-1)) if not isinstance(c.t, int) or c.t >= 4 else None
                                STT(co[:, c.slot, :], y1[:, c.slot, :], gates[0][:, 1, bass.ds(c.t, 1)],
                                    part[:, b, :], ALU.mult, ALU.add).then_inc(co_done, 1)
                            if st == 1:
                                dve.wait_ge(xchi_done, c.t + 1)
                                TT(f2(xc_lo[:, b]), bank[b][:, 0:D], f2(xc_hi[:, b]), ALU.subtract).then_inc(xclo_done, 1)

                        pipeline(dve, NT, 1, body)
                        dve.wait_ge(rl_copied, 2 + NT)
                        link(TT(r["sel"][:], logits[:],
                                router_bias[:, 1, :].unsqueeze(1).to_broadcast([P, NT, E]), ALU.add))
                        link(nc.vector.reduce_max(r["m"][:], r["sel"][:], AX.X))
                        TT(r["sel"][:], r["sel"][:], bc_e(r["m"][:]), ALU.subtract).then_inc(c_shift, 1)
                        dve.wait_ge(c_exp, 1)
                        link(nc.vector.reduce_sum(r["den"][:], r["score"][:], AX.X))
                        link(nc.vector.reciprocal(r["den"][:], r["den"][:]))
                        link(TT(r["score"][:], r["score"][:], bc_e(r["den"][:]), ALU.mult))
                        link(VCOPY(r["sel"][:], r["score"][:]))
                        select_top2(r, 1)
                        VCOPY(gates[1][:], r["val"][:])
                        assign_slots(dve, r, 1, bank[4][:, 0:NT * E], bank[5][:, 0:NT * E])
                        dve.wait_ge(ss_done, 1)
                        TS(nrm[:], bank[3][0:BATCH, 0:D], D * 1e-8, None, ALU.add).then_inc(eps_done, 1)
                        invert_vector(dve, r)
                        finish_slots(dve, r, bank[7])
                        dve.wait_ge(root_done, 1)
                        nc.vector.reciprocal(nrm[:], nrm[:]).then_inc(nrm_done, 1)
                        dve.wait_ge(wt_hi, 1)
                        TT(WT_lo[:], Wc_f[:], WT_hi[:], ALU.subtract)

            experts(1, cond_d, z_d, W1f_hi, W1f_lo, W2f_hi, W2f_lo, HF, b1_all, b2_all)

            e_scope, esb = scope()
            with e_scope:
                z0, z1, xr = (esb(n, [P, UNROLL, D], F) for n in ("z0", "z1", "xres"))
                part = esb("part1", [P, 2, D], F)
                x1 = esb("x1", [P, 2, D], F)
                x1b = esb("x1b", [P, 2, GT, D], F)
                xm = esb("xm", [P, 2, 2, P], F)
                xm_hi, xm_lo = esb("xm_hi", [P, 2, 2, P], H), esb("xm_lo", [P, 2, 2, P], H)
                zf = esb("zf", [P, 2, KC, P], F)
                zT_hi, zT_lo = esb("zT_hi", [P, 2, KC, 512], H), esb("zT_lo", [P, 2, KC, 512], H)
                norm = esb("norm", [P, 2, KC, 512], F)
                hf = esb("hf", [P, 2, 512], F)
                u_hi, u_lo = esb("u_hi", [P, FC, 512], H), esb("u_lo", [P, FC, 512], H)
                ob = esb("ob", [P, GT, D], F)
                z_in = sems("z_in", UNROLL)
                n_in = sems("n_in", 2)
                o_out = sems("o_out", GT)
                (e_part, e_sum, e_x1, e_x1b, e_xm, e_xmhi, e_xmlo, e_mm, e_zf, e_zhi, e_zlo,
                 e_up, e_relu, e_uhi, e_ulo, e_down, e_o) = map(sem, (
                     "e_part", "e_sum", "e_x1", "e_x1b", "e_xm", "e_xmhi", "e_xmlo", "e_mm", "e_zf",
                     "e_zhi", "e_zlo", "e_up", "e_relu", "e_uhi", "e_ulo", "e_down", "e_o"))
                f2 = lambda ap: ap.rearrange("p k n -> p (k n)")

                def halves(up, mix, down, eng):
                    for u in range(GT):
                        mix(Tile(0, 0, 0), u)
                    with eng.Fori(0, NG // 2 - 1) as i:
                        for k in range(2):
                            old, new = Tile(i * 2 + k, k, i), Tile(i * 2 + (k + 1), (k + 1) % 2, i + (k + 1) // 2)
                            up(old)
                            for u in range(GT):
                                mix(new, u)
                            down(old)
                    up(Tile(NG - 2, 0, NG // 2 - 1))
                    for u in range(GT):
                        mix(Tile(NG - 1, 1, NG // 2 - 1), u)
                    down(Tile(NG - 2, 0, NG // 2 - 1))
                    up(Tile(NG - 1, 1, NG // 2 - 1))
                    down(Tile(NG - 1, 1, NG // 2 - 1))

                nothing = lambda *a: None

                with nc.Block() as block:
                    @block.sync
                    def _(sp):
                        def mix(g, u):
                            t = g.t * GT + u
                            if u == 0:
                                sp.wait_ge(e_zf, (g.t - 1) * GT + 2) if not isinstance(g.t, int) or g.t > 1 else None
                                for half in range(2):
                                    sp.dma_start(norm[half * SEQ:(half + 1) * SEQ, g.slot, :, :],
                                                 norm_d[half * KC:(half + 1) * KC].rearrange("k b t -> k (b t)")[:, bass.ds(g.t * 512, 512)]
                                                 .partition_broadcast(SEQ)).then_inc(n_in[g.slot], 16)
                            sp.wait_ge(e_x1, t + (-1)) if not isinstance(t, int) or t >= 4 else None
                            for d, s in ((z0, z_d[bass.ds(t * P, P), :]), (z1, z_d[bass.ds(t * P + N, P), :]),
                                         (xr, x[bass.ds(t * P, P), :])):
                                sp.dma_start(d[:, u, :], s).then_inc(z_in[u], 16)

                        def down(g):
                            for u in range(GT):
                                sp.wait_ge(e_o, ready(g.t * GT + u))
                                sp.dma_start(out[bass.ds((g.t * GT + u) * P, P), :], ob[:, u, :]).then_inc(o_out[u], 16)

                        halves(nothing, mix, down, sp)
                        for u in range(GT):
                            sp.wait_ge(o_out[u], 16 * NG)

                    @block.gpsimd
                    def _(pool):
                        pool.sem_inc(e_x1b, 2)

                        def mix(g, u):
                            t = g.t * GT + u
                            b = u % 2
                            pool.wait_ge(e_part, ready(t))
                            nc.gpsimd.tensor_tensor(part[:, b, :], part[:, b, :], xr[:, u, :], ALU.add).then_inc(e_sum, 1)
                            pool.wait_ge(e_x1, ready(t))
                            if u == 0 and (not isinstance(g.t, int) or g.t > 1):
                                pool.wait_ge(e_o, (g.t - 1) * GT + 2)
                            nc.gpsimd.tensor_tensor(x1b[:, g.slot, u, :], x1[:, b, :], c2_sb[:], ALU.add).then_inc(e_x1b, 1)

                        halves(nothing, mix, nothing, pool)

                    @block.tensor
                    def _(pe):
                        def up(g):
                            pe.wait_ge(e_zlo, (g.t + 1) * GT)
                            for fc in range(FC):
                                n = g.t * FC + fc
                                pe.wait_ge(e_uhi, free(n))
                                o = bank[fc % 2][:, :]
                                for kc in range(KC):
                                    w = V1_q[:, kc, fc * P:(fc + 1) * P]
                                    MM(o, w, zT_hi[:, g.slot, kc, :], start=(kc == 0), stop=False)
                                    last = MM(o, w, zT_lo[:, g.slot, kc, :], start=False, stop=(kc == KC - 1))
                                last.then_inc(e_up, 1)

                        def mix(g, u):
                            t = g.t * GT + u
                            b = u % 2
                            pe.wait_ge(e_xmlo, t + 1)
                            pe.wait_ge(e_zf, free(t))
                            for bb in range(2):
                                rows = slice(bb * SEQ, (bb + 1) * SEQ)
                                for h in range(2):
                                    o = bank[2 + b][h * SEQ:(h + 1) * SEQ, bb * P:(bb + 1) * P]
                                    cols = slice(h * P, (h + 1) * P)
                                    for ql in range(2):
                                        MM(o, xm_hi[:, b, ql, rows], WT_hi[:, ql, cols], start=(ql == 0), stop=False)
                                        MM(o, xm_hi[:, b, ql, rows], WT_lo[:, ql, cols], start=False, stop=False)
                                        last = MM(o, xm_lo[:, b, ql, rows], WT_hi[:, ql, cols], start=False, stop=(ql == 1))
                            last.then_inc(e_mm, 1)

                        def down(g):
                            pe.wait_ge(e_ulo, g.t * FC + (FC + 2))
                            for u in range(GT):
                                pe.wait_ge(e_o, free(g.t * GT + u))
                                o = bank[4 + u % 2][:, 0:D]
                                tok = slice(u * P, (u + 1) * P)
                                for fc in range(FC):
                                    MM(o, u_hi[:, fc, tok], V2_q[:, fc, :], start=(fc == 0), stop=False)
                                    last = MM(o, u_lo[:, fc, tok], V2_q[:, fc, :], start=False, stop=(fc == FC - 1))
                                last.then_inc(e_down, 1)

                        halves(up, mix, down, pe)

                    @block.scalar
                    def _(act):
                        act.sem_inc(e_part, 2)
                        act.sem_inc(e_uhi, 2)
                        act.sem_inc(e_mm, 2)
                        act.sem_inc(e_zhi, 2)

                        def up(g):
                            for fc in range(FC):
                                n = g.t * FC + fc
                                act.wait_ge(e_up, n + 1)
                                act.wait_ge(e_ulo, free(n) )
                                if fc == 0 and (not isinstance(g.t, int) or g.t > 0):
                                    act.wait_ge(e_down, g.t * GT)
                                nc.scalar.activation(hf[:, fc % 2, :], bank[fc % 2][:, :], ACT.Relu,
                                                     bias=c1_sb[:, fc:fc + 1]).then_inc(e_relu, 1)
                                nc.scalar.activation(u_hi[:, fc, :], bank[fc % 2][:, :], ACT.Relu,
                                                     bias=c1_sb[:, fc:fc + 1]).then_inc(e_uhi, 1)

                        def mix(g, u):
                            t = g.t * GT + u
                            b = u % 2
                            act.wait_ge(z_in[u], (g.t + 1) * 48)
                            act.wait_ge(e_x1, free(t))
                            nc.scalar.activation(part[:, b, :], z0[:, u, :], ACT.Copy,
                                                 scale=gates[1][:, 0, bass.ds(t, 1)]).then_inc(e_part, 1)
                            act.wait_ge(e_xm, t + 1)
                            act.wait_ge(e_mm, free(t))
                            nc.scalar.activation(f2(xm_hi[:, b]), f2(xm[:, b]), ACT.Copy).then_inc(e_xmhi, 1)
                            act.wait_ge(e_zf, ready(t))
                            if u == 0 and (not isinstance(g.t, int) or g.t > 1):
                                act.wait_ge(e_up, (g.t - 1) * FC)
                            nc.scalar.activation(zT_hi[:, g.slot, :, u * P:(u + 1) * P], zf[:, b], ACT.Copy).then_inc(e_zhi, 1)

                        halves(up, mix, nothing, act)

                    @block.vector
                    def _(dve):
                        dve.sem_inc(e_x1, 2)
                        dve.sem_inc(e_zf, 2)
                        dve.sem_inc(e_ulo, 2)
                        dve.sem_inc(e_o, 2)

                        def up(g):
                            for fc in range(FC):
                                dve.wait_ge(e_uhi, ready(g.t * FC + fc))
                                TT(u_lo[:, fc, :], hf[:, fc % 2, :], u_hi[:, fc, :], ALU.subtract).then_inc(e_ulo, 1)

                        def mix(g, u):
                            t = g.t * GT + u
                            b = u % 2
                            dve.wait_ge(e_sum, t + 1)
                            dve.wait_ge(e_x1b, free(t))
                            STT(x1[:, b, :], z1[:, u, :], gates[1][:, 1, bass.ds(t, 1)], part[:, b, :],
                                ALU.mult, ALU.add).then_inc(e_x1, 1)
                            dve.wait_ge(e_x1, ready(t))
                            for bb in range(2):
                                for qh in range(2):
                                    rows = slice(bb * SEQ, (bb + 1) * SEQ)
                                    last = TT(
                                        xm[qh * SEQ:(qh + 1) * SEQ, b, :, rows],
                                        x1[rows, b, qh * P:(qh + 1) * P].rearrange("p (q l) -> p q l", q=2),
                                        modul[rows, bass.ds(t, 1), qh * 2:qh * 2 + 2].rearrange("p o q -> p (o q)")
                                        .unsqueeze(2).to_broadcast([SEQ, 2, SEQ]), ALU.mult)
                            last.then_inc(e_xm, 1)
                            dve.wait_ge(e_xmhi, t + 1)
                            TT(f2(xm_lo[:, b]), f2(xm[:, b]), f2(xm_hi[:, b]), ALU.subtract).then_inc(e_xmlo, 1)
                            dve.wait_ge(e_mm, ready(t))
                            dve.wait_ge(e_zhi, free(t))
                            if u == 0:
                                dve.wait_ge(n_in[g.slot], (g.turn + 1) * 32)
                            TT(zf[:, b].rearrange("p k (b t) -> p k b t", b=2),
                               bank[2 + b][:, 0:D].rearrange("p (b k t) -> p k b t", b=2, k=2),
                               norm[:, g.slot, :, u * P:(u + 1) * P].rearrange("p k (b t) -> p k b t", b=2),
                               ALU.mult).then_inc(e_zf, 1)
                            dve.wait_ge(e_zhi, ready(t))
                            TT(zT_lo[:, g.slot, :, u * P:(u + 1) * P], zf[:, b],
                               zT_hi[:, g.slot, :, u * P:(u + 1) * P], ALU.subtract).then_inc(e_zlo, 1)

                        def down(g):
                            for u in range(GT):
                                n = g.t * GT + u
                                dve.wait_ge(e_down, n + 1)
                                dve.wait_ge(e_x1b, ready(n))
                                dve.wait_ge(o_out[u], g.t * 16)
                                TT(ob[:, u, :], bank[4 + u % 2][:, 0:D], x1b[:, g.slot, u, :], ALU.add).then_inc(e_o, 1)

                        halves(up, mix, down, dve)


def constants():
    import numpy as np

    f = np.zeros((P, C_END), np.float32)
    p = np.arange(P)
    f[:, C_IDENT:C_IDENT + P] = np.eye(P)
    f[:, C_REV:C_REV + E] = E - np.arange(E)
    f[:, C_VALUE:C_VALUE + NT] = (np.arange(NT) % HALF) * P + p[:, None] + 1
    f[:, C_TILE:C_TILE + SLOT_TILES] = np.arange(SLOT_TILES) * P
    f[:, C_PAD:C_PAD + SLOT_TILES] = 2 * N + 1 + np.arange(SLOT_TILES) * P + p[:, None]
    for b in range(BATCH):
        f[b, C_SEL:C_SEL + P] = (p // SEQ) == b % 2
        f[b, C_OWN + b // 2] = 1
    h = np.zeros((P, H_END), np.float16)
    h[:, H_LTRI:H_LTRI + P] = p[:, None] < p[None, :]
    h[:, H_ONES:H_ONES + P] = 1
    h[:, H_IOTA:H_IOTA + P] = p
    h[:, H_TILE:H_TILE + SLOT_TILES] = np.arange(SLOT_TILES)
    return f, h


def kernel(x, cond_1024, L0_cond_router_W, L0_cond_router_bias, L0_cond_w1, L0_cond_w3, L0_cond_w2,
           L0_cond_W1e, L0_cond_W2e, L0_ffn_Wr, L0_ffn_br, L0_ffn_W1, L0_ffn_b1, L0_ffn_W2, L0_ffn_b2,
           L1_cond_weight, L1_ffn_W1, L1_ffn_b1, L1_ffn_W2, L1_ffn_b2):
    import numpy as np
    import concourse.bacc as bacc
    from concourse.bass_utils import run_bass_kernel_spmd

    def on_partitions(w):
        w = np.asarray(w)
        return w.reshape(w.shape[0] // P, P, w.shape[1]).transpose(1, 0, 2)

    def experts_on_partitions(w):
        w = np.asarray(w)
        e, k, n = w.shape
        return w.reshape(e, k // P, P, n).transpose(2, 0, 1, 3).reshape(P, e, -1)

    flat = lambda a: a.reshape(P, -1)
    xf = np.asarray(x).reshape(N, D)
    cond = np.asarray(cond_1024)
    rW = np.asarray(L0_cond_router_W)
    Wc = np.asarray(L1_cond_weight).reshape(SEQ, 2, 2, SEQ, 2, 2)
    WcT = Wc.transpose(4, 3, 5, 2, 1, 0).reshape(P, 2, D)
    condTI = cond.reshape(BATCH, SEQ, 2, 2).transpose(2, 1, 3, 0).reshape(P, 2, BATCH)
    constf, consth = constants()
    arrays = {
        "x": xf,
        "xT": xf.T.reshape(KC, P, NG, 512).transpose(1, 2, 0, 3),
        "cond": on_partitions(cond.T),
        "condTI": condTI,
        "modulation": cond.reshape(NT, P, 4).transpose(1, 0, 2),
        "rW": on_partitions(rW[:D]),
        "rWc": on_partitions(rW[D:]),
        "Wr": on_partitions(L0_ffn_Wr),
        "rb": np.asarray(L0_cond_router_bias),
        "br": np.asarray(L0_ffn_br),
        "w13": flat(np.concatenate([on_partitions(L0_cond_w1), on_partitions(L0_cond_w3)], axis=2)),
        "w2": flat(on_partitions(L0_cond_w2)),
        "wexp": np.concatenate([experts_on_partitions(w) for w in (
            L0_cond_W1e, L0_cond_W2e, L0_ffn_W1, L0_ffn_W2)], axis=2),
        "b1f": np.asarray(L0_ffn_b1),
        "b2f": np.asarray(L0_ffn_b2),
        "WcT": WcT,
        "V1": flat(on_partitions(np.asarray(L1_ffn_W1).T)),
        "c1": np.asarray(L1_ffn_b1).reshape(DF // P, P).T,
        "V2": flat(on_partitions(np.asarray(L1_ffn_W2).T)),
        "c2": np.asarray(L1_ffn_b2),
        "constf": constf,
        "consth": consth,
    }
    arrays = {k: np.ascontiguousarray(v) for k, v in arrays.items()}
    nc = bacc.Bacc("TRN2", target_bir_lowering=False, num_devices=1)
    args = [nc.dram_tensor(f"in_{k}", v.shape, mybir.dt.from_np(v.dtype), kind="ExternalInput").ap()
            for k, v in arrays.items()]
    out = nc.dram_tensor("out", (N, D), mybir.dt.float32, kind="ExternalOutput").ap()
    program(nc, *args, out)
    r = run_bass_kernel_spmd(nc, [{f"in_{k}": v for k, v in arrays.items()}], core_ids=[0])
    return r.results[0]["out"].reshape(BATCH, SEQ, D)
```

```python
import concourse.bass as bass
from concourse import mybir
from concourse.alu_op_type import AluOpType as ALU
from contextlib import ExitStack

P = 128
BATCH, SEQ, D = 64, 64, 256
N = BATCH * SEQ
NT = N // P
KC = D // P
E = 8
HS = 512
HE = 256
HF = 512
DF = 1024
SLOT_TILES = 2 * NT + E
GT = 4
NG = NT // GT
HALF = NT // 2
UNROLL = 4

C_IDENT, C_REV, C_VALUE, C_TILE, C_PAD, C_SEL, C_OWN = 0, 128, 136, 168, 240, 312, 440
C_END = C_OWN + NT
H_LTRI, H_ONES, H_IOTA, H_TILE = 0, 128, 256, 384
H_END = H_TILE + SLOT_TILES


class Tile:

    def __init__(self, t, slot, turn, place=None):
        self.t, self.slot, self.turn, self.place = t, slot, turn, place


def pipeline(eng, tiles, work, unroll=UNROLL):
    lag = max(stage for stage, _ in work)

    def step(s):
        for stage, emit in work:
            if 0 <= s - stage < tiles:
                emit(Tile(s - stage, (s - stage) % unroll, (s - stage) // unroll,
                          (s >= lag, s - stage)))

    for s in range(lag):
        step(s)
    loops = (tiles - lag) // unroll
    with eng.Fori(0, loops) as i:
        for k in range(unroll):
            for stage, emit in work:
                n = lag + k - stage
                emit(Tile(i * unroll + n, n % unroll, i + n // unroll, ("loop", n)))
    for s in range(lag + loops * unroll, tiles + lag):
        step(s)


def in_stages(lag, body):
    return [(stage, lambda c, stage=stage: body(stage, c)) for stage in range(lag + 1)]


def program(nc, x, xT, cond, condTI, modulation, rW, rWc, Wr, rb, br, w13, w2, wexp, b1f, b2f,
            WcT, V1, c1, V2, c2, constf, consth, out):
    F, H, I = mybir.dt.float32, mybir.dt.float16, mybir.dt.int32
    ACT, AX = mybir.ActivationFunctionType, mybir.AxisListType
    TT, TS = nc.vector.tensor_tensor, nc.vector.tensor_scalar
    STT, VCOPY = nc.vector.scalar_tensor_tensor, nc.vector.tensor_copy
    MM, TR = nc.tensor.matmul, nc.tensor.transpose

    def dram(name, shape):
        return nc.dram_tensor(name, shape, F).ap()

    shared_d = dram("shared_out", (N, D))
    cond_d = dram("cond_out", (N, D))
    y_d = dram("cond_slots_out", (2 * N + SLOT_TILES * P, D))
    z_d = dram("ffn_slots_out", (2 * N + SLOT_TILES * P, D))
    norm_d = dram("norms", (BATCH, D))

    root = ExitStack()
    with root:
        def scope():
            st = ExitStack()
            return st, lambda name, shape, dt: st.enter_context(nc.sbuf_tensor(name, shape, dt))

        def sem(name):
            return root.enter_context(nc.semaphore(name))

        def sems(name, n):
            return [sem(f"{name}{i}") for i in range(n)]

        sb = lambda name, shape, dt: root.enter_context(nc.sbuf_tensor(name, shape, dt))
        bank = [root.enter_context(nc.psum_tensor(f"bank{i}", [P, 512], F)) for i in range(8)]

        cf = sb("cf", [P, C_END], F)
        ch = sb("ch", [P, H_END], H)
        ident = cf[:, C_IDENT:C_IDENT + P]
        W1f_hi = sb("W1f_hi", [P, E, KC, HF], H)
        W1f_lo = sb("W1f_lo", [P, E, KC, HF], H)
        W2f_hi = sb("W2f_hi", [P, E, HF // P, D], H)
        W2f_lo = sb("W2f_lo", [P, E, HF // P, D], H)
        gates = [sb("gates_cond", [P, 2, NT], F), sb("gates_ffn", [P, 2, NT], F)]
        gather_idx = sb("gather_idx", [P, SLOT_TILES], I)
        scatter_idx = sb("scatter_idx", [P, SLOT_TILES], I)
        tile_expert = sb("tile_expert", [P, SLOT_TILES], I)
        logits = sb("logits", [P, NT, E], F)
        router_bias = sb("router_bias", [P, 2, E], F)
        ready = lambda t: t + 3
        free = lambda t: t + 1
        ready4 = lambda t: t + (1 + UNROLL)

        pool_passed, pe_passed = sem("pool_passed"), sem("pe_passed")

        chained = sem("vector_chain")
        chain_n = [0]

        def link(ins):
            chain_n[0] += 1
            ins.then_inc(chained, 1)
            nc.vector.wait_ge(chained, chain_n[0])

        def routing(lay, st_sb, names):
            r = {}
            f3 = lambda nm: st_sb(f"{nm}{lay}", [P, NT, E], F)
            r["score"], r["sel"], r["eq"], r["oh1"], r["oh2"], r["pos"] = map(
                f3, ("score", "sel", "eq", "oh1_", "oh2_", "pos"))
            r["m"] = st_sb(f"m{lay}", [P, NT], F)
            r["val"] = st_sb(f"val{lay}", [P, 2, NT], F)
            r["den"] = st_sb(f"den{lay}", [P, NT], F)
            r["choice"] = st_sb(f"choice{lay}", [P, NT, E], H)
            r["cum"] = st_sb(f"cum{lay}", [P, E, NT + 1], F)
            r["scan"] = st_sb(f"scan{lay}", [P, E, NT + 1], F)
            r["zero"] = st_sb(f"zero{lay}", [P, E * (NT + 1)], F)
            r["cnt"] = st_sb(f"cnt{lay}", [P, E], F)
            r["cnti"] = st_sb(f"cnti{lay}", [P, E], I)
            r["posi"] = st_sb(f"posi{lay}", [P, 2, 2 * NT], I)
            r["ab"] = st_sb(f"ab{lay}", [P, 2, 2 * NT], F)
            r["ohb"] = st_sb(f"ohb{lay}", [P, UNROLL, P], H)
            r["oha"] = st_sb(f"oha{lay}", [P, UNROLL, SLOT_TILES], H)
            r["inv"] = st_sb(f"inv{lay}", [P, 4, SLOT_TILES], F)
            r["iw"] = st_sb(f"iw{lay}", [P, 3, SLOT_TILES], F)
            r["ge"] = st_sb(f"ge{lay}", [P, SLOT_TILES, E], F)
            for nm in ("choice_ready", "counted", "onehot_ready", "onehot_used", "inverted"):
                r[nm] = sem(f"{nm}{lay}")
            return r

        def bc_e(ap):
            return ap.unsqueeze(2).to_broadcast([P, NT, E])

        def select_top2(r, lay):
            rev = cf[:, C_REV:C_REV + E].unsqueeze(1).to_broadcast([P, NT, E])
            for k, oh in ((0, r["oh1"]), (1, r["oh2"])):
                link(nc.vector.reduce_max(r["m"][:], r["sel"][:], AX.X))
                link(TT(r["eq"][:], r["sel"][:], bc_e(r["m"][:]), ALU.is_equal))
                link(TT(r["eq"][:], r["eq"][:], rev, ALU.mult))
                link(nc.vector.reduce_max(r["m"][:], r["eq"][:], AX.X))
                link(TT(oh[:], r["eq"][:], bc_e(r["m"][:]), ALU.is_equal))
                if k == 0:
                    link(STT(r["sel"][:], oh[:], -1e30, r["sel"][:], ALU.mult, ALU.add))
                link(TT(r["eq"][:], oh[:], r["score"][:], ALU.mult))
                link(nc.vector.reduce_sum(r["val"][:, k, :], r["eq"][:], AX.X))
            TT(r["choice"][:], r["oh1"][:], r["oh2"][:], ALU.add).then_inc(r["choice_ready"], 1)

        def assign_slots(dve, r, lay, prefix, totals):
            dve.wait_ge(r["counted"], 1)
            te = totals.rearrange("p (t e) -> p e t", e=E)
            link(nc.vector.memset(r["zero"][:], 0.0))
            link(VCOPY(r["cum"][:, :, 0:NT], te))
            link(nc.vector.reduce_sum(r["cnt"][:], r["cum"][:, :, 0:NT], AX.X))
            link(TS(r["cnti"][:], r["cnt"][:], float(P - 1), None, ALU.add))
            link(TS(r["cnti"][:], r["cnti"][:], 7, 7, ALU.logical_shift_right, ALU.logical_shift_left))
            link(TT(r["cum"][:, :, NT], r["cnti"][:], r["cnt"][:], ALU.subtract))
            flat = lambda a: a[:].rearrange("p e t -> p (e t)")
            link(nc.vector.tensor_tensor_scan(flat(r["scan"]), flat(r["cum"]), r["zero"][:], 0.0,
                                              ALU.add, ALU.add))
            ends = r["scan"][:, :, NT].unsqueeze(1).to_broadcast([P, SLOT_TILES, E])
            starts = cf[:, C_TILE:C_TILE + SLOT_TILES].unsqueeze(2).to_broadcast([P, SLOT_TILES, E])
            link(TT(r["ge"][:], ends, starts, ALU.is_le))
            link(nc.vector.reduce_sum(r["iw"][:, 0, :], r["ge"][:], AX.X))
            link(TS(tile_expert[:], r["iw"][:, 0, :], float(E - 1), None, ALU.min))
            link(TT(r["scan"][:], r["scan"][:], r["cum"][:], ALU.subtract))
            link(TT(r["pos"][:], prefix.rearrange("p (t e) -> p t e", e=E),
                    r["scan"][:, :, 0:NT].rearrange("p e t -> p t e"), ALU.add))
            for k, oh in ((0, r["oh1"]), (1, r["oh2"])):
                link(TT(r["eq"][:], oh[:], r["pos"][:], ALU.mult))
                link(nc.vector.reduce_sum(r["m"][:], r["eq"][:], AX.X))
                link(VCOPY(r["posi"][:, 1, k * NT:(k + 1) * NT], r["m"][:]))
            link(TS(r["posi"][:, 0, :], r["posi"][:, 1, :], 7, None, ALU.logical_shift_right))
            link(TS(r["posi"][:, 1, :], r["posi"][:, 1, :], P - 1, None, ALU.bitwise_and))
            link(VCOPY(r["ab"][:], r["posi"][:]))

        def invert_vector(dve, r):
            dve.sem_inc(r["onehot_used"], UNROLL)
            for k in range(2):
                for half in range(2):
                    base = k * NT + half * HALF
                    with dve.Fori(0, HALF // UNROLL) as i:
                        for u in range(UNROLL):
                            c = i * UNROLL + (base + u)
                            tok = i * UNROLL + (half * HALF + u)
                            dve.wait_ge(r["onehot_used"], c + 1)
                            TS(r["ohb"][:, u, :], ch[:, H_IOTA:H_IOTA + P],
                               r["ab"][:, 1, bass.ds(c, 1)], None, ALU.is_equal)
                            TS(r["oha"][:, u, :], ch[:, H_TILE:H_TILE + SLOT_TILES],
                               r["ab"][:, 0, bass.ds(c, 1)],
                               cf[:, bass.ds(tok + C_VALUE, 1)],
                               ALU.is_equal, ALU.mult).then_inc(r["onehot_ready"], 1)

        def invert_tensor(pe, r, inverse):
            for k in range(2):
                for half in range(2):
                    g = 2 * k + half
                    base = k * NT + half * HALF

                    def pair(c, u, first, last):
                        pe.wait_ge(r["onehot_ready"], c + 1)
                        MM(inverse[:, g * SLOT_TILES:(g + 1) * SLOT_TILES], r["ohb"][:, u, :],
                           r["oha"][:, u, :], start=first, stop=last).then_inc(r["onehot_used"], 1)

                    for u in range(UNROLL):
                        pair(base + u, u, u == 0, False)
                    with pe.Fori(1, HALF // UNROLL - 1) as i:
                        for u in range(UNROLL):
                            pair(i * UNROLL + (base + u), u, False, False)
                    for u in range(UNROLL):
                        pair(base + HALF - UNROLL + u, u, False, u == UNROLL - 1)

        def count_choices(pe, r, prefix, totals):
            pe.wait_ge(r["choice_ready"], 1)
            rhs = r["choice"][:].rearrange("p t e -> p (t e)")
            MM(prefix, ch[:, H_LTRI:H_LTRI + P], rhs, start=True, stop=True)
            MM(totals, ch[:, H_ONES:H_ONES + P], rhs, start=True, stop=True).then_inc(r["counted"], 1)

        def finish_slots(dve, r, inverse):
            dve.wait_ge(r["onehot_used"], UNROLL + 2 * NT)
            inv, iw = r["inv"], r["iw"]
            link(VCOPY(inv[:].rearrange("p g s -> p (g s)"), inverse[:, 0:4 * SLOT_TILES]))
            link(TT(iw[:, 0, :], inv[:, 1, :], inv[:, 3, :], ALU.add))
            link(TT(iw[:, 1, :], inv[:, 2, :], inv[:, 3, :], ALU.add))
            link(TT(inv[:, 0, :], inv[:, 0, :], inv[:, 2, :], ALU.add))
            link(TT(inv[:, 0, :], inv[:, 0, :], iw[:, 0, :], ALU.add))
            link(TS(iw[:, 0, :], iw[:, 0, :], 0.0, float(HALF * P), ALU.is_gt, ALU.mult))
            link(TT(inv[:, 0, :], inv[:, 0, :], iw[:, 0, :], ALU.add))
            link(TS(gather_idx[:], inv[:, 0, :], -1.0, 0.0, ALU.add, ALU.max))
            link(TS(iw[:, 1, :], iw[:, 1, :], 0.0, float(N), ALU.is_gt, ALU.mult))
            link(TS(iw[:, 2, :], inv[:, 0, :], 0.0, None, ALU.is_equal))
            link(TT(iw[:, 2, :], iw[:, 2, :], cf[:, C_PAD:C_PAD + SLOT_TILES], ALU.mult))
            link(TT(iw[:, 1, :], iw[:, 1, :], iw[:, 2, :], ALU.add))
            link(TT(iw[:, 1, :], iw[:, 1, :], inv[:, 0, :], ALU.add))
            link(TS(scatter_idx[:], iw[:, 1, :], -1.0, None, ALU.add))

        def experts(lay, src, dst, up_hi, up_lo, down_hi, down_lo, hidden, b1_all, b2_all):
            HC = hidden // P
            ffn = b1_all is not None
            nm = "ffn_" if ffn else "cond_"
            S = lambda n: sem(nm + n)
            x_in, y_out = sems(nm + "x_in", UNROLL), sems(nm + "y_out", UNROLL)
            gidx_ready, sidx_ready = S("gidx_ready"), S("sidx_ready")
            x_posed, xhi_done, xlo_done, up_done = S("x_posed"), S("xhi_done"), S("xlo_done"), S("up_done")
            act_done, h_posed, hhi_done, hlo_done = S("act_done"), S("h_posed"), S("hhi_done"), S("hlo_done")
            down_done, y_done = S("down_done"), S("y_done")
            gathered, scattered = S("gathered"), S("scattered")
            st, psb = scope()
            with st:
                xg = psb(nm + "xg", [P, UNROLL, D], F)
                gi = psb(nm + "gi", [P, UNROLL, 1], I)
                si = psb(nm + "si", [P, UNROLL, 1], I)
                xb_hi = psb(nm + "xb_hi", [P, 2, KC, P], H)
                xb_lo = psb(nm + "xb_lo", [P, 2, KC, P], H)
                hs = psb(nm + "hs", [P, 2, hidden], F)
                hb_hi = psb(nm + "hb_hi", [P, 2, HC, P], H)
                hb_lo = psb(nm + "hb_lo", [P, 2, HC, P], H)
                yo = psb(nm + "yo", [P, UNROLL, D], F)
                xT_ps = [bank[0][:, 0:D], bank[1][:, 0:D]]
                up_ps = [bank[2][:, 0:hidden], bank[3][:, 0:hidden]]
                hT_ps = [bank[4][:, 0:hidden], bank[5][:, 0:hidden]]
                y_ps = [bank[6][:, 0:D], bank[7][:, 0:D]]
                flat = lambda a, b: a[:, b].rearrange("p c n -> p (c n)")


                with nc.Block() as block:
                    @block.gpsimd
                    def _(pool):
                        def gather(c):
                            pool.wait_ge(gidx_ready, c.t + 1)
                            pool.wait_ge(x_posed, c.t + 1)
                            pool.sem_inc(pool_passed, 1)
                            pool.indirect_dma_start(
                                out=xg[:, c.slot, :], out_offset=None, in_=src,
                                in_offset=bass.IndirectOffsetOnAxis(ap=gi[:, c.slot, :], axis=0),
                            ).then_inc(x_in[c.slot], 16)

                        def scatter(c):
                            pool.wait_ge(sidx_ready, c.t + 1)
                            pool.wait_ge(y_done, ready(c.t))
                            pool.sem_inc(pool_passed, 1)
                            pool.indirect_dma_start(
                                out=dst, out_offset=bass.IndirectOffsetOnAxis(ap=si[:, c.slot, :], axis=0),
                                in_=yo[:, c.slot, :], in_offset=None).then_inc(y_out[c.slot], 16)

                        pool.sem_inc(x_posed, UNROLL)
                        pipeline(pool, SLOT_TILES, [(0, gather), (8, scatter)])
                        for u in range(UNROLL):
                            pool.wait_ge(y_out[u], 16 * (SLOT_TILES // UNROLL))

                    @block.sync
                    def _(sp):
                        def gather_end(c):
                            sp.wait_ge(x_in[c.slot], (c.turn + 1) * 16)
                            sp.sem_inc(gathered, 1)

                        def scatter_end(c):
                            sp.wait_ge(y_out[c.slot], (c.turn + 1) * 16)
                            sp.sem_inc(scattered, 1)

                        sp.sem_inc(gathered, UNROLL)
                        sp.sem_inc(scattered, UNROLL)
                        pipeline(sp, SLOT_TILES, [(0, gather_end), (8, scatter_end)])

                    @block.tensor
                    def _(pe):
                        loaded = {}

                        def expert_of(c):
                            if c.place not in loaded:
                                loaded[c.place] = pe.value_load(tile_expert[0:1, bass.ds(c.t, 1)],
                                                                min_val=0, max_val=E - 1)
                            return loaded[c.place]

                        def pose_x(c):
                            b = c.slot % 2
                            pe.wait_ge(gathered, ready4(c.t))
                            for kc in range(KC):
                                last = TR(xT_ps[b][:, kc * P:(kc + 1) * P],
                                          xg[:, c.slot, kc * P:(kc + 1) * P], ident)
                            last.then_inc(x_posed, 1)

                        def up(c):
                            b = c.slot % 2
                            e = expert_of(c)
                            pe.wait_ge(xlo_done, ready(c.t))
                            for kc in range(KC):
                                wh = up_hi[:, bass.ds(e, 1), kc, :].rearrange("p o n -> p (o n)")
                                wl = up_lo[:, bass.ds(e, 1), kc, :].rearrange("p o n -> p (o n)")
                                MM(up_ps[b], xb_hi[:, b, kc, :], wh, start=(kc == 0), stop=False)
                                MM(up_ps[b], xb_lo[:, b, kc, :], wh, start=False, stop=False)
                                last = MM(up_ps[b], xb_hi[:, b, kc, :], wl, start=False, stop=(kc == KC - 1))
                            last.then_inc(up_done, 1)

                        def pose_h(c):
                            b = c.slot % 2
                            pe.wait_ge(act_done, ready(c.t))
                            for hc in range(HC):
                                last = TR(hT_ps[b][:, hc * P:(hc + 1) * P],
                                          hs[:, b, hc * P:(hc + 1) * P], ident)
                            last.then_inc(h_posed, 1)

                        def down(c):
                            b = c.slot % 2
                            e = expert_of(c)
                            pe.wait_ge(hlo_done, ready(c.t))
                            pe.wait_ge(y_done, free(c.t))
                            for hc in range(HC):
                                wh = down_hi[:, bass.ds(e, 1), hc, :].rearrange("p o n -> p (o n)")
                                wl = down_lo[:, bass.ds(e, 1), hc, :].rearrange("p o n -> p (o n)")
                                MM(y_ps[b], hb_hi[:, b, hc, :], wh, start=(hc == 0), stop=False)
                                MM(y_ps[b], hb_lo[:, b, hc, :], wh, start=False, stop=False)
                                last = MM(y_ps[b], hb_hi[:, b, hc, :], wl, start=False, stop=(hc == HC - 1))
                            last.then_inc(down_done, 1)

                        pipeline(pe, SLOT_TILES, [(3, pose_x), (4, up), (5, pose_h), (6, down)])

                    @block.scalar
                    def _(act):
                        def x_high(c):
                            b = c.slot % 2
                            act.wait_ge(x_posed, c.t + 1 + UNROLL)
                            act.wait_ge(up_done, free(c.t))
                            nc.scalar.activation(flat(xb_hi, b), xT_ps[b], ACT.Copy).then_inc(xhi_done, 1)

                        def gelu(c):
                            b = c.slot % 2
                            act.wait_ge(up_done, ready(c.t))
                            act.wait_ge(h_posed, free(c.t))
                            nc.scalar.activation(hs[:, b, :], up_ps[b], ACT.Gelu).then_inc(act_done, 1)

                        def h_high(c):
                            b = c.slot % 2
                            act.wait_ge(h_posed, ready(c.t))
                            act.wait_ge(down_done, free(c.t))
                            nc.scalar.activation(flat(hb_hi, b), hT_ps[b],
                                                 ACT.Relu if ffn else ACT.Copy).then_inc(hhi_done, 1)

                        for s in (up_done, h_posed, down_done):
                            act.sem_inc(s, 2)
                        pipeline(act, SLOT_TILES, [(3, x_high)] + ([] if ffn else [(4, gelu)]) + [(5, h_high)])

                    @block.vector
                    def _(dve):
                        def expert_of(t):
                            return dve.value_load(tile_expert[0:1, bass.ds(t, 1)], min_val=0, max_val=E - 1)

                        def gather_index(c):
                            dve.wait_ge(gathered, free(c.t))
                            VCOPY(gi[:, c.slot, :], gather_idx[:, bass.ds(c.t, 1)]).then_inc(gidx_ready, 1)

                        def scatter_index(c):
                            dve.wait_ge(scattered, free(c.t))
                            VCOPY(si[:, c.slot, :], scatter_idx[:, bass.ds(c.t, 1)]).then_inc(sidx_ready, 1)

                        def x_low(c):
                            b = c.slot % 2
                            dve.wait_ge(xhi_done, c.t + 1)
                            TT(flat(xb_lo, b), xT_ps[b], flat(xb_hi, b), ALU.subtract).then_inc(xlo_done, 1)

                        def bias(c):
                            b = c.slot % 2
                            e = expert_of(c.t)
                            dve.wait_ge(up_done, ready(c.t))
                            dve.wait_ge(h_posed, free(c.t))
                            TT(hs[:, b, :], up_ps[b],
                               b1_all[:, bass.ds(e, 1), :].rearrange("p o n -> p (o n)"),
                               ALU.add).then_inc(act_done, 1)

                        def h_low(c):
                            b = c.slot % 2
                            dve.wait_ge(hhi_done, c.t + 1)
                            if ffn:
                                i = STT(flat(hb_lo, b), hT_ps[b], 0.0, flat(hb_hi, b), ALU.max, ALU.subtract)
                            else:
                                i = TT(flat(hb_lo, b), hT_ps[b], flat(hb_hi, b), ALU.subtract)
                            i.then_inc(hlo_done, 1)

                        def result(c):
                            b = c.slot % 2
                            if ffn:
                                e = expert_of(c.t)
                            dve.wait_ge(down_done, ready(c.t))
                            if ffn:
                                i = TT(yo[:, c.slot, :], y_ps[b],
                                       b2_all[:, bass.ds(e, 1), :].rearrange("p o n -> p (o n)"), ALU.add)
                            else:
                                i = VCOPY(yo[:, c.slot, :], y_ps[b])
                            i.then_inc(y_done, 1)

                        for s in (xlo_done, act_done, hlo_done, y_done):
                            dve.sem_inc(s, 2)
                        pipeline(dve, SLOT_TILES, [(0, gather_index), (3, x_low)] + ([(4, bias)] if ffn else []) +
                                 [(5, h_low), (7, scatter_index), (7, result)])

        cond_scope, csb = scope()
        with cond_scope:
            W1e_hi, W1e_lo = csb("W1e_hi", [P, E, KC, HE], H), csb("W1e_lo", [P, E, KC, HE], H)
            W2e_hi, W2e_lo = csb("W2e_hi", [P, E, HE // P, D], H), csb("W2e_lo", [P, E, HE // P, D], H)
            parts = []
            at = 0
            for hi, lo, n in ((W1e_hi, W1e_lo, KC * HE), (W2e_hi, W2e_lo, HE // P * D),
                              (W1f_hi, W1f_lo, KC * HF), (W2f_hi, W2f_lo, HF // P * D)):
                parts.append((hi, lo, at, at + n))
                at += n
            WEXP = at
            SC = HS // P

            a_scope, asb = scope()
            with a_scope:
                xT_hi, xT_lo = asb("xT_hi", [P, NG, KC, 512], H), asb("xT_lo", [P, NG, KC, 512], H)
                w13_hi, w13_lo = asb("w13_hi", [P, KC, 2 * HS], H), asb("w13_lo", [P, KC, 2 * HS], H)
                w2_hi, w2_lo = asb("w2_hi", [P, SC, D], H), asb("w2_lo", [P, SC, D], H)
                stage = asb("stage", [P, WEXP], F)
                rW_f, rW_hi, rW_lo = (asb("rW_f", [P, KC, E], F), asb("rW_hi", [P, KC, E], H),
                                      asb("rW_lo", [P, KC, E], H))
                rWc_sb = asb("rWc_sb", [P, KC, E], F)
                condT = asb("condT", [P, KC, BATCH], F)
                cond_logit = asb("cond_logit", [BATCH, NT, E], F)
                logT = asb("logT", [E, 2, 512], F)
                h_hi, h_lo = asb("h_hi", [P, 2, SC, 512], H), asb("h_lo", [P, 2, SC, 512], H)
                work = asb("work", [P, 4, 512], F)
                xstage = work[:].rearrange("p (b k) n -> p b k n", b=2)
                silu, prod = work[:, 0:2, :], work[:, 2:4, :]
                ys = asb("ys", [P, GT, D], F)
                r = routing(0, asb, None)

                consts_in, rw_in, shared_w_in = sem("consts_in"), sem("rw_in"), sem("shared_w_in")
                xT_in = sems("xT_in", 2)
                rw_split, x_hi_done, x_lo_done = sem("rw_split"), sem("x_hi_done"), sem("x_lo_done")
                logT_done, logT_copied, log_posed, log_copied = map(
                    sem, ("logT_done", "logT_copied", "log_posed", "log_copied"))
                cl_done, cl_spread, cl_added = sem("cl_done"), sem("cl_spread"), sem("cl_added")
                z_ready, s_ready = sem("z_ready"), sem("s_ready")
                shw_hi, shw_lo = sem("shw_hi"), sem("shw_lo")
                exp_in, exp_hi, exp_lo = sem("exp_in"), sem("exp_hi"), sem("exp_lo")
                sh_up, sh_silu, sh_prod, sh_hi, sh_lo = map(
                    sem, ("sh_up", "sh_silu", "sh_prod", "sh_hi", "sh_lo"))
                sh_down, sh_y = sem("sh_down"), sem("sh_y")
                sh_out = sems("sh_out", GT)
                SHW = 2 * KC * HS + SC * D
                f2 = lambda ap: ap.rearrange("p k n -> p (k n)")

                with nc.Block() as block:
                    @block.sync
                    def _(sp):
                        sp.dma_start(cf[:], constf).then_inc(consts_in, 16)
                        sp.dma_start(ch[:], consth).then_inc(consts_in, 16)
                        sp.dma_start(router_bias[:, 0, :], rb.partition_broadcast(P)).then_inc(consts_in, 16)
                        sp.dma_start(router_bias[:, 1, :], br.partition_broadcast(P)).then_inc(consts_in, 16)
                        sp.dma_start(rW_f[:], rW).then_inc(rw_in, 16)
                        sp.dma_start(rWc_sb[:], rWc).then_inc(rw_in, 16)
                        sp.dma_start(condT[:], cond).then_inc(rw_in, 16)
                        for g in range(2):
                            sp.dma_start(xstage[:, g], xT[:, g]).then_inc(xT_in[g], 16)
                        sp.dma_start(stage[:, 0:2 * KC * HS], w13).then_inc(shared_w_in, 16)
                        sp.dma_start(stage[:, 2 * KC * HS:SHW], w2).then_inc(shared_w_in, 16)
                        with sp.Fori(1, NG // 2) as i:
                            for b in range(2):
                                sp.wait_ge(x_lo_done, i * 2 + (b - 1))
                                sp.dma_start(xstage[:, b], xT[:, bass.ds(i * 2 + b, 1)].rearrange(
                                    "p o k n -> p (o k) n")).then_inc(xT_in[b], 16)
                        sp.wait_ge(shw_lo, 1)
                        sp.dma_start(stage[:], wexp[:, 0]).then_inc(exp_in, 16)

                        def body(st, c):
                            if st == 1:
                                for u in range(GT):
                                    sp.wait_ge(sh_y, ready(c.t * GT + u))
                                    sp.dma_start(shared_d[bass.ds(c.t * (GT * P) + u * P, P), :],
                                                 ys[:, u, :]).then_inc(sh_out[u], 16)
                            if st == 0 and not (isinstance(c.t, int) and c.t == 0):
                                sp.wait_ge(exp_lo, c.t)
                                sp.dma_start(stage[:], wexp[:, bass.ds(c.t, 1)].rearrange(
                                    "p o n -> p (o n)")).then_inc(exp_in, 16)

                        pipeline(sp, NG, in_stages(1, body), unroll=2)
                        for u in range(GT):
                            sp.wait_ge(sh_out[u], 16 * NG)

                    @block.tensor
                    def _(pe):
                        pe.wait_ge(rw_in, 48)
                        for kc in range(KC):
                            last = MM(bank[4][0:BATCH, 0:E], condT[:, kc, :], rWc_sb[:, kc, :],
                                      start=(kc == 0), stop=(kc == KC - 1))
                        last.then_inc(cl_done, 1)
                        pe.wait_ge(cl_spread, 1)
                        MM(bank[3][:, 0:NT * E], cf[0:BATCH, C_SEL:C_SEL + P],
                           cond_logit[:].rearrange("b t e -> b (t e)"), start=True, stop=True).then_inc(cl_added, 1)
                        pe.wait_ge(rw_split, 2)

                        def body(st, c):
                            b = c.slot % 2
                            if st == 0:
                                pe.wait_ge(x_lo_done, c.t + 1)
                                pe.wait_ge(logT_copied, free(c.t))
                                for kc in range(KC):
                                    xh = xT_hi[:, bass.ds(c.t, 1), kc, :].rearrange("p o n -> p (o n)")
                                    xl = xT_lo[:, bass.ds(c.t, 1), kc, :].rearrange("p o n -> p (o n)")
                                    o = bank[5 + b][0:E, :]
                                    MM(o, rW_hi[:, kc, :], xh, start=(kc == 0), stop=False)
                                    MM(o, rW_lo[:, kc, :], xh, start=False, stop=False)
                                    last = MM(o, rW_hi[:, kc, :], xl, start=False, stop=(kc == KC - 1))
                                last.then_inc(logT_done, 1)
                            if st == 1:
                                pe.wait_ge(logT_copied, ready(c.t))
                                pe.wait_ge(log_copied, free(c.t))
                                pe.sem_inc(pe_passed, 1)
                                for u in range(GT):
                                    last = TR(bank[1 + b][:, u * E:(u + 1) * E], logT[:, b, u * P:(u + 1) * P],
                                              cf[0:E, C_IDENT:C_IDENT + E])
                                last.then_inc(log_posed, 1)

                        pipeline(pe, NG, in_stages(1, body), unroll=2)
                        count_choices(pe, r, bank[0][:, 0:NT * E], bank[1][:, 0:NT * E])
                        invert_tensor(pe, r, bank[7])

                        pe.wait_ge(shw_lo, 1)

                        def shared(st, c):
                            b = c.slot % 2
                            if st == 0:
                                for j in range(SC):
                                    n = c.t * SC + j
                                    pe.wait_ge(sh_prod, free(n))
                                    for m in range(2):
                                        o = bank[2 * (j % 2) + m][:, :]
                                        cols = slice(m * HS + j * P, m * HS + (j + 1) * P)
                                        for kc in range(KC):
                                            xh = xT_hi[:, bass.ds(c.t, 1), kc, :].rearrange("p o n -> p (o n)")
                                            xl = xT_lo[:, bass.ds(c.t, 1), kc, :].rearrange("p o n -> p (o n)")
                                            MM(o, w13_hi[:, kc, cols], xh, start=(kc == 0), stop=False)
                                            MM(o, w13_hi[:, kc, cols], xl, start=False, stop=False)
                                            last = MM(o, w13_lo[:, kc, cols], xh, start=False, stop=(kc == KC - 1))
                                    last.then_inc(sh_up, 1)
                            else:
                                pe.wait_ge(sh_lo, (c.t + 1) * SC)
                                for u in range(GT):
                                    pe.wait_ge(sh_y, free(c.t * GT + u))
                                    o = bank[4 + u % 2][:, 0:D]
                                    for hc in range(SC):
                                        tok = slice(u * P, (u + 1) * P)
                                        MM(o, h_hi[:, b, hc, tok], w2_hi[:, hc, :], start=(hc == 0), stop=False)
                                        MM(o, h_hi[:, b, hc, tok], w2_lo[:, hc, :], start=False, stop=False)
                                        last = MM(o, h_lo[:, b, hc, tok], w2_hi[:, hc, :], start=False, stop=(hc == SC - 1))
                                    last.then_inc(sh_down, 1)

                        pipeline(pe, NG, in_stages(1, shared), unroll=2)

                    @block.scalar
                    def _(act):
                        act.sem_inc(logT_copied, 2)
                        act.sem_inc(log_copied, 2)
                        act.sem_inc(log_posed, 2)
                        act.sem_inc(sh_y, 2)
                        act.sem_inc(sh_down, 2 * GT)
                        act.wait_ge(rw_in, 48)
                        nc.scalar.activation(f2(rW_hi[:]), f2(rW_f[:]), ACT.Copy).then_inc(rw_split, 1)

                        def body(st, c):
                            b = c.slot % 2
                            if st == 0:
                                act.wait_ge(xT_in[b], (c.turn + 1) * 16)
                                nc.scalar.activation(
                                    xT_hi[:, bass.ds(c.t, 1), :, :].rearrange("p o k n -> p (o k n)"),
                                    f2(xstage[:, b]), ACT.Copy).then_inc(x_hi_done, 1)
                            if st == 1:
                                act.wait_ge(logT_done, c.t + 1)
                                act.wait_ge(log_posed, free(c.t))
                                nc.scalar.activation(logT[:, b, :], bank[5 + b][0:E, :], ACT.Copy).then_inc(logT_copied, 1)
                            if st == 2:
                                act.wait_ge(log_posed, ready(c.t))
                                nc.scalar.activation(
                                    logits[:, bass.ds(c.t * GT, GT), :].rearrange("p t e -> p (t e)"),
                                    bank[1 + b][:, 0:GT * E], ACT.Copy).then_inc(log_copied, 1)

                        pipeline(act, NG, in_stages(2, body), unroll=2)
                        act.wait_ge(z_ready, 1)
                        nc.scalar.activation(r["score"][:], r["sel"][:], ACT.Sigmoid).then_inc(s_ready, 1)
                        act.wait_ge(shared_w_in, 32)
                        nc.scalar.activation(f2(w13_hi[:]), stage[:, 0:2 * KC * HS], ACT.Copy)
                        nc.scalar.activation(f2(w2_hi[:]), stage[:, 2 * KC * HS:SHW], ACT.Copy).then_inc(shw_hi, 1)

                        def shared(st, c):
                            b = c.slot % 2
                            if st == 0:
                                for j in range(SC):
                                    n = c.t * SC + j
                                    act.wait_ge(sh_up, n + 1)
                                    act.wait_ge(sh_prod, free(n))
                                    nc.scalar.activation(silu[:, j % 2, :], bank[2 * (j % 2)][:, :],
                                                         ACT.Silu).then_inc(sh_silu, 1)
                                act.wait_ge(exp_in, (c.t + 1) * 16)
                                for hi, lo, a, z in parts:
                                    last = nc.scalar.activation(
                                        hi[:, bass.ds(c.t, 1), :, :].rearrange("p o k n -> p (o k n)"),
                                        stage[:, a:z], ACT.Copy)
                                last.then_inc(exp_hi, 1)
                            else:
                                for u in range(GT):
                                    n = c.t * GT + u
                                    act.wait_ge(sh_down, n + (1 + 2 * GT))
                                    act.wait_ge(sh_out[u], c.t * 16)
                                    nc.scalar.activation(ys[:, u, :], bank[4 + u % 2][:, 0:D], ACT.Copy,
                                                         scale=1.0 / 3.0).then_inc(sh_y, 1)

                        pipeline(act, NG, in_stages(1, shared), unroll=2)

                    @block.vector
                    def _(dve):
                        dve.sem_inc(sh_prod, 2)
                        dve.wait_ge(rw_split, 1)
                        TT(f2(rW_lo[:]), f2(rW_f[:]), f2(rW_hi[:]), ALU.subtract).then_inc(rw_split, 1)
                        dve.wait_ge(consts_in, 64)
                        dve.wait_ge(cl_done, 1)
                        TT(cond_logit[:], bank[4][0:BATCH, 0:E].unsqueeze(1).to_broadcast([BATCH, NT, E]),
                           cf[0:BATCH, C_OWN:C_OWN + NT].unsqueeze(2).to_broadcast([BATCH, NT, E]),
                           ALU.mult).then_inc(cl_spread, 1)

                        def body(st, c):
                            b = c.slot % 2
                            dve.wait_ge(x_hi_done, c.t + 1)
                            TT(xT_lo[:, bass.ds(c.t, 1), :, :].rearrange("p o k n -> p (o k n)"),
                               f2(xstage[:, b]),
                               xT_hi[:, bass.ds(c.t, 1), :, :].rearrange("p o k n -> p (o k n)"),
                               ALU.subtract).then_inc(x_lo_done, 1)

                        pipeline(dve, NG, in_stages(0, body), unroll=2)
                        dve.wait_ge(log_copied, 2 + NG)
                        dve.wait_ge(cl_added, 1)
                        TT(r["sel"][:], logits[:], bank[3][:, 0:NT * E].rearrange("p (t e) -> p t e", e=E),
                           ALU.add).then_inc(z_ready, 1)
                        dve.wait_ge(s_ready, 1)
                        link(TT(r["sel"][:], r["score"][:],
                                router_bias[:, 0, :].unsqueeze(1).to_broadcast([P, NT, E]), ALU.add))
                        select_top2(r, 0)
                        g0 = gates[0]
                        link(TT(r["den"][:], r["val"][:, 0, :], r["val"][:, 1, :], ALU.add))
                        link(TS(r["m"][:], r["den"][:], 1e-9, None, ALU.is_gt))
                        link(TS(r["den"][:], r["den"][:], 1e-9, None, ALU.add))
                        link(nc.vector.reciprocal(r["den"][:], r["den"][:]))
                        for k in range(2):
                            link(TT(g0[:, k, :], r["val"][:, k, :], r["den"][:], ALU.mult))
                            link(TS(g0[:, k, :], g0[:, k, :], -0.5, None, ALU.add))
                            link(TT(g0[:, k, :], g0[:, k, :], r["m"][:], ALU.mult))
                            link(TS(g0[:, k, :], g0[:, k, :], 0.5, 1.0 / 3.0, ALU.add, ALU.mult))
                        assign_slots(dve, r, 0, bank[0][:, 0:NT * E], bank[1][:, 0:NT * E])
                        invert_vector(dve, r)
                        finish_slots(dve, r, bank[7])
                        dve.wait_ge(shw_hi, 1)
                        TT(f2(w13_lo[:]), stage[:, 0:2 * KC * HS], f2(w13_hi[:]), ALU.subtract)
                        TT(f2(w2_lo[:]), stage[:, 2 * KC * HS:SHW], f2(w2_hi[:]), ALU.subtract).then_inc(shw_lo, 1)

                        def shared(st, c):
                            b = c.slot % 2
                            for j in range(SC):
                                n = c.t * SC + j
                                dve.wait_ge(sh_silu, n + 1)
                                TT(prod[:, j % 2, :], silu[:, j % 2, :], bank[2 * (j % 2) + 1][:, :],
                                   ALU.mult).then_inc(sh_prod, 1)
                                dve.wait_ge(sh_prod, ready(n))
                                if j == 0:
                                    dve.wait_ge(sh_down, c.t * GT + GT)
                                VCOPY(h_hi[:, b, j, :], prod[:, j % 2, :]).then_inc(sh_hi, 1)
                                dve.wait_ge(sh_hi, n + 1)
                                TT(h_lo[:, b, j, :], prod[:, j % 2, :], h_hi[:, b, j, :], ALU.subtract).then_inc(sh_lo, 1)
                            dve.wait_ge(exp_hi, c.t + 1)
                            for hi, lo, a, z in parts:
                                last = TT(lo[:, bass.ds(c.t, 1), :, :].rearrange("p o k n -> p (o k n)"),
                                          stage[:, a:z],
                                          hi[:, bass.ds(c.t, 1), :, :].rearrange("p o k n -> p (o k n)"),
                                          ALU.subtract)
                            last.then_inc(exp_lo, 1)

                        pipeline(dve, NG, in_stages(0, shared), unroll=2)

            experts(0, x, y_d, W1e_hi, W1e_lo, W2e_hi, W2e_lo, HE, None, None)

        late_scope, lsb = scope()
        with late_scope:
            b1_all, b2_all = lsb("b1_all", [P, E, HF], F), lsb("b2_all", [P, E, D], F)
            WT_hi, WT_lo = lsb("WT_hi", [P, 2, D], H), lsb("WT_lo", [P, 2, D], H)
            FC = DF // P
            V1_q, V2_q = lsb("V1_q", [P, KC, DF], H), lsb("V2_q", [P, FC, D], H)
            c1_sb, c2_sb = lsb("c1_sb", [P, FC], F), lsb("c2_sb", [P, D], F)
            modul = lsb("modul", [P, NT, 4], F)

            c_scope, csb2 = scope()
            with c_scope:
                r = routing(1, csb2, None)
                y, sh = csb2("y", [P, UNROLL, 2, D], F), csb2("sh", [P, UNROLL, D], F)
                part, co = csb2("part", [P, UNROLL, D], F), csb2("co", [P, UNROLL, D], F)
                xc_hi, xc_lo = (csb2(n, [P, UNROLL, KC, P], H) for n in ("xc_hi", "xc_lo"))
                y_rows = y_d[0:2 * N].rearrange("(k n) d -> n k d", k=2)
                Wr_f, Wr_hi, Wr_lo = (csb2("Wr_f", [P, KC, E], F), csb2("Wr_hi", [P, KC, E], H),
                                      csb2("Wr_lo", [P, KC, E], H))
                V_f = csb2("V_f", [P, 2, KC * DF], F)
                above = csb2("above", [P, KC * DF], H)
                below = csb2("below", [P, KC * DF], H)
                asum, limit = csb2("asum", [P, 2], F), csb2("limit", [P, 2, 2], F)
                Wc_f = csb2("Wc_f", [P, 2, D], F)
                Wsq = csb2("Wsq", [P, 2, D], F)
                cI, cIsq = csb2("cI", [P, 2, BATCH], F), csb2("cIsq", [P, 2, BATCH], F)
                nrm = csb2("nrm", [BATCH, D], F)
                onesf = csb2("onesf", [P, P], F)
                y_in = sems("cy_in", UNROLL)
                c_out = sems("c_out", UNROLL)
                (wr_in, wr_split, w_in, v_in, part_done, part_sum, co_done, co_posed, xchi_done, xclo_done,
                 rl_done, rl_copied, c_shift, c_exp) = map(sem, (
                     "wr_in", "wr_split", "w_in", "v_in", "part_done", "part_sum", "co_done", "co_posed",
                     "xchi_done", "xclo_done", "rl_done", "rl_copied", "c_shift", "c_exp"))
                (abs_done, ones_done, sum_done, limit_done, above_done, below_done, quant_done, sq_done,
                 ss_done, eps_done, root_done, nrm_done, wt_hi, nrm_out) = map(sem, (
                     "abs_done", "ones_done", "sum_done", "limit_done", "above_done", "below_done",
                     "quant_done", "sq_done", "ss_done", "eps_done", "root_done", "nrm_done", "wt_hi",
                     "nrm_out"))
                f2 = lambda ap: ap.rearrange("p k n -> p (k n)")

                with nc.Block() as block:
                    @block.sync
                    def _(sp):
                        sp.dma_start(Wr_f[:], Wr).then_inc(wr_in, 16)

                        def load(c):
                            sp.wait_ge(co_done, free(c.t))
                            sp.dma_start(y[:, c.slot], y_rows[bass.ds(c.t * P, P)]).then_inc(y_in[c.slot], 16)
                            sp.dma_start(sh[:, c.slot, :], shared_d[bass.ds(c.t * P, P), :]).then_inc(y_in[c.slot], 16)

                        def store(c):
                            sp.wait_ge(co_done, ready4(c.t))
                            sp.dma_start(cond_d[bass.ds(c.t * P, P), :], co[:, c.slot, :]).then_inc(c_out[c.slot], 16)

                        pipeline(sp, NT, [(0, load), (4, store)])
                        for t, s in ((b1_all[:], b1f.partition_broadcast(P)), (b2_all[:], b2f.partition_broadcast(P)),
                                     (c1_sb[:], c1), (c2_sb[:], c2.partition_broadcast(P)),
                                     (modul[:], modulation), (cI[:], condTI), (Wc_f[:], WcT)):
                            sp.dma_start(t, s).then_inc(w_in, 16)
                        sp.dma_start(V_f[:, 0, :], V1).then_inc(v_in, 16)
                        sp.dma_start(V_f[:, 1, :], V2).then_inc(v_in, 16)
                        for u in range(UNROLL):
                            sp.wait_ge(c_out[u], 16 * (NT // UNROLL + 1))
                        sp.wait_ge(w_in, 16 * 7)
                        sp.wait_ge(nrm_done, 1)
                        sp.dma_start(norm_d, nrm[:]).then_inc(nrm_out, 16)
                        sp.wait_ge(nrm_out, 16)

                    @block.gpsimd
                    def _(pool):
                        nc.gpsimd.memset(onesf[:], 1.0).then_inc(ones_done, 1)

                        def add_shared(c):
                            pool.wait_ge(part_done, ready4(c.t))
                            nc.gpsimd.tensor_tensor(part[:, c.slot, :], part[:, c.slot, :], sh[:, c.slot, :],
                                                    ALU.add).then_inc(part_sum, 1)

                        pipeline(pool, NT, [(0, add_shared)])
                        pool.wait_ge(limit_done, 2)
                        for m, q in ((0, f2(V1_q[:])), (1, f2(V2_q[:]))):
                            if m:
                                pool.wait_ge(quant_done, 1)
                            nc.gpsimd.tensor_scalar(above[:], V_f[:, m, :], limit[:, 0, m:m + 1], None,
                                                    ALU.is_gt).then_inc(above_done, 1)
                            nc.gpsimd.tensor_scalar(below[:], V_f[:, m, :], limit[:, 1, m:m + 1], None,
                                                    ALU.is_lt).then_inc(above_done, 1)
                            pool.wait_ge(above_done, 2 * (m + 1))
                            nc.gpsimd.tensor_tensor(q, above[:], below[:], ALU.subtract).then_inc(quant_done, 1)

                    @block.tensor
                    def _(pe):
                        pe.wait_ge(wr_split, 2)

                        def pose(c):
                            pe.wait_ge(co_done, ready4(c.t))
                            pe.wait_ge(xclo_done, free(c.t))
                            for kc in range(KC):
                                last = TR(bank[c.slot][:, kc * P:(kc + 1) * P],
                                          co[:, c.slot, kc * P:(kc + 1) * P], ident)
                            last.then_inc(co_posed, 1)

                        def router(c):
                            pe.wait_ge(xclo_done, ready4(c.t))
                            pe.wait_ge(rl_copied, free(c.t))
                            o = bank[4 + c.slot][:, 0:E]
                            for kc in range(KC):
                                MM(o, xc_hi[:, c.slot, kc, :], Wr_hi[:, kc, :], start=(kc == 0), stop=False)
                                MM(o, xc_hi[:, c.slot, kc, :], Wr_lo[:, kc, :], start=False, stop=False)
                                last = MM(o, xc_lo[:, c.slot, kc, :], Wr_hi[:, kc, :], start=False, stop=(kc == KC - 1))
                            last.then_inc(rl_done, 1)

                        pipeline(pe, NT, [(0, pose), (4, router)])
                        count_choices(pe, r, bank[4][:, 0:NT * E], bank[5][:, 0:NT * E])
                        pe.wait_ge(ones_done, 1)
                        pe.wait_ge(abs_done, 1)
                        MM(bank[6][:, 0:2], onesf[:], asum[:], start=True, stop=True).then_inc(sum_done, 1)
                        pe.wait_ge(sq_done, 1)
                        for ql in range(2):
                            last = MM(bank[3][0:BATCH, 0:D], cIsq[:, ql, :], Wsq[:, ql, :], start=(ql == 0), stop=(ql == 1))
                        last.then_inc(ss_done, 1)
                        invert_tensor(pe, r, bank[7])

                    @block.scalar
                    def _(act):
                        for m in (part_done, rl_copied, co_posed, rl_done):
                            act.sem_inc(m, UNROLL)
                        act.wait_ge(wr_in, 16)
                        nc.scalar.activation(f2(Wr_hi[:]), f2(Wr_f[:]), ACT.Copy).then_inc(wr_split, 1)

                        def first_term(c):
                            act.wait_ge(y_in[c.slot], (c.turn + 1) * 32)
                            act.wait_ge(co_done, free(c.t))
                            nc.scalar.activation(part[:, c.slot, :], y[:, c.slot, 0, :], ACT.Copy,
                                                 scale=gates[0][:, 0, bass.ds(c.t, 1)]).then_inc(part_done, 1)

                        def high(c):
                            act.wait_ge(co_posed, ready4(c.t))
                            act.wait_ge(rl_done, free(c.t))
                            nc.scalar.activation(f2(xc_hi[:, c.slot]), bank[c.slot][:, 0:D], ACT.Copy).then_inc(xchi_done, 1)

                        def take_logits(c):
                            act.wait_ge(rl_done, ready4(c.t))
                            nc.scalar.activation(logits[:, bass.ds(c.t, 1), :].rearrange("p o e -> p (o e)"),
                                                 bank[4 + c.slot][:, 0:E], ACT.Copy).then_inc(rl_copied, 1)

                        pipeline(act, NT, [(0, first_term), (2, high), (6, take_logits)])
                        act.wait_ge(c_shift, 1)
                        nc.scalar.activation(r["score"][:], r["sel"][:], ACT.Exp).then_inc(c_exp, 1)
                        act.wait_ge(v_in, 32)
                        nc.scalar.activation(above[:], V_f[:, 0, :], ACT.Abs, accum_out=asum[:, 0:1])
                        nc.scalar.activation(below[:], V_f[:, 1, :], ACT.Abs, accum_out=asum[:, 1:2]).then_inc(abs_done, 1)
                        act.wait_ge(w_in, 16 * 7)
                        nc.scalar.activation(cIsq[:], cI[:], ACT.Square)
                        nc.scalar.activation(Wsq[:], Wc_f[:], ACT.Square).then_inc(sq_done, 1)
                        act.wait_ge(sum_done, 1)
                        for s, sign in ((0, 1.0), (1, -1.0)):
                            nc.scalar.activation(limit[:, s, :], bank[6][:, 0:2], ACT.Copy,
                                                 scale=sign * 0.5 / (D * DF), bias=sign * 0.5e-5).then_inc(limit_done, 1)
                        nc.scalar.activation(WT_hi[:], Wc_f[:], ACT.Copy).then_inc(wt_hi, 1)
                        act.wait_ge(eps_done, 1)
                        nc.scalar.activation(nrm[:], nrm[:], ACT.Sqrt).then_inc(root_done, 1)

                    @block.vector
                    def _(dve):
                        for m in (co_done, xclo_done):
                            dve.sem_inc(m, UNROLL)
                        for u in range(UNROLL):
                            dve.sem_inc(c_out[u], 16)
                        dve.wait_ge(wr_split, 1)
                        TT(f2(Wr_lo[:]), f2(Wr_f[:]), f2(Wr_hi[:]), ALU.subtract).then_inc(wr_split, 1)

                        def combine(c):
                            dve.wait_ge(part_sum, c.t + 1)
                            dve.wait_ge(c_out[c.slot], (c.turn + 1) * 16)
                            dve.wait_ge(co_posed, free(c.t))
                            STT(co[:, c.slot, :], y[:, c.slot, 1, :], gates[0][:, 1, bass.ds(c.t, 1)],
                                part[:, c.slot, :], ALU.mult, ALU.add).then_inc(co_done, 1)

                        def low(c):
                            dve.wait_ge(xchi_done, c.t + 1)
                            TT(f2(xc_lo[:, c.slot]), bank[c.slot][:, 0:D], f2(xc_hi[:, c.slot]), ALU.subtract).then_inc(xclo_done, 1)

                        pipeline(dve, NT, [(0, combine), (3, low)])
                        dve.wait_ge(rl_copied, UNROLL + NT)
                        link(TT(r["sel"][:], logits[:],
                                router_bias[:, 1, :].unsqueeze(1).to_broadcast([P, NT, E]), ALU.add))
                        link(nc.vector.reduce_max(r["m"][:], r["sel"][:], AX.X))
                        TT(r["sel"][:], r["sel"][:], bc_e(r["m"][:]), ALU.subtract).then_inc(c_shift, 1)
                        dve.wait_ge(c_exp, 1)
                        link(nc.vector.reduce_sum(r["den"][:], r["score"][:], AX.X))
                        link(nc.vector.reciprocal(r["den"][:], r["den"][:]))
                        link(TT(r["score"][:], r["score"][:], bc_e(r["den"][:]), ALU.mult))
                        link(VCOPY(r["sel"][:], r["score"][:]))
                        select_top2(r, 1)
                        VCOPY(gates[1][:], r["val"][:])
                        assign_slots(dve, r, 1, bank[4][:, 0:NT * E], bank[5][:, 0:NT * E])
                        dve.wait_ge(ss_done, 1)
                        TS(nrm[:], bank[3][0:BATCH, 0:D], D * 1e-8, None, ALU.add).then_inc(eps_done, 1)
                        invert_vector(dve, r)
                        finish_slots(dve, r, bank[7])
                        dve.wait_ge(root_done, 1)
                        nc.vector.reciprocal(nrm[:], nrm[:]).then_inc(nrm_done, 1)
                        dve.wait_ge(wt_hi, 1)
                        TT(WT_lo[:], Wc_f[:], WT_hi[:], ALU.subtract)

            experts(1, cond_d, z_d, W1f_hi, W1f_lo, W2f_hi, W2f_lo, HF, b1_all, b2_all)

            e_scope, esb = scope()
            with e_scope:
                PAIR = 2 * P
                CH = FC // 2
                z0, z1, xr = (esb(n, [P, UNROLL, D], F) for n in ("z0", "z1", "xres"))
                norm = esb("norm", [P, UNROLL, D], F)
                part = esb("part1", [P, 2, D], F)
                x1 = esb("x1", [P, 2, D], F)
                x1b = esb("x1b", [P, NT, D], F)
                xm = esb("xm", [P, 2, 2, P], F)
                xm_hi, xm_lo = esb("xm_hi", [P, 2, 2, P], H), esb("xm_lo", [P, 2, 2, P], H)
                zf = esb("zf", [P, 2, KC, P], F)
                zT_hi, zT_lo = esb("zT_hi", [P, 2, KC, PAIR], H), esb("zT_lo", [P, 2, KC, PAIR], H)
                hf = esb("hf", [P, 2, CH, PAIR], F)
                u_hi, u_lo = esb("u_hi", [P, 2, FC, PAIR], H), esb("u_lo", [P, 2, FC, PAIR], H)
                ob = esb("ob", [P, UNROLL, D], F)
                z_in, o_out = sems("z_in", UNROLL), sems("o_out", UNROLL)
                (e_part, e_sum, e_x1, e_x1b, e_xm, e_xmhi, e_xmlo, e_mix, e_zf, e_zhi, e_zlo,
                 e_up, e_relu, e_uhi, e_ulo, e_down, e_o) = map(sem, (
                     "e_part", "e_sum", "e_x1", "e_x1b", "e_xm", "e_xmhi", "e_xmlo", "e_mix", "e_zf",
                     "e_zhi", "e_zlo", "e_up", "e_relu", "e_uhi", "e_ulo", "e_down", "e_o"))
                f2 = lambda ap: ap.rearrange("p k n -> p (k n)")
                mix_ps = [bank[2][:, 0:D], bank[3][:, 0:D]]
                up_ps = [bank[j][:, 0:PAIR] for j in (0, 1, 6, 7)]
                down_ps = [bank[4][:, 0:D], bank[5][:, 0:D]]

                with nc.Block() as block:
                    @block.sync
                    def _(sp):
                        def load(c):
                                if not isinstance(c.t, int) or c.t >= UNROLL:
                                    sp.wait_ge(e_x1, c.t + (-1))
                                    sp.wait_ge(e_zf, c.t + (-1))
                                for d, s in ((z0, z_d[bass.ds(c.t * P, P), :]), (z1, z_d[bass.ds(c.t * P + N, P), :]),
                                             (xr, x[bass.ds(c.t * P, P), :])):
                                    sp.dma_start(d[:, c.slot, :], s).then_inc(z_in[c.slot], 16)
                                for bb in range(2):
                                    sp.dma_start(norm[bb * SEQ:(bb + 1) * SEQ, c.slot, :],
                                                 norm_d[bass.ds(c.t * 2 + bb, 1), :].rearrange("o d -> (o d)")
                                                 .partition_broadcast(SEQ)).then_inc(z_in[c.slot], 16)
                        def store(c):
                                sp.wait_ge(e_o, ready(c.t))
                                sp.dma_start(out[bass.ds(c.t * P, P), :], ob[:, c.slot, :]).then_inc(o_out[c.slot], 16)

                        pipeline(sp, NT, [(0, load), (10, store)])
                        for u in range(UNROLL):
                            sp.wait_ge(o_out[u], 16 * (NT // UNROLL + 1))

                    @block.gpsimd
                    def _(pool):
                        def add_x(c):
                            b = c.slot % 2
                            pool.wait_ge(e_part, ready(c.t))
                            nc.gpsimd.tensor_tensor(part[:, b, :], part[:, b, :], xr[:, c.slot, :],
                                                    ALU.add).then_inc(e_sum, 1)

                        def add_c2(c):
                            b = c.slot % 2
                            pool.wait_ge(e_x1, ready(c.t))
                            nc.gpsimd.tensor_tensor(x1b[:, bass.ds(c.t, 1), :].rearrange("p o d -> p (o d)"),
                                                    x1[:, b, :], c2_sb[:], ALU.add).then_inc(e_x1b, 1)

                        def mod_lo(c):
                            b = c.slot % 2
                            pool.wait_ge(e_xmhi, c.t + 1)
                            pool.wait_ge(e_mix, free(c.t))
                            nc.gpsimd.tensor_tensor(f2(xm_lo[:, b]), f2(xm[:, b]), f2(xm_hi[:, b]),
                                                    ALU.subtract).then_inc(e_xmlo, 1)

                        pool.sem_inc(e_x1b, 2)
                        pool.sem_inc(e_xmlo, 2)
                        pipeline(pool, NT, [(2, mod_lo), (1, add_c2), (0, add_x)])

                    @block.tensor
                    def _(pe):
                        def mix(c):
                            b = c.slot % 2
                            pe.wait_ge(e_xmlo, ready(c.t))
                            pe.wait_ge(e_zf, free(c.t))
                            for ql in range(2):
                                MM(mix_ps[b], xm_hi[:, b, ql, :], WT_hi[:, ql, :], start=(ql == 0), stop=False)
                                MM(mix_ps[b], xm_hi[:, b, ql, :], WT_lo[:, ql, :], start=False, stop=False)
                                last = MM(mix_ps[b], xm_lo[:, b, ql, :], WT_hi[:, ql, :], start=False, stop=(ql == 1))
                            last.then_inc(e_mix, 1)

                        def up(c):
                            b = c.slot % 2
                            pr = c.slot // 2
                            pe.wait_ge(e_zlo, c.t + (2 - b))
                            for j in range(CH):
                                fc = CH * b + j
                                pe.wait_ge(e_relu, c.t * CH + (j + 1))
                                for kc in range(KC):
                                    w = V1_q[:, kc, fc * P:(fc + 1) * P]
                                    MM(up_ps[j], w, zT_hi[:, pr, kc, :], start=(kc == 0), stop=False)
                                    last = MM(up_ps[j], w, zT_lo[:, pr, kc, :], start=False, stop=(kc == KC - 1))
                                last.then_inc(e_up, 1)

                        def down(c):
                            b = c.slot % 2
                            pr = c.slot // 2
                            pe.wait_ge(e_ulo, c.t * 2 + (8 - 2 * b))
                            pe.wait_ge(e_o, free(c.t))
                            tok = slice(b * P, (b + 1) * P)
                            for fc in range(FC):
                                MM(down_ps[b], u_hi[:, pr, fc, tok], V2_q[:, fc, :], start=(fc == 0), stop=False)
                                last = MM(down_ps[b], u_lo[:, pr, fc, tok], V2_q[:, fc, :], start=False, stop=(fc == FC - 1))
                            last.then_inc(e_down, 1)

                        pipeline(pe, NT, [(5, up), (7, down), (2, mix)])

                    @block.scalar
                    def _(act):
                        for s, n in ((e_part, 2), (e_mix, 2), (e_zhi, 2), (e_relu, CH), (e_uhi, 2),
                                     (e_up, UNROLL * CH), (e_down, UNROLL)):
                            act.sem_inc(s, n)

                        def first_term(c):
                            b = c.slot % 2
                            act.wait_ge(z_in[c.slot], (c.turn + 1) * 80)
                            act.wait_ge(e_x1, free(c.t))
                            nc.scalar.activation(part[:, b, :], z0[:, c.slot, :], ACT.Copy,
                                                 scale=gates[1][:, 0, bass.ds(c.t, 1)]).then_inc(e_part, 1)

                        def mod_hi(c):
                            b = c.slot % 2
                            act.wait_ge(e_xm, c.t + 1)
                            act.wait_ge(e_mix, free(c.t))
                            nc.scalar.activation(f2(xm_hi[:, b]), f2(xm[:, b]), ACT.Copy).then_inc(e_xmhi, 1)

                        def mixed_hi(c):
                            b = c.slot % 2
                            pr = c.slot // 2
                            act.wait_ge(e_zf, ready(c.t))
                            if b == 0:
                                act.wait_ge(e_up, (c.t + 2) * CH)
                            nc.scalar.activation(zT_hi[:, pr, :, b * P:(b + 1) * P], zf[:, b], ACT.Copy).then_inc(e_zhi, 1)

                        def hidden(c):
                            b, pr = c.slot % 2, c.slot // 2

                            def split(j):
                                fc = CH * b + j
                                act.wait_ge(e_relu, c.t * CH + (j + 2 + CH))
                                if fc == 0:
                                    act.wait_ge(e_down, c.t + 2)
                                nc.scalar.activation(u_hi[:, pr, fc:fc + 2, :], hf[:, b, j:j + 2, :],
                                                     ACT.Copy).then_inc(e_uhi, 1)

                            for j in range(CH):
                                fc = CH * b + j
                                act.wait_ge(e_up, (c.t + UNROLL) * CH + (j + 1))
                                if j % 2 == 0:
                                    act.wait_ge(e_ulo, c.t * 2 + (j // 2 + 1))
                                nc.scalar.activation(hf[:, b, j, :], up_ps[j], ACT.Relu,
                                                     bias=c1_sb[:, fc:fc + 1]).then_inc(e_relu, 1)
                                if j % 2 == 0 and j > 0:
                                    split(j - 2)
                            split(CH - 2)

                        pipeline(act, NT, [(2, mod_hi), (0, first_term), (3, mixed_hi), (5, hidden)])

                    @block.vector
                    def _(dve):
                        for s in (e_x1, e_zf, e_ulo, e_ulo, e_o):
                            dve.sem_inc(s, 2)
                        for u in range(UNROLL):
                            dve.sem_inc(o_out[u], 16)

                        def x_one(c):
                            b = c.slot % 2
                            dve.wait_ge(e_sum, c.t + 1)
                            dve.wait_ge(e_x1b, free(c.t))
                            STT(x1[:, b, :], z1[:, c.slot, :], gates[1][:, 1, bass.ds(c.t, 1)], part[:, b, :],
                                ALU.mult, ALU.add).then_inc(e_x1, 1)

                        def modulate(c):
                            b = c.slot % 2
                            dve.wait_ge(e_x1, ready(c.t))
                            dve.wait_ge(e_xmlo, free(c.t))
                            for bb in range(2):
                                for qh in range(2):
                                    rows = slice(bb * SEQ, (bb + 1) * SEQ)
                                    last = TT(
                                        xm[qh * SEQ:(qh + 1) * SEQ, b, :, rows],
                                        x1[rows, b, qh * P:(qh + 1) * P].rearrange("p (q l) -> p q l", q=2),
                                        modul[rows, bass.ds(c.t, 1), qh * 2:qh * 2 + 2].rearrange("p o q -> p (o q)")
                                        .unsqueeze(2).to_broadcast([SEQ, 2, SEQ]), ALU.mult)
                            last.then_inc(e_xm, 1)

                        def normalise(c):
                            b = c.slot % 2
                            pr = c.slot // 2
                            dve.wait_ge(e_mix, ready(c.t))
                            dve.wait_ge(e_zhi, free(c.t))
                            for bb in range(2):
                                for h in range(2):
                                    rows, cols = slice(bb * SEQ, (bb + 1) * SEQ), slice(h * P, (h + 1) * P)
                                    last = TT(zf[h * SEQ:(h + 1) * SEQ, b, :, rows],
                                              mix_ps[b][rows, cols].rearrange("p (k t) -> p k t", k=KC),
                                              norm[rows, c.slot, cols].rearrange("p (k t) -> p k t", k=KC), ALU.mult)
                            last.then_inc(e_zf, 1)

                        def mixed_lo(c):
                            b, pr = c.slot % 2, c.slot // 2
                            dve.wait_ge(e_zhi, ready(c.t))
                            TT(zT_lo[:, pr, :, b * P:(b + 1) * P], zf[:, b],
                               zT_hi[:, pr, :, b * P:(b + 1) * P], ALU.subtract).then_inc(e_zlo, 1)

                        def hidden_lo(c):
                            b = c.slot % 2
                            pr = c.slot // 2
                            for j in range(0, CH, 2):
                                fc = CH * b + j
                                dve.wait_ge(e_uhi, c.t * 2 + (j // 2 + 3))
                                TT(u_lo[:, pr, fc:fc + 2, :], hf[:, b, j:j + 2, :], u_hi[:, pr, fc:fc + 2, :],
                                   ALU.subtract).then_inc(e_ulo, 1)

                        def total(c):
                            b = c.slot % 2
                            dve.wait_ge(e_down, c.t + (1 + UNROLL))
                            dve.wait_ge(o_out[c.slot], (c.turn + 1) * 16)
                            TT(ob[:, c.slot, :], down_ps[b], x1b[:, bass.ds(c.t, 1), :].rearrange("p o d -> p (o d)"),
                               ALU.add).then_inc(e_o, 1)

                        pipeline(dve, NT, [(3, normalise), (6, hidden_lo), (3, mixed_lo), (1, x_one), (8, total), (1, modulate)])


def constants():
    import numpy as np

    f = np.zeros((P, C_END), np.float32)
    p = np.arange(P)
    f[:, C_IDENT:C_IDENT + P] = np.eye(P)
    f[:, C_REV:C_REV + E] = E - np.arange(E)
    f[:, C_VALUE:C_VALUE + NT] = (np.arange(NT) % HALF) * P + p[:, None] + 1
    f[:, C_TILE:C_TILE + SLOT_TILES] = np.arange(SLOT_TILES) * P
    f[:, C_PAD:C_PAD + SLOT_TILES] = 2 * N + 1 + np.arange(SLOT_TILES) * P + p[:, None]
    for b in range(BATCH):
        f[b, C_SEL:C_SEL + P] = (p // SEQ) == b % 2
        f[b, C_OWN + b // 2] = 1
    h = np.zeros((P, H_END), np.float16)
    h[:, H_LTRI:H_LTRI + P] = p[:, None] < p[None, :]
    h[:, H_ONES:H_ONES + P] = 1
    h[:, H_IOTA:H_IOTA + P] = p
    h[:, H_TILE:H_TILE + SLOT_TILES] = np.arange(SLOT_TILES)
    return f, h


def kernel(x, cond_1024, L0_cond_router_W, L0_cond_router_bias, L0_cond_w1, L0_cond_w3, L0_cond_w2,
           L0_cond_W1e, L0_cond_W2e, L0_ffn_Wr, L0_ffn_br, L0_ffn_W1, L0_ffn_b1, L0_ffn_W2, L0_ffn_b2,
           L1_cond_weight, L1_ffn_W1, L1_ffn_b1, L1_ffn_W2, L1_ffn_b2):
    import numpy as np
    import concourse.bacc as bacc
    from concourse.bass_utils import run_bass_kernel_spmd

    def on_partitions(w):
        w = np.asarray(w)
        return w.reshape(w.shape[0] // P, P, w.shape[1]).transpose(1, 0, 2)

    def experts_on_partitions(w):
        w = np.asarray(w)
        e, k, n = w.shape
        return w.reshape(e, k // P, P, n).transpose(2, 0, 1, 3).reshape(P, e, -1)

    flat = lambda a: a.reshape(P, -1)
    xf = np.asarray(x).reshape(N, D)
    cond = np.asarray(cond_1024)
    rW = np.asarray(L0_cond_router_W)
    Wc = np.asarray(L1_cond_weight).reshape(SEQ, 2, 2, SEQ, 2, 2)
    WcT = Wc.transpose(4, 3, 5, 2, 1, 0).reshape(P, 2, D)
    condTI = cond.reshape(BATCH, SEQ, 2, 2).transpose(2, 1, 3, 0).reshape(P, 2, BATCH)
    constf, consth = constants()
    arrays = {
        "x": xf,
        "xT": xf.T.reshape(KC, P, NG, 512).transpose(1, 2, 0, 3),
        "cond": on_partitions(cond.T),
        "condTI": condTI,
        "modulation": cond.reshape(NT, P, 4).transpose(1, 0, 2),
        "rW": on_partitions(rW[:D]),
        "rWc": on_partitions(rW[D:]),
        "Wr": on_partitions(L0_ffn_Wr),
        "rb": np.asarray(L0_cond_router_bias),
        "br": np.asarray(L0_ffn_br),
        "w13": flat(np.concatenate([on_partitions(L0_cond_w1), on_partitions(L0_cond_w3)], axis=2)),
        "w2": flat(on_partitions(L0_cond_w2)),
        "wexp": np.concatenate([experts_on_partitions(w) for w in (
            L0_cond_W1e, L0_cond_W2e, L0_ffn_W1, L0_ffn_W2)], axis=2),
        "b1f": np.asarray(L0_ffn_b1),
        "b2f": np.asarray(L0_ffn_b2),
        "WcT": WcT,
        "V1": flat(on_partitions(np.asarray(L1_ffn_W1).T)),
        "c1": np.asarray(L1_ffn_b1).reshape(DF // P, P).T,
        "V2": flat(on_partitions(np.asarray(L1_ffn_W2).T)),
        "c2": np.asarray(L1_ffn_b2),
        "constf": constf,
        "consth": consth,
    }
    arrays = {k: np.ascontiguousarray(v) for k, v in arrays.items()}
    nc = bacc.Bacc("TRN2", target_bir_lowering=False, num_devices=1)
    args = [nc.dram_tensor(f"in_{k}", v.shape, mybir.dt.from_np(v.dtype), kind="ExternalInput").ap()
            for k, v in arrays.items()]
    out = nc.dram_tensor("out", (N, D), mybir.dt.float32, kind="ExternalOutput").ap()
    program(nc, *args, out)
    r = run_bass_kernel_spmd(nc, [{f"in_{k}": v for k, v in arrays.items()}], core_ids=[0])
    return r.results[0]["out"].reshape(BATCH, SEQ, D)
```

```python
import concourse.bass as bass
from concourse import mybir
from concourse.alu_op_type import AluOpType as ALU
from contextlib import ExitStack
import numpy

P = 128
BATCH, SEQ, D = 64, 64, 256
N = BATCH * SEQ
NT = N // P
KC = D // P
E = 8
HS = 512
HE = 256
HF = 512
DF = 1024
SLOT_TILES = 2 * NT + E
GT = 4
NG = NT // GT
HALF = NT // 2
UNROLL = 4

C_IDENT, C_REV, C_VALUE, C_TILE, C_PAD, C_SEL, C_OWN = 0, 128, 136, 168, 240, 312, 440
C_END = C_OWN + NT
H_LTRI, H_ONES, H_IOTA = 0, 128, 256
BATCH_COLS = 8
H_END = H_IOTA + P * BATCH_COLS


class Tile:

    def __init__(self, t, slot, turn, place=None):
        self.t, self.slot, self.turn, self.place = t, slot, turn, place


def pipeline(eng, tiles, work, unroll=UNROLL, slots=None, before_loop=None):
    lag = max(stage for stage, _ in work)
    slots = slots or unroll
    each = unroll // slots

    def step(s):
        for stage, emit in work:
            if 0 <= s - stage < tiles:
                emit(Tile(s - stage, (s - stage) % slots, (s - stage) // slots,
                          (s >= lag, s - stage)))

    for s in range(lag):
        step(s)
    if before_loop:
        before_loop()
    loops = (tiles - lag) // unroll
    with eng.Fori(0, loops) as i:
        for k in range(unroll):
            for stage, emit in work:
                n = lag + k - stage
                turn = i * each + n // slots if each > 1 else i + n // slots
                emit(Tile(i * unroll + n, n % slots, turn, ("loop", n)))
    for s in range(lag + loops * unroll, tiles + lag):
        step(s)


def in_stages(lag, body):
    return [(stage, lambda c, stage=stage: body(stage, c)) for stage in range(lag + 1)]


def program(nc, x, xT, cond, condTI, modulation, rW, rWc, Wr, rb, br, w13, w2, wexp, b1f, b2f,
            WcT, V1, c1, V2, c2, constf, consth, out):
    F, H, I = mybir.dt.float32, mybir.dt.float16, mybir.dt.int32
    ACT, AX = mybir.ActivationFunctionType, mybir.AxisListType
    TT, TS = nc.vector.tensor_tensor, nc.vector.tensor_scalar
    STT, VCOPY = nc.vector.scalar_tensor_tensor, nc.vector.tensor_copy
    MM, TR = nc.tensor.matmul, nc.tensor.transpose

    def dram(name, shape):
        return nc.dram_tensor(name, shape, F).ap()

    shared_d = dram("shared_out", (N, D))
    cond_d = dram("cond_out", (N, D))
    xs_d = dram("cond_slots_in", (SLOT_TILES * P, D))
    y_d = dram("cond_experts_out", (2 * N + SLOT_TILES * P, D))
    z_d = dram("ffn_experts_out", (2 * N + SLOT_TILES * P, D))
    norm_d = dram("norms", (BATCH, D))

    root = ExitStack()
    with root:
        def scope():
            st = ExitStack()
            return st, lambda name, shape, dt: st.enter_context(nc.sbuf_tensor(name, shape, dt))

        phase_sems = []

        def sem(name):
            phase_sems.append(nc.alloc_semaphore(name=name))
            return phase_sems[-1]

        def end_phase():
            nc.clear_and_free_semaphores(phase_sems)
            phase_sems.clear()
            nc.all_engine_barrier()

        def sems(name, n):
            return [sem(f"{name}{i}") for i in range(n)]

        def room(region):
            taken = [0]

            def take(name, shape, dt):
                words = int(numpy.prod(shape[1:])) * (1 if dt == H else 2)
                assert taken[0] + words <= region.shape[1]
                ap = region[:, taken[0]:taken[0] + words]
                taken[0] += words
                if dt != H:
                    ap = ap.bitcast(dt)
                return ap.rearrange("p (a b) -> p a b", a=shape[1])

            return take

        sb = lambda name, shape, dt: root.enter_context(nc.sbuf_tensor(name, shape, dt))
        bank = [root.enter_context(nc.psum_tensor(f"bank{i}", [P, 512], F)) for i in range(8)]

        cf = sb("cf", [P, C_END], F)
        ch = sb("ch", [P, H_END], H)
        ident = cf[:, C_IDENT:C_IDENT + P]
        W1f = sb("W1f", [P, 2, E, KC, HF], H)
        W1f_hi, W1f_lo = W1f[:, 0], W1f[:, 1]
        W2f_hi = sb("W2f_hi", [P, E, HF // P, D], H)
        W2f_lo = sb("W2f_lo", [P, E, HF // P, D], H)
        gates = [sb("gates_cond", [P, 2, NT], F), sb("gates_ffn", [P, 2, NT], F)]
        slot_of = sb("slot_of", [P, 2, NT], I)
        asum = sb("asum", [P, 2], F)
        gather_idx = sb("gather_idx", [P, SLOT_TILES], I)
        scatter_idx = sb("scatter_idx", [P, SLOT_TILES], I)
        tile_expert = sb("tile_expert", [P, SLOT_TILES], I)
        logits = sb("logits", [P, NT, E], F)
        router_bias = sb("router_bias", [P, 2, E], F)
        ready = lambda t: t + 3
        free = lambda t: t + 1
        ready4 = lambda t: t + (1 + UNROLL)

        pool_passed, pe_passed, chained = (root.enter_context(nc.semaphore(n)) for n in (
            "pool_passed", "pe_passed", "vector_chain"))

        chain_n = [0]

        def link(*several):
            for ins in several:
                ins.then_inc(chained, 1)
            chain_n[0] += len(several)
            nc.vector.wait_ge(chained, chain_n[0])

        BATCHES = 2 * NT // BATCH_COLS
        COL_GROUPS = 2 * NT // HALF

        def routing(lay, st_sb):
            r = {}
            for nm in ("score", "sel", "eq", "pos"):
                r[nm] = st_sb(f"{nm}{lay}", [P, NT, E], F)
            r["oh"] = st_sb(f"oh{lay}", [P, 2, NT, E], F)
            r["picked"] = st_sb(f"picked{lay}", [P, 2, NT, E], F)
            r["m"] = st_sb(f"m{lay}", [P, NT], F)
            r["val"] = st_sb(f"val{lay}", [P, 2, NT], F)
            r["den"] = st_sb(f"den{lay}", [P, NT], F)
            r["choice"] = st_sb(f"choice{lay}", [P, NT, E], H)
            r["cum"] = st_sb(f"cum{lay}", [P, E, NT + 1], F)
            r["scan"] = st_sb(f"scan{lay}", [P, E, NT + 1], F)
            r["zero"] = st_sb(f"zero{lay}", [P, E * (NT + 1)], F)
            r["cnt"] = st_sb(f"cnt{lay}", [P, E], F)
            r["cnti"] = st_sb(f"cnti{lay}", [P, E], I)
            r["slotf"] = st_sb(f"slotf{lay}", [P, 2, NT], F)
            r["ge"] = st_sb(f"ge{lay}", [P, SLOT_TILES, E], F)
            r["te"] = st_sb(f"te{lay}", [P, SLOT_TILES], F)
            r["choice_ready"], r["counted"] = sem(f"choice_ready{lay}"), sem(f"counted{lay}")
            return r

        def bc_e(ap):
            return ap.unsqueeze(2).to_broadcast([P, NT, E])

        def select_top2(r):
            rev = cf[:, C_REV:C_REV + E].unsqueeze(1).to_broadcast([P, NT, E])
            for k in range(2):
                oh = r["oh"][:, k]
                link(nc.vector.reduce_max(r["m"][:], r["sel"][:], AX.X))
                link(TT(r["eq"][:], r["sel"][:], bc_e(r["m"][:]), ALU.is_equal))
                link(TT(r["eq"][:], r["eq"][:], rev, ALU.mult))
                link(nc.vector.reduce_max(r["m"][:], r["eq"][:], AX.X))
                link(TT(oh, r["eq"][:], bc_e(r["m"][:]), ALU.is_equal))
                if k == 0:
                    link(STT(r["sel"][:], oh, -1e30, r["sel"][:], ALU.mult, ALU.add))
            TT(r["choice"][:], r["oh"][:, 0], r["oh"][:, 1], ALU.add).then_inc(r["choice_ready"], 1)

        def pick(r, what, out):
            link(TT(r["picked"][:], r["oh"][:], what[:].unsqueeze(1).to_broadcast([P, 2, NT, E]), ALU.mult))
            link(nc.vector.reduce_sum(out[:], r["picked"][:], AX.X))

        def count_choices(pe, r, prefix, totals):
            pe.wait_ge(r["choice_ready"], 1)
            rhs = r["choice"][:].rearrange("p t e -> p (t e)")
            MM(prefix, ch[:, H_LTRI:H_LTRI + P], rhs, start=True, stop=True)
            MM(totals, ch[:, H_ONES:H_ONES + P], rhs, start=True, stop=True).then_inc(r["counted"], 1)

        def assign_slots(dve, r, prefix, totals):
            te = totals.rearrange("p (t e) -> p e t", e=E)
            dve.wait_ge(r["counted"], 1)
            link(nc.vector.memset(r["zero"][:], 0.0), VCOPY(r["cum"][:, :, 0:NT], te),
                 nc.vector.reduce_sum(r["cnt"][:], te, AX.X))
            link(TS(r["cnti"][:], r["cnt"][:], float(P - 1), None, ALU.add))
            link(TS(r["cnti"][:], r["cnti"][:], 7, 7, ALU.logical_shift_right, ALU.logical_shift_left))
            link(TT(r["cum"][:, :, NT], r["cnti"][:], r["cnt"][:], ALU.subtract))
            flat = lambda a: a[:].rearrange("p e t -> p (e t)")
            link(nc.vector.tensor_tensor_scan(flat(r["scan"]), flat(r["cum"]), r["zero"][:], 0.0,
                                              ALU.add, ALU.add))
            before = r["cum"][:, :, 0:NT]
            link(TT(before, r["scan"][:, :, 0:NT], before, ALU.subtract))
            link(TT(r["pos"][:], prefix.rearrange("p (t e) -> p t e", e=E),
                    before.rearrange("p e t -> p t e"), ALU.add))
            pick(r, r["pos"], r["slotf"])

        def expert_of_tiles(r):
            ends = r["scan"][:, :, NT].unsqueeze(1).to_broadcast([P, SLOT_TILES, E])
            starts = cf[:, C_TILE:C_TILE + SLOT_TILES].unsqueeze(2).to_broadcast([P, SLOT_TILES, E])
            link(TT(r["ge"][:], ends, starts, ALU.is_le))
            link(nc.vector.reduce_sum(r["te"][:], r["ge"][:], AX.X))
            link(TS(tile_expert[:], r["te"][:], float(E - 1), None, ALU.min))

        def inversion(st_sb, lay):
            v = {}
            v["slot"] = st_sb(f"slot_int{lay}", [P, 2 * NT], I)
            v["place_int"] = st_sb(f"place_int{lay}", [P, 2, 2 * NT], I)
            v["place"] = st_sb(f"place{lay}", [P, 2, 2 * NT], H)
            v["rows"] = st_sb(f"onehot_rows{lay}", [P, 2, P, BATCH_COLS], H)
            v["cols"] = st_sb(f"onehot_cols{lay}", [P, 2, SLOT_TILES, BATCH_COLS], H)
            v["inv"] = st_sb(f"inv{lay}", [P, COL_GROUPS, SLOT_TILES], F)
            v["iw"] = st_sb(f"iw{lay}", [P, 3, SLOT_TILES], F)
            for nm in ("onehot_ready", "coded_ready", "onehot_used"):
                v[nm] = sem(f"{nm}{lay}")
            return v

        def slot_places(r, v):
            link(VCOPY(v["slot"][:], r["slotf"][:].rearrange("p k t -> p (k t)")))
            link(TS(v["place_int"][:, 0, :], v["slot"][:], 7, None, ALU.logical_shift_right),
                 TS(v["place_int"][:, 1, :], v["slot"][:], P - 1, None, ALU.bitwise_and))
            link(VCOPY(v["place"][:], v["place_int"][:]))

        def one_hot(dve, v, j, b):
            dve.wait_ge(v["onehot_used"], free(j))
            for nm, part, size in (("cols", 0, SLOT_TILES), ("rows", 1, P)):
                number = ch[:, H_IOTA:H_IOTA + size * BATCH_COLS].rearrange("p (n c) -> p n c", c=BATCH_COLS)
                place = v["place"][:, part, bass.ds(j * BATCH_COLS, BATCH_COLS)]
                TT(v[nm][:, b], number, place.unsqueeze(1).to_broadcast([P, size, BATCH_COLS]),
                   ALU.is_equal).then_inc(v["onehot_ready"], 1)

        def code_columns(pool, v, j, b):
            pool.wait_ge(v["onehot_ready"], j * 2 + 1)
            value = cf[:, C_VALUE + b * BATCH_COLS:C_VALUE + (b + 1) * BATCH_COLS]
            nc.gpsimd.tensor_tensor(v["cols"][:, b], v["cols"][:, b], value.unsqueeze(1)
                                    .to_broadcast([P, SLOT_TILES, BATCH_COLS]),
                                    ALU.mult).then_inc(v["coded_ready"], 1)

        def sum_codes(pe, v, inverse, j, g, b):
            pe.wait_ge(v["coded_ready"], j + 1)
            pe.wait_ge(v["onehot_ready"], j * 2 + 2)
            for u in range(BATCH_COLS):
                last = MM(inverse[:, bass.ds(g * SLOT_TILES, SLOT_TILES)], v["rows"][:, b, :, u],
                          v["cols"][:, b, :, u], start=(b == 0 and u == 0),
                          stop=(b == 1 and u == BATCH_COLS - 1))
            last.then_inc(v["onehot_used"], 1)

        def finish_slots(dve, v, inverse):
            dve.wait_ge(v["onehot_used"], 2 + BATCHES)
            inv, iw = v["inv"], v["iw"]
            token = inv[:, 0, :]
            link(VCOPY(inv[:].rearrange("p g s -> p (g s)"), inverse[:, 0:COL_GROUPS * SLOT_TILES]))
            link(TT(iw[:, 0, :], inv[:, 1, :], inv[:, 3, :], ALU.add),
                 TT(iw[:, 1, :], inv[:, 2, :], inv[:, 3, :], ALU.add),
                 TT(token, token, inv[:, 2, :], ALU.add))
            link(TS(iw[:, 2, :], iw[:, 0, :], 0.0, float(HALF * P), ALU.is_gt, ALU.mult),
                 TT(token, token, iw[:, 0, :], ALU.add),
                 TS(iw[:, 1, :], iw[:, 1, :], 0.0, float(N), ALU.is_gt, ALU.mult))
            link(TT(token, token, iw[:, 2, :], ALU.add))
            link(TS(gather_idx[:], token, -1.0, 0.0, ALU.add, ALU.max),
                 TS(iw[:, 2, :], token, 0.0, None, ALU.is_equal),
                 TT(iw[:, 1, :], iw[:, 1, :], token, ALU.add))
            link(TT(iw[:, 2, :], iw[:, 2, :], cf[:, C_PAD:C_PAD + SLOT_TILES], ALU.mult))
            link(STT(scatter_idx[:], iw[:, 2, :], -1.0, iw[:, 1, :], ALU.add, ALU.add))

        def load_expert(engine, t):
            return nc.values_load(tile_expert[0:1, bass.ds(t, 1)], engines=[engine], min_val=0, max_val=E - 1,
                                  skip_runtime_bounds_check_because="a count of experts, at most the last one's number")

        def experts(src, dst, up_hi, up_lo, down_hi, down_lo, hidden, b1_all=None, b2_all=None,
                    side={}):
            HC = hidden // P
            ffn = b1_all is not None
            nm = "ffn_" if ffn else "cond_"
            S = lambda n: sem(nm + n)
            x_in, y_out = sems(nm + "x_in", UNROLL), sems(nm + "y_out", UNROLL)
            x_posed, xhi_done, xlo_done, up_done = S("x_posed"), S("xhi_done"), S("xlo_done"), S("up_done")
            act_done, h_posed, hhi_done, hlo_done = S("act_done"), S("h_posed"), S("hhi_done"), S("hlo_done")
            down_done, y_done = S("down_done"), S("y_done")
            sidx_ready, scattered = S("sidx_ready"), S("scattered")
            if ffn:
                gidx_ready, gathered = S("gidx_ready"), S("gathered")
            st, psb = scope()
            with st:
                xg = psb(nm + "xg", [P, UNROLL, D], F)
                gi = psb(nm + "gi", [P, UNROLL, 1], I)
                si = psb(nm + "si", [P, UNROLL, 1], I)
                xb_hi = psb(nm + "xb_hi", [P, 2, KC, P], H)
                xb_lo = psb(nm + "xb_lo", [P, 2, KC, P], H)
                hs = psb(nm + "hs", [P, 2, hidden], F)
                hb_hi = psb(nm + "hb_hi", [P, 2, HC, P], H)
                hb_lo = psb(nm + "hb_lo", [P, 2, HC, P], H)
                yo = psb(nm + "yo", [P, UNROLL, D], F)
                xT_ps = [bank[0][:, 0:D], bank[1][:, 0:D]]
                up_ps = [bank[2][:, 0:hidden], bank[3][:, 0:hidden]]
                hT_ps = [bank[4][:, 0:hidden], bank[5][:, 0:hidden]]
                y_ps = [bank[6][:, 0:D], bank[7][:, 0:D]]
                flat = lambda a, b: a[:, b].rearrange("p c n -> p (c n)")


                with nc.Block() as block:
                    @block.gpsimd
                    def _(pool):
                        if not ffn:
                            side["pool"](pool)

                        def gather(c):
                            pool.wait_ge(gidx_ready, c.t + 1)
                            pool.wait_ge(x_posed, c.t + 1)
                            pool.sem_inc(pool_passed, 1)
                            pool.indirect_dma_start(
                                out=xg[:, c.slot, :], out_offset=None, in_=src,
                                in_offset=bass.IndirectOffsetOnAxis(ap=gi[:, c.slot, :], axis=0),
                            ).then_inc(x_in[c.slot], 16)

                        def scatter(c):
                            pool.wait_ge(sidx_ready, c.t + 1)
                            pool.wait_ge(y_done, ready(c.t))
                            pool.sem_inc(pool_passed, 1)
                            pool.indirect_dma_start(
                                out=dst, out_offset=bass.IndirectOffsetOnAxis(ap=si[:, c.slot, :], axis=0),
                                in_=yo[:, c.slot, :], in_offset=None).then_inc(y_out[c.slot], 16)

                        pipeline(pool, SLOT_TILES, ([(0, gather)] if ffn else []) + [(8, scatter)])
                        for u in range(UNROLL):
                            pool.wait_ge(y_out[u], 16 * (SLOT_TILES // UNROLL))

                    @block.sync
                    def _(sp):
                        def gather_end(c):
                            sp.wait_ge(x_in[c.slot], (c.turn + 1) * 16)
                            sp.sem_inc(gathered, 1)

                        def scatter_end(c):
                            sp.wait_ge(y_out[c.slot], (c.turn + 1) * 16)
                            sp.sem_inc(scattered, 1)

                        def load(c):
                            sp.wait_ge(x_posed, free(c.t))
                            sp.dma_start(xg[:, c.slot, :], src[bass.ds(c.t * P, P), :]).then_inc(x_in[c.slot], 16)

                        sp.sem_inc(scattered, UNROLL)
                        if ffn:
                            sp.sem_inc(gathered, UNROLL)
                            pipeline(sp, SLOT_TILES, [(0, gather_end), (8, scatter_end)])
                        else:
                            pipeline(sp, SLOT_TILES, [(0, load), (8, scatter_end)],
                                     before_loop=lambda: side["sync"](sp))

                    @block.tensor
                    def _(pe):
                        loaded = {}

                        def expert_of(c):
                            if c.place not in loaded:
                                loaded[c.place] = load_expert(mybir.EngineType.PE, c.t)
                            return loaded[c.place]

                        def pose_x(c):
                            b = c.slot % 2
                            if ffn:
                                pe.wait_ge(gathered, ready4(c.t))
                            else:
                                pe.wait_ge(x_in[c.slot], (c.turn + 1) * 16)
                            for kc in range(KC):
                                last = TR(xT_ps[b][:, kc * P:(kc + 1) * P],
                                          xg[:, c.slot, kc * P:(kc + 1) * P], ident)
                            last.then_inc(x_posed, 1)

                        def up(c):
                            b = c.slot % 2
                            e = expert_of(c)
                            pe.wait_ge(xlo_done, ready(c.t))
                            for kc in range(KC):
                                wh = up_hi[:, bass.ds(e, 1), kc, :].rearrange("p o n -> p (o n)")
                                wl = up_lo[:, bass.ds(e, 1), kc, :].rearrange("p o n -> p (o n)")
                                MM(up_ps[b], xb_hi[:, b, kc, :], wh, start=(kc == 0), stop=False)
                                MM(up_ps[b], xb_lo[:, b, kc, :], wh, start=False, stop=False)
                                last = MM(up_ps[b], xb_hi[:, b, kc, :], wl, start=False, stop=(kc == KC - 1))
                            last.then_inc(up_done, 1)

                        def pose_h(c):
                            b = c.slot % 2
                            pe.wait_ge(act_done, ready(c.t))
                            for hc in range(HC):
                                last = TR(hT_ps[b][:, hc * P:(hc + 1) * P],
                                          hs[:, b, hc * P:(hc + 1) * P], ident)
                            last.then_inc(h_posed, 1)

                        def down(c):
                            b = c.slot % 2
                            e = expert_of(c)
                            pe.wait_ge(hlo_done, ready(c.t))
                            pe.wait_ge(y_done, free(c.t))
                            for hc in range(HC):
                                wh = down_hi[:, bass.ds(e, 1), hc, :].rearrange("p o n -> p (o n)")
                                wl = down_lo[:, bass.ds(e, 1), hc, :].rearrange("p o n -> p (o n)")
                                MM(y_ps[b], hb_hi[:, b, hc, :], wh, start=(hc == 0), stop=False)
                                MM(y_ps[b], hb_lo[:, b, hc, :], wh, start=False, stop=False)
                                last = MM(y_ps[b], hb_hi[:, b, hc, :], wl, start=False, stop=(hc == HC - 1))
                            last.then_inc(down_done, 1)

                        pipeline(pe, SLOT_TILES, [(3, pose_x), (4, up), (5, pose_h), (6, down)],
                                 unroll=2 * UNROLL, slots=UNROLL,
                                 before_loop=side and (lambda: side["tensor"](pe)))

                    @block.scalar
                    def _(act):
                        def x_high(c):
                            b = c.slot % 2
                            act.wait_ge(x_posed, c.t + 1 + UNROLL)
                            act.wait_ge(up_done, free(c.t))
                            nc.scalar.activation(flat(xb_hi, b), xT_ps[b], ACT.Copy).then_inc(xhi_done, 1)

                        def gelu(c):
                            b = c.slot % 2
                            act.wait_ge(up_done, ready(c.t))
                            act.wait_ge(h_posed, free(c.t))
                            nc.scalar.activation(hs[:, b, :], up_ps[b], ACT.Gelu).then_inc(act_done, 1)

                        def h_high(c):
                            b = c.slot % 2
                            act.wait_ge(h_posed, ready(c.t))
                            act.wait_ge(down_done, free(c.t))
                            nc.scalar.activation(flat(hb_hi, b), hT_ps[b],
                                                 ACT.Relu if ffn else ACT.Copy).then_inc(hhi_done, 1)

                        act.sem_inc(x_posed, UNROLL)
                        for s in (up_done, h_posed, down_done):
                            act.sem_inc(s, 2)
                        if side:
                            side["small"](act)
                            act.wait_ge(x_in[UNROLL - 1], 16)
                            side["loads"](act)
                        pipeline(act, SLOT_TILES, [(3, x_high)] + ([] if ffn else [(4, gelu)]) + [(5, h_high)],
                                 before_loop=side and (lambda: side["scalar"](act)))

                    @block.vector
                    def _(dve):
                        def expert_of(t):
                            return load_expert(mybir.EngineType.DVE, t)

                        def gather_index(c):
                            dve.wait_ge(gathered, free(c.t))
                            VCOPY(gi[:, c.slot, :], gather_idx[:, bass.ds(c.t, 1)]).then_inc(gidx_ready, 1)

                        def scatter_index(c):
                            dve.wait_ge(scattered, free(c.t))
                            VCOPY(si[:, c.slot, :], scatter_idx[:, bass.ds(c.t, 1)]).then_inc(sidx_ready, 1)

                        def x_low(c):
                            b = c.slot % 2
                            dve.wait_ge(xhi_done, c.t + 1)
                            TT(flat(xb_lo, b), xT_ps[b], flat(xb_hi, b), ALU.subtract).then_inc(xlo_done, 1)

                        def bias(c):
                            b = c.slot % 2
                            e = expert_of(c.t)
                            dve.wait_ge(up_done, ready(c.t))
                            dve.wait_ge(h_posed, free(c.t))
                            TT(hs[:, b, :], up_ps[b],
                               b1_all[:, bass.ds(e, 1), :].rearrange("p o n -> p (o n)"),
                               ALU.add).then_inc(act_done, 1)

                        def h_low(c):
                            b = c.slot % 2
                            dve.wait_ge(hhi_done, c.t + 1)
                            if ffn:
                                i = STT(flat(hb_lo, b), hT_ps[b], 0.0, flat(hb_hi, b), ALU.max, ALU.subtract)
                            else:
                                i = TT(flat(hb_lo, b), hT_ps[b], flat(hb_hi, b), ALU.subtract)
                            i.then_inc(hlo_done, 1)

                        def result(c):
                            b = c.slot % 2
                            if ffn:
                                e = expert_of(c.t)
                            dve.wait_ge(down_done, ready(c.t))
                            if ffn:
                                i = TT(yo[:, c.slot, :], y_ps[b],
                                       b2_all[:, bass.ds(e, 1), :].rearrange("p o n -> p (o n)"), ALU.add)
                            else:
                                i = VCOPY(yo[:, c.slot, :], y_ps[b])
                            i.then_inc(y_done, 1)

                        for s in (xlo_done, act_done, hlo_done):
                            dve.sem_inc(s, 2)
                        def side_work():
                            side["vector"](dve)
                            dve.sem_inc(y_done, 2)

                        if ffn:
                            dve.sem_inc(y_done, 2)
                            pipeline(dve, SLOT_TILES, [(0, gather_index), (3, x_low), (4, bias), (5, h_low),
                                                       (7, scatter_index), (7, result)])
                        else:
                            pipeline(dve, SLOT_TILES, [(3, x_low), (5, h_low), (7, scatter_index), (7, result)],
                                     before_loop=side_work)

        W1e_hi, W1e_lo = sb("W1e_hi", [P, E, KC, HE], H), sb("W1e_lo", [P, E, KC, HE], H)
        W2e_hi, W2e_lo = sb("W2e_hi", [P, E, HE // P, D], H), sb("W2e_lo", [P, E, HE // P, D], H)
        parts = []
        at = 0
        for hi, lo, n in ((W1e_hi, W1e_lo, KC * HE), (W2e_hi, W2e_lo, HE // P * D),
                          (W1f_hi, W1f_lo, KC * HF), (W2f_hi, W2f_lo, HF // P * D)):
            parts.append((hi, lo, at, at + n))
            at += n
        WEXP = at
        turns = [[], parts[0:2], parts[2:3], parts[3:4]]
        SC = HS // P

        a_scope, asb = scope()
        with a_scope:
            xT_hi, xT_lo = asb("xT_hi", [P, NG, KC, 512], H), asb("xT_lo", [P, NG, KC, 512], H)
            w13_hi, w13_lo = asb("w13_hi", [P, KC, 2 * HS], H), asb("w13_lo", [P, KC, 2 * HS], H)
            w2_hi, w2_lo = asb("w2_hi", [P, SC, D], H), asb("w2_lo", [P, SC, D], H)
            stage = asb("stage", [P, WEXP], F)
            rW_f, rW_hi, rW_lo = (asb("rW_f", [P, KC, E], F), asb("rW_hi", [P, KC, E], H),
                                  asb("rW_lo", [P, KC, E], H))
            rWc_sb = asb("rWc_sb", [P, KC, E], F)
            cond_logit = asb("cond_logit", [BATCH, NT, E], F)
            hidden = asb("hidden", [P, 2, 2, SC, 512], H)
            h_hi, h_lo = hidden[:, 0], hidden[:, 1]
            xstage = hidden[:].rearrange("p a b s n -> p (a b s n)").bitcast(F).rearrange(
                "p (g k n) -> p g k n", k=KC, n=512)
            work = asb("work", [P, 4, 512], F)
            condT = work[:, 0, 0:KC * BATCH].rearrange("p (k b) -> p k b", k=KC)
            V_early = hidden[:].rearrange("p a b s n -> p (a b s n)").bitcast(F).rearrange("p (m n) -> p m n", m=2)
            silu, prod = work[:, 0:2, :], work[:, 2:4, :]
            ys = asb("ys", [P, GT, D], F)
            group = lambda t, g, n: t[:, g].rearrange("p b k n -> p b (k n)")[:, :, 0:n * BATCH_COLS].rearrange(
                "p b (n c) -> p b n c", c=BATCH_COLS)
            last_tables = room(xT_hi[:, 2].rearrange("p k n -> p (k n)"))

            def inversion_home(name, shape, dt):
                if name in ("slot_int0", "place_int0"):
                    whole = prod[:, ("slot_int0", "place_int0").index(name)].bitcast(I)
                    return whole[:, 0:2 * NT] if name == "slot_int0" else whole[:, 0:4 * NT].rearrange(
                        "p (a t) -> p a t", a=2)
                if name == "onehot_rows0":
                    return group(xT_hi, slice(0, 2), P)
                if name == "onehot_cols0":
                    return group(xT_lo, slice(0, 2), SLOT_TILES)
                return (last_tables if name in ("inv0", "iw0") else asb)(name, shape, dt)

            r, v = routing(0, asb), inversion(inversion_home, 0)
            xrow = asb("xrow", [P, UNROLL, D], F)
            logT = xrow[0:E].rearrange("e (b u) d -> e b (u d)", b=2)
            row_idx = asb("row_idx", [P, UNROLL, 2], I)

            consts_in, rw_in, shared_w_in = sem("consts_in"), sem("rw_in"), sem("shared_w_in")
            xT_in = sems("xT_in", UNROLL)
            rw_split, x_hi_done, x_lo_done = sem("rw_split"), sem("x_hi_done"), sem("x_lo_done")
            logT_done, logT_copied, log_posed, log_copied = map(
                sem, ("logT_done", "logT_copied", "log_posed", "log_copied"))
            cl_done, cl_spread, cl_added = sem("cl_done"), sem("cl_spread"), sem("cl_added")
            z_ready, s_ready = sem("z_ready"), sem("s_ready")
            shw_hi, shw_lo = sem("shw_hi"), sem("shw_lo")
            exp_in, exp_hi, exp_lo = sem("exp_in"), sem("exp_hi"), sem("exp_lo")
            sh_up, sh_silu, sh_prod, sh_hi, sh_lo = map(
                sem, ("sh_up", "sh_silu", "sh_prod", "sh_hi", "sh_lo"))
            sh_down, sh_y = sem("sh_down"), sem("sh_y")
            sh_out = sems("sh_out", GT)
            v_in, abs_done = sem("v_early_in"), sem("abs_done")
            zeroed, filled, slots_ready, row_idx_ready = map(sem, ("zeroed", "filled", "slots_ready", "row_idx_ready"))
            xrow_in, rows_out = sems("xrow_in", UNROLL), sems("rows_out", UNROLL)
            FILL = SLOT_TILES * D // (GT * D)
            SHW = 2 * KC * HS + SC * D
            f2 = lambda ap: ap.rearrange("p k n -> p (k n)")

            with nc.Block() as block:
                @block.sync
                def _(sp):
                    sp.dma_start(cf[:], constf).then_inc(consts_in, 16)
                    sp.dma_start(ch[:], consth).then_inc(consts_in, 16)
                    sp.dma_start(router_bias[:, 0, :], rb.partition_broadcast(P)).then_inc(consts_in, 16)
                    sp.dma_start(router_bias[:, 1, :], br.partition_broadcast(P)).then_inc(consts_in, 16)
                    sp.dma_start(rW_f[:], rW).then_inc(rw_in, 16)
                    sp.dma_start(rWc_sb[:], rWc).then_inc(rw_in, 16)
                    sp.dma_start(condT, cond).then_inc(rw_in, 16)
                    for g in range(UNROLL):
                        if g == 2:
                            sp.dma_start(stage[:, 0:2 * KC * HS], w13).then_inc(shared_w_in, 16)
                            sp.dma_start(stage[:, 2 * KC * HS:SHW], w2).then_inc(shared_w_in, 16)
                        sp.dma_start(xstage[:, g], xT[:, g]).then_inc(xT_in[g], 16)
                    for g in range(UNROLL, NG):
                        sp.wait_ge(x_lo_done, g - UNROLL + 1)
                        sp.dma_start(xstage[:, g % UNROLL], xT[:, g]).then_inc(xT_in[g % UNROLL], 16)
                    sp.wait_ge(zeroed, 1)

                    def fill(i):
                        sp.dma_start(xs_d.rearrange("(p r) d -> p (r d)", p=P)[:, bass.ds(i * (GT * D), GT * D)],
                                     ys[:].rearrange("p t d -> p (t d)")).then_inc(filled, 16)

                    with sp.Fori(0, FILL // 2) as i:
                        fill(i)
                    sp.wait_ge(x_lo_done, NG)
                    for m, w in ((0, V1), (1, V2)):
                        sp.dma_start(V_early[:, m, :], w).then_inc(v_in, 16)
                    sp.wait_ge(shw_lo, 1)
                    sp.dma_start(stage[:], wexp[:, 0]).then_inc(exp_in, 16)
                    with sp.Fori(FILL // 2, FILL) as i:
                        fill(i)
                    sp.wait_ge(slots_ready, 1)

                    def load_expert(c):
                        if not isinstance(c.t, int) or c.t > 0:
                            sp.wait_ge(exp_lo, c.t)
                            sp.dma_start(stage[:], wexp[:, bass.ds(c.t, 1)].rearrange(
                                "p o n -> p (o n)")).then_inc(exp_in, 16)

                    def load_rows(c):
                        for u in range(GT):
                            if not isinstance(c.t, int) or c.t > 0:
                                sp.wait_ge(rows_out[u], c.t * 32)
                            sp.dma_start(xrow[:, u, :], x[bass.ds(c.t * (GT * P) + u * P, P), :]
                                         ).then_inc(xrow_in[u], 16)

                    def store_shared(c):
                        for u in range(GT):
                            sp.wait_ge(sh_y, ready(c.t * GT + u))
                            sp.dma_start(shared_d[bass.ds(c.t * (GT * P) + u * P, P), :],
                                         ys[:, u, :]).then_inc(sh_out[u], 16)

                    pipeline(sp, NG, [(0, load_expert), (0, load_rows), (1, store_shared)], unroll=2)
                    for u in range(GT):
                        sp.wait_ge(sh_out[u], 16 * (NG + 1))

                @block.gpsimd
                def _(pool):
                    nc.gpsimd.memset(ys[:], 0.0).then_inc(zeroed, 1)
                    pool.sem_inc(v["onehot_used"], 2)
                    pool.wait_ge(slots_ready, 1)
                    pool.wait_ge(filled, 16 * FILL)

                    def scatter_group(c):
                        for u in range(GT):
                            pool.wait_ge(xrow_in[u], (c.t + 1) * 16)
                            nc.gpsimd.tensor_copy(row_idx[:, u, :], slot_of[:, :, bass.ds(c.t * GT + u, 1)].rearrange(
                                "p k o -> p (k o)")).then_inc(row_idx_ready, 1)
                            pool.wait_ge(row_idx_ready, c.t * GT + (u + 1))
                            pool.sem_inc(pool_passed, 1)
                            for k in range(2):
                                pool.indirect_dma_start(
                                    out=xs_d, out_offset=bass.IndirectOffsetOnAxis(ap=row_idx[:, u, k:k + 1], axis=0),
                                    in_=xrow[:, u, :], in_offset=None).then_inc(rows_out[u], 16)

                    pipeline(pool, NG, [(0, scatter_group), (0, lambda c: code_columns(pool, v, c.t, c.slot))],
                             unroll=2)
                    for u in range(UNROLL):
                        pool.wait_ge(rows_out[u], 32 * (NT // UNROLL))

                @block.tensor
                def _(pe):
                    pe.wait_ge(rw_in, 48)
                    for kc in range(KC):
                        last = MM(bank[4][0:BATCH, 0:E], condT[:, kc, :], rWc_sb[:, kc, :],
                                  start=(kc == 0), stop=(kc == KC - 1))
                    last.then_inc(cl_done, 1)
                    pe.wait_ge(cl_spread, 1)
                    MM(bank[3][:, 0:NT * E], cf[0:BATCH, C_SEL:C_SEL + P],
                       cond_logit[:].rearrange("b t e -> b (t e)"), start=True, stop=True).then_inc(cl_added, 1)
                    pe.wait_ge(rw_split, 2)

                    def body(st, c):
                        b = c.slot % 2
                        if st == 0:
                            pe.wait_ge(x_lo_done, c.t + 1)
                            pe.wait_ge(logT_copied, free(c.t))
                            for kc in range(KC):
                                xh = xT_hi[:, bass.ds(c.t, 1), kc, :].rearrange("p o n -> p (o n)")
                                xl = xT_lo[:, bass.ds(c.t, 1), kc, :].rearrange("p o n -> p (o n)")
                                o = bank[5 + b][0:E, :]
                                MM(o, rW_hi[:, kc, :], xh, start=(kc == 0), stop=False)
                                MM(o, rW_lo[:, kc, :], xh, start=False, stop=False)
                                last = MM(o, rW_hi[:, kc, :], xl, start=False, stop=(kc == KC - 1))
                            last.then_inc(logT_done, 1)
                        if st == 1:
                            pe.wait_ge(logT_copied, ready(c.t))
                            pe.wait_ge(log_copied, free(c.t))
                            pe.sem_inc(pe_passed, 1)
                            for u in range(GT):
                                last = TR(bank[1 + b][:, u * E:(u + 1) * E], logT[:, b, u * P:(u + 1) * P],
                                          cf[0:E, C_IDENT:C_IDENT + E])
                            last.then_inc(log_posed, 1)

                    pipeline(pe, NG, in_stages(1, body))
                    count_choices(pe, r, bank[6][:, 0:NT * E], bank[7][:, 0:NT * E])

                    pe.wait_ge(shw_lo, 1)

                    def shared(st, c):
                        b = c.slot % 2
                        if st == 0:
                            for j in range(SC):
                                n = c.t * SC + j
                                pe.wait_ge(sh_prod, free(n))
                                for m in range(2):
                                    o = bank[2 * (j % 2) + m][:, :]
                                    cols = slice(m * HS + j * P, m * HS + (j + 1) * P)
                                    for kc in range(KC):
                                        xh = xT_hi[:, bass.ds(c.t, 1), kc, :].rearrange("p o n -> p (o n)")
                                        xl = xT_lo[:, bass.ds(c.t, 1), kc, :].rearrange("p o n -> p (o n)")
                                        MM(o, w13_hi[:, kc, cols], xh, start=(kc == 0), stop=False)
                                        MM(o, w13_hi[:, kc, cols], xl, start=False, stop=False)
                                        last = MM(o, w13_lo[:, kc, cols], xh, start=False, stop=(kc == KC - 1))
                                last.then_inc(sh_up, 1)
                        else:
                            pe.wait_ge(sh_lo, (c.t + 1) * SC)
                            for u in range(GT):
                                pe.wait_ge(sh_y, free(c.t * GT + u))
                                o = bank[4 + u % 2][:, 0:D]
                                for hc in range(SC):
                                    tok = slice(u * P, (u + 1) * P)
                                    MM(o, h_hi[:, b, hc, tok], w2_hi[:, hc, :], start=(hc == 0), stop=False)
                                    MM(o, h_hi[:, b, hc, tok], w2_lo[:, hc, :], start=False, stop=False)
                                    last = MM(o, h_lo[:, b, hc, tok], w2_hi[:, hc, :], start=False, stop=(hc == SC - 1))
                                last.then_inc(sh_down, 1)
                            sum_codes(pe, v, bank[6], c.t, c.turn, b)

                    pipeline(pe, NG, in_stages(1, shared), unroll=2)

                @block.scalar
                def _(act):
                    act.sem_inc(logT_copied, 2)
                    act.sem_inc(log_copied, 2)
                    act.sem_inc(log_posed, 2)
                    act.sem_inc(sh_y, 2)
                    for u in range(GT):
                        act.sem_inc(sh_out[u], 16)
                    act.sem_inc(sh_down, 2 * GT)
                    act.wait_ge(rw_in, 48)
                    nc.scalar.activation(f2(rW_hi[:]), f2(rW_f[:]), ACT.Copy).then_inc(rw_split, 1)

                    def body(st, c):
                        b = c.slot % 2
                        if st == 0:
                            act.wait_ge(xT_in[c.slot], (c.turn + 1) * 16)
                            nc.scalar.activation(
                                xT_hi[:, bass.ds(c.t, 1), :, :].rearrange("p o k n -> p (o k n)"),
                                f2(xstage[:, c.slot]), ACT.Copy).then_inc(x_hi_done, 1)
                        if st == 1:
                            act.wait_ge(logT_done, c.t + 1)
                            act.wait_ge(log_posed, free(c.t))
                            nc.scalar.activation(logT[:, b, :], bank[5 + b][0:E, :], ACT.Copy).then_inc(logT_copied, 1)
                        if st == 2:
                            act.wait_ge(log_posed, ready(c.t))
                            nc.scalar.activation(
                                logits[:, bass.ds(c.t * GT, GT), :].rearrange("p t e -> p (t e)"),
                                bank[1 + b][:, 0:GT * E], ACT.Copy).then_inc(log_copied, 1)

                    def split_weights():
                        act.wait_ge(shared_w_in, 32)
                        nc.scalar.activation(f2(w13_hi[:]), stage[:, 0:2 * KC * HS], ACT.Copy)
                        nc.scalar.activation(f2(w2_hi[:]), stage[:, 2 * KC * HS:SHW], ACT.Copy).then_inc(shw_hi, 1)

                    pipeline(act, NG, in_stages(2, body), before_loop=split_weights)
                    act.wait_ge(z_ready, 1)
                    nc.scalar.activation(r["score"][:], r["sel"][:], ACT.Sigmoid).then_inc(s_ready, 1)
                    act.wait_ge(v_in, 32)
                    for m in range(2):
                        last = nc.scalar.activation(V_early[:, m, :], V_early[:, m, :], ACT.Abs,
                                                    accum_out=asum[:, m:m + 1])
                    last.then_inc(abs_done, 1)

                    def shared(st, c):
                        b = c.slot % 2
                        if st == 0:
                            for j in range(SC):
                                n = c.t * SC + j
                                act.wait_ge(sh_up, n + 1)
                                act.wait_ge(sh_prod, free(n))
                                nc.scalar.activation(silu[:, j % 2, :], bank[2 * (j % 2)][:, :],
                                                     ACT.Silu).then_inc(sh_silu, 1)
                                if j == 1:
                                    act.wait_ge(exp_in, (c.t + 1) * 16)
                                for hi, lo, a, z in turns[j]:
                                    last = nc.scalar.activation(
                                        hi[:, bass.ds(c.t, 1), :, :].rearrange("p o k n -> p (o k n)"),
                                        stage[:, a:z], ACT.Copy)
                                if turns[j]:
                                    last.then_inc(exp_hi, 1)
                        else:
                            for u in range(GT):
                                n = c.t * GT + u
                                act.wait_ge(sh_down, n + (1 + 2 * GT))
                                act.wait_ge(sh_out[u], (c.t + 1) * 16)
                                nc.scalar.activation(ys[:, u, :], bank[4 + u % 2][:, 0:D], ACT.Copy,
                                                     scale=1.0 / 3.0).then_inc(sh_y, 1)

                    pipeline(act, NG, in_stages(1, shared), unroll=2,
                             before_loop=lambda: act.wait_ge(filled, 16 * FILL))

                @block.vector
                def _(dve):
                    dve.sem_inc(sh_prod, 2)
                    dve.wait_ge(rw_split, 1)
                    TT(f2(rW_lo[:]), f2(rW_f[:]), f2(rW_hi[:]), ALU.subtract).then_inc(rw_split, 1)
                    dve.wait_ge(consts_in, 64)
                    dve.wait_ge(cl_done, 1)
                    TT(cond_logit[:], bank[4][0:BATCH, 0:E].unsqueeze(1).to_broadcast([BATCH, NT, E]),
                       cf[0:BATCH, C_OWN:C_OWN + NT].unsqueeze(2).to_broadcast([BATCH, NT, E]),
                       ALU.mult).then_inc(cl_spread, 1)

                    def body(st, c):
                        dve.wait_ge(x_hi_done, c.t + 1)
                        TT(xT_lo[:, bass.ds(c.t, 1), :, :].rearrange("p o k n -> p (o k n)"),
                           f2(xstage[:, c.slot]),
                           xT_hi[:, bass.ds(c.t, 1), :, :].rearrange("p o k n -> p (o k n)"),
                           ALU.subtract).then_inc(x_lo_done, 1)

                    pipeline(dve, NG, in_stages(0, body))
                    dve.wait_ge(shw_hi, 1)
                    TT(f2(w13_lo[:]), stage[:, 0:2 * KC * HS], f2(w13_hi[:]), ALU.subtract)
                    TT(f2(w2_lo[:]), stage[:, 2 * KC * HS:SHW], f2(w2_hi[:]), ALU.subtract).then_inc(shw_lo, 1)
                    dve.wait_ge(log_copied, 2 + NG)
                    dve.wait_ge(cl_added, 1)
                    TT(r["sel"][:], logits[:], bank[3][:, 0:NT * E].rearrange("p (t e) -> p t e", e=E),
                       ALU.add).then_inc(z_ready, 1)
                    dve.wait_ge(s_ready, 1)
                    link(TT(r["sel"][:], r["score"][:],
                            router_bias[:, 0, :].unsqueeze(1).to_broadcast([P, NT, E]), ALU.add))
                    select_top2(r)
                    assign_slots(dve, r, bank[6][:, 0:NT * E], bank[7][:, 0:NT * E])
                    VCOPY(slot_of[:], r["slotf"][:]).then_inc(slots_ready, 1)
                    slot_places(r, v)
                    assert BATCHES == NG

                    dve.wait_ge(abs_done, 1)

                    def shared(st, c):
                        b = c.slot % 2
                        for j in range(SC):
                            n = c.t * SC + j
                            dve.wait_ge(sh_silu, n + 1)
                            TT(prod[:, j % 2, :], silu[:, j % 2, :], bank[2 * (j % 2) + 1][:, :],
                               ALU.mult).then_inc(sh_prod, 1)
                            dve.wait_ge(sh_prod, ready(n))
                            if j == 0:
                                dve.wait_ge(sh_down, c.t * GT + GT)
                            VCOPY(h_hi[:, b, j, :], prod[:, j % 2, :]).then_inc(sh_hi, 1)
                            dve.wait_ge(sh_hi, n + 1)
                            TT(h_lo[:, b, j, :], prod[:, j % 2, :], h_hi[:, b, j, :], ALU.subtract).then_inc(sh_lo, 1)
                            for hi, lo, a, z in turns[j]:
                                if j == 1:
                                    dve.wait_ge(exp_hi, c.t * 3 + 1)
                                if j > 1:
                                    dve.wait_ge(exp_hi, c.t * 3 + j)
                                last = TT(lo[:, bass.ds(c.t, 1), :, :].rearrange("p o k n -> p (o k n)"),
                                          stage[:, a:z],
                                          hi[:, bass.ds(c.t, 1), :, :].rearrange("p o k n -> p (o k n)"),
                                          ALU.subtract)
                        last.then_inc(exp_lo, 1)
                        one_hot(dve, v, c.t, b)

                    pipeline(dve, NG, in_stages(0, shared), unroll=2)
                    expert_of_tiles(r)
                    g0 = gates[0]
                    pick(r, r["score"], r["val"])
                    link(TT(r["den"][:], r["val"][:, 0, :], r["val"][:, 1, :], ALU.add))
                    link(TS(r["m"][:], r["den"][:], 1e-9, None, ALU.is_gt))
                    link(TS(r["den"][:], r["den"][:], 1e-9, None, ALU.add))
                    link(nc.vector.reciprocal(r["den"][:], r["den"][:]))
                    both = lambda ap: ap.unsqueeze(1).to_broadcast([P, 2, NT])
                    link(TT(g0[:], r["val"][:], both(r["den"][:]), ALU.mult))
                    link(TS(g0[:], g0[:], -0.5, None, ALU.add))
                    link(TT(g0[:], g0[:], both(r["m"][:]), ALU.mult))
                    link(TS(g0[:], g0[:], 0.5, 1.0 / 3.0, ALU.add, ALU.mult))
                    finish_slots(dve, v, bank[6])

        end_phase()

        late_scope, lsb = scope()
        b1_all, b2_all = lsb("b1_all", [P, E, HF], F), lsb("b2_all", [P, E, D], F)
        WT_hi, WT_lo = lsb("WT_hi", [P, 2, D], H), lsb("WT_lo", [P, 2, D], H)
        FC = DF // P
        V1_q, V2_q = lsb("V1_q", [P, KC, DF], H), lsb("V2_q", [P, FC, D], H)
        c1_sb, c2_sb = lsb("c1_sb", [P, FC], F), lsb("c2_sb", [P, D], F)
        modul = lsb("modul", [P, NT, 4], F)
        Wc_f, nrm = lsb("Wc_f", [P, 2, D], F), lsb("nrm", [BATCH, D], F)

        v_scope, vsb = scope()
        V_f = vsb("V_f", [P, 2, KC * DF], F)
        limit = vsb("limit", [P, 2, 2], F)

        b_scope, bsb = scope()
        with b_scope:
            Wsq = bsb("Wsq", [P, 2, D], F)
            cI, cIsq = bsb("cI", [P, 2, BATCH], F), bsb("cIsq", [P, 2, BATCH], F)
            onesf = bsb("onesf", [P, P], F)
            (v_in, vf_in, w_in, ones_done, sum_done, limit_done, above_done, quant_done, sq_done,
             ss_done) = map(sem, ("v_in", "vf_in", "w_in", "ones_done", "sum_done", "limit_done",
                                  "above_done", "quant_done", "sq_done", "ss_done"))
            sum_ps, ss_ps = bank[6][:, 0:2], bank[7][0:BATCH, 0:D]

            def side_small(act):
                for t, w in ((cI[:], condTI), (Wc_f[:], WcT)):
                    act.dma_start(t, w).then_inc(v_in, 16)

            def side_loads(act):
                for m, w in ((0, V1), (1, V2)):
                    act.dma_start(V_f[:, m, :], w).then_inc(vf_in, 16)

            def side_sync(sp):
                for t, w in ((b1_all[:], b1f.partition_broadcast(P)), (b2_all[:], b2f.partition_broadcast(P)),
                             (c1_sb[:], c1), (c2_sb[:], c2.partition_broadcast(P)), (modul[:], modulation)):
                    sp.dma_start(t, w).then_inc(w_in, 16)

            def side_scalar(act):
                act.wait_ge(v_in, 16 * 2)
                nc.scalar.activation(cIsq[:], cI[:], ACT.Square)
                nc.scalar.activation(Wsq[:], Wc_f[:], ACT.Square).then_inc(sq_done, 1)

            def side_tensor(pe):
                pe.wait_ge(ones_done, 1)
                MM(sum_ps, onesf[:], asum[:], start=True, stop=True).then_inc(sum_done, 1)
                pe.wait_ge(sq_done, 1)
                for ql in range(2):
                    last = MM(ss_ps, cIsq[:, ql, :], Wsq[:, ql, :], start=(ql == 0), stop=(ql == 1))
                last.then_inc(ss_done, 1)

            def side_vector(dve):
                dve.wait_ge(sum_done, 1)
                for i, sign in ((0, 1.0), (1, -1.0)):
                    TS(limit[:, i, :], sum_ps, sign * 0.5 / (D * DF), sign * 0.5e-5,
                       ALU.mult, ALU.add).then_inc(limit_done, 1)
                dve.wait_ge(limit_done, 2)
                dve.wait_ge(ss_done, 1)
                link(TS(nrm[:], ss_ps, D * 1e-8, None, ALU.add))

            def side_pool(pool):
                nc.gpsimd.memset(onesf[:], 1.0).then_inc(ones_done, 1)

            experts(xs_d, y_d, W1e_hi, W1e_lo, W2e_hi, W2e_lo, HE,
                    side={"small": side_small, "loads": side_loads, "sync": side_sync, "scalar": side_scalar,
                          "tensor": side_tensor, "vector": side_vector, "pool": side_pool})

        with late_scope:
            c_scope, csb2 = scope()
            with c_scope:
                r, v = routing(1, csb2), inversion(csb2, 1)
                y, sh = csb2("y", [P, UNROLL, 2, D], F), csb2("sh", [P, UNROLL, D], F)
                flat_w = lambda w: w[:].rearrange("p e k n -> p (e k n)")
                above, below = flat_w(W1e_hi)[:, 0:KC * DF], flat_w(W2e_hi)[:, 0:KC * DF]
                part, co = (flat_w(w)[:, 0:UNROLL * D * 2].bitcast(F).rearrange("p (u d) -> p u d", d=D)
                            for w in (W1e_lo, W2e_lo))
                xc_hi, xc_lo = (csb2(n, [P, UNROLL, KC, P], H) for n in ("xc_hi", "xc_lo"))
                Wr_f, Wr_hi, Wr_lo = (csb2("Wr_f", [P, KC, E], F), csb2("Wr_hi", [P, KC, E], H),
                                      csb2("Wr_lo", [P, KC, E], H))
                y_in, sh_in = sems("cy_in", UNROLL), sems("sh_in", UNROLL)
                c_out = sems("c_out", UNROLL)
                (wr_in, wr_split, part_done, part_sum, co_done, co_posed, xchi_done, xclo_done,
                 rl_done, rl_copied, c_shift, c_exp, root_done, nrm_done, wt_hi, nrm_out) = map(sem, (
                     "wr_in", "wr_split", "part_done", "part_sum", "co_done", "co_posed",
                     "xchi_done", "xclo_done", "rl_done", "rl_copied", "c_shift", "c_exp",
                     "root_done", "nrm_done", "wt_hi", "nrm_out"))
                f2 = lambda ap: ap.rearrange("p k n -> p (k n)")

                with nc.Block() as block:
                    @block.sync
                    def _(sp):
                        sp.dma_start(Wr_f[:], Wr).then_inc(wr_in, 16)
                        sp.wait_ge(w_in, 16 * 5)
                        sp.wait_ge(nrm_done, 1)
                        sp.dma_start(norm_d, nrm[:]).then_inc(nrm_out, 16)

                        def load(c):
                            sp.wait_ge(co_done, free(c.t))
                            sp.dma_start(sh[:, c.slot, :], shared_d[bass.ds(c.t * P, P), :]).then_inc(sh_in[c.slot], 16)

                        def store(c):
                            sp.wait_ge(co_done, ready4(c.t))
                            sp.dma_start(cond_d[bass.ds(c.t * P, P), :], co[:, c.slot, :]).then_inc(c_out[c.slot], 16)

                        pipeline(sp, NT, [(0, load), (4, store)])
                        for u in range(UNROLL):
                            sp.wait_ge(c_out[u], 16 * (NT // UNROLL + 1))
                        sp.wait_ge(nrm_out, 16)

                    @block.gpsimd
                    def _(pool):
                        def load_pair(c):
                            pool.wait_ge(co_done, free(c.t))
                            pool.dma_start(y[:, c.slot], y_d[0:2 * N].rearrange("(k n) d -> n k d", k=2)
                                           [bass.ds(c.t * P, P)]).then_inc(y_in[c.slot], 16)

                        pipeline(pool, NT, [(0, load_pair)])
                        pool.wait_ge(limit_done, 2)
                        pool.wait_ge(vf_in, 32)
                        for m, q in ((0, V1_q), (1, V2_q)):
                            if m:
                                pool.wait_ge(quant_done, 1)
                            nc.gpsimd.tensor_scalar(above, V_f[:, m, :], limit[:, 0, m:m + 1], None,
                                                    ALU.is_gt).then_inc(above_done, 1)
                            nc.gpsimd.tensor_scalar(below, V_f[:, m, :], limit[:, 1, m:m + 1], None,
                                                    ALU.is_lt).then_inc(above_done, 1)
                            pool.wait_ge(above_done, 2 * (m + 1))
                            nc.gpsimd.tensor_tensor(q[:].rearrange("p k n -> p (k n)"), above, below,
                                                    ALU.subtract).then_inc(quant_done, 1)
                        pool.sem_inc(v["onehot_used"], 2)
                        with pool.Fori(0, BATCHES // 2) as i:
                            for b in range(2):
                                code_columns(pool, v, i * 2 + b, b)

                    @block.tensor
                    def _(pe):
                        pe.wait_ge(wr_split, 2)

                        def pose(c):
                            pe.wait_ge(co_done, ready4(c.t))
                            pe.wait_ge(xclo_done, free(c.t))
                            for kc in range(KC):
                                last = TR(bank[c.slot][:, kc * P:(kc + 1) * P],
                                          co[:, c.slot, kc * P:(kc + 1) * P], ident)
                            last.then_inc(co_posed, 1)

                        def router(c):
                            pe.wait_ge(xclo_done, ready4(c.t))
                            pe.wait_ge(rl_copied, free(c.t))
                            o = bank[4 + c.slot][:, 0:E]
                            for kc in range(KC):
                                MM(o, xc_hi[:, c.slot, kc, :], Wr_hi[:, kc, :], start=(kc == 0), stop=False)
                                MM(o, xc_hi[:, c.slot, kc, :], Wr_lo[:, kc, :], start=False, stop=False)
                                last = MM(o, xc_lo[:, c.slot, kc, :], Wr_hi[:, kc, :], start=False, stop=(kc == KC - 1))
                            last.then_inc(rl_done, 1)

                        pipeline(pe, NT, [(0, pose), (4, router)])
                        count_choices(pe, r, bank[4][:, 0:NT * E], bank[5][:, 0:NT * E])
                        with pe.Fori(0, COL_GROUPS) as g:
                            for b in range(2):
                                sum_codes(pe, v, bank[7], g * 2 + b, g, b)

                    @block.scalar
                    def _(act):
                        for m in (part_done, rl_copied, co_posed, rl_done):
                            act.sem_inc(m, UNROLL)
                        nc.scalar.activation(nrm[:], nrm[:], ACT.Sqrt).then_inc(root_done, 1)
                        nc.scalar.activation(WT_hi[:], Wc_f[:], ACT.Copy).then_inc(wt_hi, 1)
                        act.wait_ge(wr_in, 16)
                        nc.scalar.activation(f2(Wr_hi[:]), f2(Wr_f[:]), ACT.Copy).then_inc(wr_split, 1)

                        def first_term(c):
                            act.wait_ge(y_in[c.slot], (c.turn + 1) * 16)
                            act.wait_ge(co_done, free(c.t))
                            nc.scalar.activation(part[:, c.slot, :], y[:, c.slot, 0, :], ACT.Copy,
                                                 scale=gates[0][:, 0, bass.ds(c.t, 1)]).then_inc(part_done, 1)

                        def high(c):
                            act.wait_ge(co_posed, ready4(c.t))
                            act.wait_ge(rl_done, free(c.t))
                            nc.scalar.activation(f2(xc_hi[:, c.slot]), bank[c.slot][:, 0:D],
                                                 ACT.Copy).then_inc(xchi_done, 1)

                        def take_logits(c):
                            act.wait_ge(rl_done, ready4(c.t))
                            nc.scalar.activation(logits[:, bass.ds(c.t, 1), :].rearrange("p o e -> p (o e)"),
                                                 bank[4 + c.slot][:, 0:E], ACT.Copy).then_inc(rl_copied, 1)

                        pipeline(act, NT, [(3, first_term), (6, high), (10, take_logits)])
                        act.wait_ge(c_shift, 1)
                        nc.scalar.activation(r["score"][:], r["sel"][:], ACT.Exp).then_inc(c_exp, 1)

                    @block.vector
                    def _(dve):
                        for m in (co_done, xclo_done):
                            dve.sem_inc(m, UNROLL)
                        for u in range(UNROLL):
                            dve.sem_inc(c_out[u], 16)
                        dve.wait_ge(root_done, 1)
                        nc.vector.reciprocal(nrm[:], nrm[:]).then_inc(nrm_done, 1)
                        dve.wait_ge(wt_hi, 1)
                        TT(WT_lo[:], Wc_f[:], WT_hi[:], ALU.subtract)
                        dve.wait_ge(wr_split, 1)
                        TT(f2(Wr_lo[:]), f2(Wr_f[:]), f2(Wr_hi[:]), ALU.subtract).then_inc(wr_split, 1)

                        def add_shared(c):
                            dve.wait_ge(part_done, ready4(c.t))
                            dve.wait_ge(sh_in[c.slot], (c.turn + 1) * 16)
                            TT(part[:, c.slot, :], part[:, c.slot, :], sh[:, c.slot, :], ALU.add).then_inc(part_sum, 1)

                        def combine(c):
                            dve.wait_ge(part_sum, c.t + 1)
                            dve.wait_ge(c_out[c.slot], (c.turn + 1) * 16)
                            dve.wait_ge(co_posed, free(c.t))
                            STT(co[:, c.slot, :], y[:, c.slot, 1, :], gates[0][:, 1, bass.ds(c.t, 1)],
                                part[:, c.slot, :], ALU.mult, ALU.add).then_inc(co_done, 1)

                        def low(c):
                            dve.wait_ge(xchi_done, c.t + 1)
                            TT(f2(xc_lo[:, c.slot]), bank[c.slot][:, 0:D], f2(xc_hi[:, c.slot]),
                               ALU.subtract).then_inc(xclo_done, 1)

                        pipeline(dve, NT, [(4, combine), (3, add_shared), (7, low)])
                        dve.wait_ge(rl_copied, UNROLL + NT)
                        link(TT(r["sel"][:], logits[:],
                                router_bias[:, 1, :].unsqueeze(1).to_broadcast([P, NT, E]), ALU.add))
                        link(nc.vector.reduce_max(r["m"][:], r["sel"][:], AX.X))
                        TT(r["sel"][:], r["sel"][:], bc_e(r["m"][:]), ALU.subtract).then_inc(c_shift, 1)
                        dve.wait_ge(c_exp, 1)
                        link(nc.vector.reduce_sum(r["den"][:], r["score"][:], AX.X))
                        link(nc.vector.reciprocal(r["den"][:], r["den"][:]))
                        link(TT(r["score"][:], r["score"][:], bc_e(r["den"][:]), ALU.mult))
                        link(VCOPY(r["sel"][:], r["score"][:]))
                        select_top2(r)
                        assign_slots(dve, r, bank[4][:, 0:NT * E], bank[5][:, 0:NT * E])
                        slot_places(r, v)
                        with dve.Fori(0, BATCHES // 2) as i:
                            for b in range(2):
                                one_hot(dve, v, i * 2 + b, b)
                        expert_of_tiles(r)
                        pick(r, r["score"], gates[1])
                        finish_slots(dve, v, bank[7])

            v_scope.close()

            experts(cond_d, z_d, W1f_hi, W1f_lo, W2f_hi, W2f_lo, HF, b1_all, b2_all)

            e_scope, esb = scope()
            with e_scope:
                PAIR = 2 * P
                CH = FC // 2
                z0, z1, xr = (esb(n, [P, UNROLL, D], F) for n in ("z0", "z1", "xres"))
                norm = esb("norm", [P, UNROLL, D], F)
                part = esb("part1", [P, 2, D], F)
                x1 = esb("x1", [P, 2, D], F)
                x1b = W1f[:].rearrange("p a e k n -> p (a e k n)").bitcast(F).rearrange("p (t d) -> p t d", d=D)
                xm = esb("xm", [P, 2, 2, P], F)
                xm_hi, xm_lo = esb("xm_hi", [P, 2, 2, P], H), esb("xm_lo", [P, 2, 2, P], H)
                zf = esb("zf", [P, 2, KC, P], F)
                zT_hi, zT_lo = esb("zT_hi", [P, 2, KC, PAIR], H), esb("zT_lo", [P, 2, KC, PAIR], H)
                hf = esb("hf", [P, 2, CH, PAIR], F)
                u_hi, u_lo = esb("u_hi", [P, 2, FC, PAIR], H), esb("u_lo", [P, 2, FC, PAIR], H)
                ob = esb("ob", [P, UNROLL, D], F)
                z_in, o_out = sems("z_in", UNROLL), sems("o_out", UNROLL)
                (e_part, e_sum, e_x1, e_x1b, e_xm, e_xmhi, e_xmlo, e_mix, e_zf, e_zhi, e_zlo,
                 e_up, e_relu, e_uhi, e_ulo, e_down, e_o) = map(sem, (
                     "e_part", "e_sum", "e_x1", "e_x1b", "e_xm", "e_xmhi", "e_xmlo", "e_mix", "e_zf",
                     "e_zhi", "e_zlo", "e_up", "e_relu", "e_uhi", "e_ulo", "e_down", "e_o"))
                f2 = lambda ap: ap.rearrange("p k n -> p (k n)")
                mix_ps = [bank[2][:, 0:D], bank[3][:, 0:D]]
                up_ps = [bank[j][:, 0:PAIR] for j in (0, 1, 6, 7)]
                down_ps = [bank[4][:, 0:D], bank[5][:, 0:D]]

                with nc.Block() as block:
                    @block.sync
                    def _(sp):
                        def load(c):
                                if not isinstance(c.t, int) or c.t >= UNROLL:
                                    sp.wait_ge(e_x1, c.t + (-1))
                                    sp.wait_ge(e_zf, c.t + (-1))
                                for d, s in ((z0, z_d[bass.ds(c.t * P, P), :]), (z1, z_d[bass.ds(c.t * P + N, P), :]),
                                             (xr, x[bass.ds(c.t * P, P), :])):
                                    sp.dma_start(d[:, c.slot, :], s).then_inc(z_in[c.slot], 16)
                                for bb in range(2):
                                    sp.dma_start(norm[bb * SEQ:(bb + 1) * SEQ, c.slot, :],
                                                 norm_d[bass.ds(c.t * 2 + bb, 1), :].rearrange("o d -> (o d)")
                                                 .partition_broadcast(SEQ)).then_inc(z_in[c.slot], 16)
                        def store(c):
                                sp.wait_ge(e_o, ready(c.t))
                                sp.dma_start(out[bass.ds(c.t * P, P), :], ob[:, c.slot, :]).then_inc(o_out[c.slot], 16)

                        pipeline(sp, NT, [(0, load), (10, store)])
                        for u in range(UNROLL):
                            sp.wait_ge(o_out[u], 16 * (NT // UNROLL + 1))

                    @block.gpsimd
                    def _(pool):
                        def add_x(c):
                            b = c.slot % 2
                            pool.wait_ge(e_part, ready(c.t))
                            nc.gpsimd.tensor_tensor(part[:, b, :], part[:, b, :], xr[:, c.slot, :],
                                                    ALU.add).then_inc(e_sum, 1)

                        def add_c2(c):
                            b = c.slot % 2
                            pool.wait_ge(e_x1, ready(c.t))
                            nc.gpsimd.tensor_tensor(x1b[:, bass.ds(c.t, 1), :].rearrange("p o d -> p (o d)"),
                                                    x1[:, b, :], c2_sb[:], ALU.add).then_inc(e_x1b, 1)

                        def mod_lo(c):
                            b = c.slot % 2
                            pool.wait_ge(e_xmhi, c.t + 1)
                            pool.wait_ge(e_mix, free(c.t))
                            nc.gpsimd.tensor_tensor(f2(xm_lo[:, b]), f2(xm[:, b]), f2(xm_hi[:, b]),
                                                    ALU.subtract).then_inc(e_xmlo, 1)

                        pool.sem_inc(e_x1b, 2)
                        pool.sem_inc(e_xmlo, 2)
                        pipeline(pool, NT, [(2, mod_lo), (1, add_c2), (0, add_x)])

                    @block.tensor
                    def _(pe):
                        def mix(c):
                            b = c.slot % 2
                            pe.wait_ge(e_xmlo, ready(c.t))
                            pe.wait_ge(e_zf, free(c.t))
                            for ql in range(2):
                                MM(mix_ps[b], xm_hi[:, b, ql, :], WT_hi[:, ql, :], start=(ql == 0), stop=False)
                                MM(mix_ps[b], xm_hi[:, b, ql, :], WT_lo[:, ql, :], start=False, stop=False)
                                last = MM(mix_ps[b], xm_lo[:, b, ql, :], WT_hi[:, ql, :], start=False, stop=(ql == 1))
                            last.then_inc(e_mix, 1)

                        def up(c):
                            b = c.slot % 2
                            pr = c.slot // 2
                            pe.wait_ge(e_zlo, c.t + (2 - b))
                            for j in range(CH):
                                fc = CH * b + j
                                pe.wait_ge(e_relu, c.t * CH + (j + 1))
                                for kc in range(KC):
                                    w = V1_q[:, kc, fc * P:(fc + 1) * P]
                                    MM(up_ps[j], w, zT_hi[:, pr, kc, :], start=(kc == 0), stop=False)
                                    last = MM(up_ps[j], w, zT_lo[:, pr, kc, :], start=False, stop=(kc == KC - 1))
                                last.then_inc(e_up, 1)

                        def down(c):
                            b = c.slot % 2
                            pr = c.slot // 2
                            pe.wait_ge(e_ulo, c.t * 2 + (8 - 2 * b))
                            pe.wait_ge(e_o, free(c.t))
                            tok = slice(b * P, (b + 1) * P)
                            for fc in range(FC):
                                MM(down_ps[b], u_hi[:, pr, fc, tok], V2_q[:, fc, :], start=(fc == 0), stop=False)
                                last = MM(down_ps[b], u_lo[:, pr, fc, tok], V2_q[:, fc, :], start=False,
                                          stop=(fc == FC - 1))
                            last.then_inc(e_down, 1)

                        pipeline(pe, NT, [(5, up), (7, down), (2, mix)])

                    @block.scalar
                    def _(act):
                        for s, n in ((e_part, 2), (e_mix, 2), (e_zhi, 2), (e_relu, CH), (e_uhi, 2),
                                     (e_up, UNROLL * CH), (e_down, UNROLL)):
                            act.sem_inc(s, n)

                        def first_term(c):
                            b = c.slot % 2
                            act.wait_ge(z_in[c.slot], (c.turn + 1) * 80)
                            act.wait_ge(e_x1, free(c.t))
                            nc.scalar.activation(part[:, b, :], z0[:, c.slot, :], ACT.Copy,
                                                 scale=gates[1][:, 0, bass.ds(c.t, 1)]).then_inc(e_part, 1)

                        def mod_hi(c):
                            b = c.slot % 2
                            act.wait_ge(e_xm, c.t + 1)
                            act.wait_ge(e_mix, free(c.t))
                            nc.scalar.activation(f2(xm_hi[:, b]), f2(xm[:, b]), ACT.Copy).then_inc(e_xmhi, 1)

                        def mixed_hi(c):
                            b = c.slot % 2
                            pr = c.slot // 2
                            act.wait_ge(e_zf, ready(c.t))
                            if b == 0:
                                act.wait_ge(e_up, (c.t + 2) * CH)
                            nc.scalar.activation(zT_hi[:, pr, :, b * P:(b + 1) * P], zf[:, b],
                                                 ACT.Copy).then_inc(e_zhi, 1)

                        def hidden(c):
                            b, pr = c.slot % 2, c.slot // 2

                            def split(j):
                                fc = CH * b + j
                                act.wait_ge(e_relu, c.t * CH + (j + 2 + CH))
                                if fc == 0:
                                    act.wait_ge(e_down, c.t + 2)
                                nc.scalar.activation(u_hi[:, pr, fc:fc + 2, :], hf[:, b, j:j + 2, :],
                                                     ACT.Copy).then_inc(e_uhi, 1)

                            for j in range(CH):
                                fc = CH * b + j
                                act.wait_ge(e_up, (c.t + UNROLL) * CH + (j + 1))
                                if j % 2 == 0:
                                    act.wait_ge(e_ulo, c.t * 2 + (j // 2 + 1))
                                nc.scalar.activation(hf[:, b, j, :], up_ps[j], ACT.Relu,
                                                     bias=c1_sb[:, fc:fc + 1]).then_inc(e_relu, 1)
                                if j % 2 == 0 and j > 0:
                                    split(j - 2)
                            split(CH - 2)

                        pipeline(act, NT, [(2, mod_hi), (0, first_term), (3, mixed_hi), (5, hidden)])

                    @block.vector
                    def _(dve):
                        for s in (e_x1, e_zf, e_ulo, e_ulo, e_o):
                            dve.sem_inc(s, 2)
                        for u in range(UNROLL):
                            dve.sem_inc(o_out[u], 16)

                        def x_one(c):
                            b = c.slot % 2
                            dve.wait_ge(e_sum, c.t + 1)
                            dve.wait_ge(e_x1b, free(c.t))
                            STT(x1[:, b, :], z1[:, c.slot, :], gates[1][:, 1, bass.ds(c.t, 1)], part[:, b, :],
                                ALU.mult, ALU.add).then_inc(e_x1, 1)

                        def modulate(c):
                            b = c.slot % 2
                            dve.wait_ge(e_x1, ready(c.t))
                            dve.wait_ge(e_xmlo, free(c.t))
                            for bb in range(2):
                                for qh in range(2):
                                    rows = slice(bb * SEQ, (bb + 1) * SEQ)
                                    last = TT(
                                        xm[qh * SEQ:(qh + 1) * SEQ, b, :, rows],
                                        x1[rows, b, qh * P:(qh + 1) * P].rearrange("p (q l) -> p q l", q=2),
                                        modul[rows, bass.ds(c.t, 1), qh * 2:qh * 2 + 2].rearrange("p o q -> p (o q)")
                                        .unsqueeze(2).to_broadcast([SEQ, 2, SEQ]), ALU.mult)
                            last.then_inc(e_xm, 1)

                        def normalise(c):
                            b = c.slot % 2
                            pr = c.slot // 2
                            dve.wait_ge(e_mix, ready(c.t))
                            dve.wait_ge(e_zhi, free(c.t))
                            for bb in range(2):
                                for h in range(2):
                                    rows, cols = slice(bb * SEQ, (bb + 1) * SEQ), slice(h * P, (h + 1) * P)
                                    last = TT(zf[h * SEQ:(h + 1) * SEQ, b, :, rows],
                                              mix_ps[b][rows, cols].rearrange("p (k t) -> p k t", k=KC),
                                              norm[rows, c.slot, cols].rearrange("p (k t) -> p k t", k=KC), ALU.mult)
                            last.then_inc(e_zf, 1)

                        def mixed_lo(c):
                            b, pr = c.slot % 2, c.slot // 2
                            dve.wait_ge(e_zhi, ready(c.t))
                            TT(zT_lo[:, pr, :, b * P:(b + 1) * P], zf[:, b],
                               zT_hi[:, pr, :, b * P:(b + 1) * P], ALU.subtract).then_inc(e_zlo, 1)

                        def hidden_lo(c):
                            b = c.slot % 2
                            pr = c.slot // 2
                            for j in range(0, CH, 2):
                                fc = CH * b + j
                                dve.wait_ge(e_uhi, c.t * 2 + (j // 2 + 3))
                                TT(u_lo[:, pr, fc:fc + 2, :], hf[:, b, j:j + 2, :], u_hi[:, pr, fc:fc + 2, :],
                                   ALU.subtract).then_inc(e_ulo, 1)

                        def total(c):
                            b = c.slot % 2
                            dve.wait_ge(e_down, c.t + (1 + UNROLL))
                            dve.wait_ge(o_out[c.slot], (c.turn + 1) * 16)
                            TT(ob[:, c.slot, :], down_ps[b], x1b[:, bass.ds(c.t, 1), :].rearrange("p o d -> p (o d)"),
                               ALU.add).then_inc(e_o, 1)

                        pipeline(dve, NT, [(3, normalise), (6, hidden_lo), (3, mixed_lo), (1, x_one), (8, total),
                                           (1, modulate)])


def constants():
    import numpy as np

    f = np.zeros((P, C_END), np.float32)
    p = np.arange(P)
    f[:, C_IDENT:C_IDENT + P] = np.eye(P)
    f[:, C_REV:C_REV + E] = E - np.arange(E)
    f[:, C_VALUE:C_VALUE + NT] = (np.arange(NT) % HALF) * P + p[:, None] + 1
    f[:, C_TILE:C_TILE + SLOT_TILES] = np.arange(SLOT_TILES) * P
    f[:, C_PAD:C_PAD + SLOT_TILES] = 2 * N + 1 + np.arange(SLOT_TILES) * P + p[:, None]
    for b in range(BATCH):
        f[b, C_SEL:C_SEL + P] = (p // SEQ) == b % 2
        f[b, C_OWN + b // 2] = 1
    h = np.zeros((P, H_END), np.float16)
    h[:, H_LTRI:H_LTRI + P] = p[:, None] < p[None, :]
    h[:, H_ONES:H_ONES + P] = 1
    h[:, H_IOTA:] = np.repeat(p, BATCH_COLS)
    return f, h


def kernel(x, cond_1024, L0_cond_router_W, L0_cond_router_bias, L0_cond_w1, L0_cond_w3, L0_cond_w2,
           L0_cond_W1e, L0_cond_W2e, L0_ffn_Wr, L0_ffn_br, L0_ffn_W1, L0_ffn_b1, L0_ffn_W2, L0_ffn_b2,
           L1_cond_weight, L1_ffn_W1, L1_ffn_b1, L1_ffn_W2, L1_ffn_b2):
    import numpy as np
    import concourse.bacc as bacc
    from concourse.bass_utils import run_bass_kernel_spmd

    def on_partitions(w):
        w = np.asarray(w)
        return w.reshape(w.shape[0] // P, P, w.shape[1]).transpose(1, 0, 2)

    def experts_on_partitions(w):
        w = np.asarray(w)
        e, k, n = w.shape
        return w.reshape(e, k // P, P, n).transpose(2, 0, 1, 3).reshape(P, e, -1)

    flat = lambda a: a.reshape(P, -1)
    xf = np.asarray(x).reshape(N, D)
    cond = np.asarray(cond_1024)
    rW = np.asarray(L0_cond_router_W)
    Wc = np.asarray(L1_cond_weight).reshape(SEQ, 2, 2, SEQ, 2, 2)
    WcT = Wc.transpose(4, 3, 5, 2, 1, 0).reshape(P, 2, D)
    condTI = cond.reshape(BATCH, SEQ, 2, 2).transpose(2, 1, 3, 0).reshape(P, 2, BATCH)
    constf, consth = constants()
    arrays = {
        "x": xf,
        "xT": xf.T.reshape(KC, P, NG, 512).transpose(1, 2, 0, 3),
        "cond": on_partitions(cond.T),
        "condTI": condTI,
        "modulation": cond.reshape(NT, P, 4).transpose(1, 0, 2),
        "rW": on_partitions(rW[:D]),
        "rWc": on_partitions(rW[D:]),
        "Wr": on_partitions(L0_ffn_Wr),
        "rb": np.asarray(L0_cond_router_bias),
        "br": np.asarray(L0_ffn_br),
        "w13": flat(np.concatenate([on_partitions(L0_cond_w1), on_partitions(L0_cond_w3)], axis=2)),
        "w2": flat(on_partitions(L0_cond_w2)),
        "wexp": np.concatenate([experts_on_partitions(w) for w in (
            L0_cond_W1e, L0_cond_W2e, L0_ffn_W1, L0_ffn_W2)], axis=2),
        "b1f": np.asarray(L0_ffn_b1),
        "b2f": np.asarray(L0_ffn_b2),
        "WcT": WcT,
        "V1": flat(on_partitions(np.asarray(L1_ffn_W1).T)),
        "c1": np.asarray(L1_ffn_b1).reshape(DF // P, P).T,
        "V2": flat(on_partitions(np.asarray(L1_ffn_W2).T)),
        "c2": np.asarray(L1_ffn_b2),
        "constf": constf,
        "consth": consth,
    }
    arrays = {k: np.ascontiguousarray(v) for k, v in arrays.items()}
    nc = bacc.Bacc("TRN2", target_bir_lowering=False, num_devices=1)
    args = [nc.dram_tensor(f"in_{k}", v.shape, mybir.dt.from_np(v.dtype), kind="ExternalInput").ap()
            for k, v in arrays.items()]
    out = nc.dram_tensor("out", (N, D), mybir.dt.float32, kind="ExternalOutput").ap()
    program(nc, *args, out)
    r = run_bass_kernel_spmd(nc, [{f"in_{k}": v for k, v in arrays.items()}], core_ids=[0])
    return r.results[0]["out"].reshape(BATCH, SEQ, D)
```
